# Optimizing a Trainium2 kernel written in Bass

```python
import numpy as np
import jax
import jax.numpy as jnp

def _softmax(x, axis=-1):
    return jax.nn.softmax(x, axis=axis)

def _gelu(x):
    return jax.nn.gelu(x, approximate=True)

def _silu(x):
    return jax.nn.silu(x)

def _sigmoid(x):
    return jax.nn.sigmoid(x)

def _layernorm(x, axis=-1, eps=1e-05):
    m = jnp.mean(x, axis=axis, keepdims=True)
    v = jnp.var(x, axis=axis, keepdims=True)
    return (x - m) / jnp.sqrt(v + eps)

def _scatter_add(tgt, idx, src, axis=0):
    return tgt.at[idx].add(src)

def _segment_sum(src, seg, n):
    return jax.ops.segment_sum(src, seg, n)
kernel_name = 'mk_decoder_preln_d1_seqx_r4_3ad1a2'

def setup_inputs(seed: int=0):
    np.random.seed(seed)
    _w = jnp.asarray

    def _rec_inputs():
        import jax
        import jax.numpy as jnp
        _rk = jax.random.key(seed)
        x = 7.22e-05 + 1 * jax.random.normal(jax.random.fold_in(_rk, 1), (4, 1024, 256), jnp.float32)
        _lenS = 1024 - jax.random.randint(jax.random.fold_in(_rk, 7), (4,), 0, max(1, 1024 // 4) + 1, jnp.int32)
        _lenS2 = 77 - jax.random.randint(jax.random.fold_in(_rk, 8), (4,), 0, max(1, 77 // 4) + 1, jnp.int32)
        _ctx_1024P = jax.random.normal(jax.random.fold_in(_rk, 11), (4, 16, 256), jnp.float32)
        _ctx_1024c = jax.random.dirichlet(jax.random.fold_in(_rk, 511), 0.3 * jnp.ones((16,), jnp.float32), (4, 77))
        _ctx_1024t = jnp.einsum('bsk,bkd->bsd', _ctx_1024c, _ctx_1024P)
        _ctx_1024t = _ctx_1024t * jax.lax.rsqrt(jnp.mean(jnp.square(_ctx_1024t)) + 1e-12) * 0.953939
        ctx_1024 = 4.13588e-05 + 0.999923 * (_ctx_1024t + 0.3 * jax.random.normal(jax.random.fold_in(_rk, 611), (4, 77, 256), jnp.float32))
        _validS = jnp.arange(1024)[None, :] < _lenS[:, None]
        _validS2 = jnp.arange(77)[None, :] < _lenS2[:, None]
        _causal = jnp.tril(jnp.ones((1024, 1024), dtype=bool))
        mask_BxSxS2_ik1 = jnp.where(jnp.broadcast_to(_validS2[:, None, :], (4, 1024, 77)), 1, 0).astype(jnp.int32)
        return (x, ctx_1024, mask_BxSxS2_ik1)
    x, ctx_1024, mask_BxSxS2_ik1 = _rec_inputs()

    def _L0_attn_setup():
        import jax, jax.numpy as jnp
        import numpy as np
        HIDDEN = 256
        NUM_HEADS = 16
        NUM_KV = 4
        HEAD_DIM = HIDDEN // NUM_HEADS
        GROUPS = NUM_HEADS // NUM_KV
        SCALE = HEAD_DIM ** 0.5
        key = jax.random.key(seed)
        ks = jax.random.split(key, 9)
        s = 0.02
        B, N = (4, 512)
        return {'x': jax.random.normal(ks[0], (B, N, HIDDEN), dtype=jnp.float32), 'Wq': jax.random.normal(ks[1], (HIDDEN, NUM_HEADS * HEAD_DIM), dtype=jnp.float32) * s, 'bq': jnp.zeros((NUM_HEADS * HEAD_DIM,), dtype=jnp.float32), 'Wk': jax.random.normal(ks[2], (HIDDEN, NUM_KV * HEAD_DIM), dtype=jnp.float32) * s, 'bk': jnp.zeros((NUM_KV * HEAD_DIM,), dtype=jnp.float32), 'Wv': jax.random.normal(ks[3], (HIDDEN, NUM_KV * HEAD_DIM), dtype=jnp.float32) * s, 'bv': jnp.zeros((NUM_KV * HEAD_DIM,), dtype=jnp.float32), 'Wo': jax.random.normal(ks[4], (NUM_HEADS * HEAD_DIM, HIDDEN), dtype=jnp.float32) * s, 'bo': jnp.zeros((HIDDEN,), dtype=jnp.float32)}
    _L0_attn_all = _L0_attn_setup()
    _L0_attn_in = {k: v for k, v in _L0_attn_all.items() if k in ('Wq', 'bq', 'Wk', 'bk', 'Wv', 'bv', 'Wo', 'bo')}
    del _L0_attn_all

    def _L0_xattn_setup():
        import jax, jax.numpy as jnp
        import numpy as np
        B, S, D = (4, 512, 256)
        H, DK, DV = (16, 64, 64)
        NEG = -10000000000.0
        key = jax.random.key(seed)
        ks = jax.random.split(key, 8)
        queries = jax.random.normal(ks[0], (B, S, D), dtype=jnp.float32)
        keys_ = jax.random.normal(ks[1], (B, S, D), dtype=jnp.float32)
        values = jax.random.normal(ks[2], (B, S, D), dtype=jnp.float32)
        mask = jax.random.randint(ks[3], (B, S, S), 0, 2, dtype=jnp.int32)
        sq = 1.0 / np.sqrt(D)
        Wq = jax.random.normal(ks[4], (H, D, DK), dtype=jnp.float32) * sq
        Wk = jax.random.normal(ks[5], (H, D, DK), dtype=jnp.float32) * sq
        Wv = jax.random.normal(ks[6], (H, D, DV), dtype=jnp.float32) * sq
        Wo = jax.random.normal(ks[7], (H * DV, D), dtype=jnp.float32) * (1.0 / np.sqrt(H * DV))
        return {'queries': queries, 'keys': keys_, 'values': values, 'mask': mask, 'Wq': Wq, 'Wk': Wk, 'Wv': Wv, 'Wo': Wo}
    _L0_xattn_all = _L0_xattn_setup()
    _L0_xattn_in = {k: v for k, v in _L0_xattn_all.items() if k in ('Wq', 'Wk', 'Wv', 'Wo')}
    del _L0_xattn_all

    def _L0_ffn_setup():
        import jax, jax.numpy as jnp
        import numpy as np
        EPS = 1e-05
        LN_EPS = 1e-05
        NUM_EXPERTS = 8
        TOP_K = 2
        HIDDEN = 256
        INTER = 512

        def _swiglu(x, wg, wu, wd):
            return jax.nn.silu(x @ wg) * (x @ wu) @ wd
        key = jax.random.key(seed)
        ks = jax.random.split(key, 10)
        B, S, H, I, E = (8, 1024, HIDDEN, INTER, NUM_EXPERTS)
        std_h = 1.0 / np.sqrt(H)
        std_i = 1.0 / np.sqrt(I)
        return {'x': jax.random.normal(ks[0], (B, S, H), dtype=jnp.float32), 'ln_scale': jnp.ones((H,), dtype=jnp.float32), 'ln_bias': jnp.zeros((H,), dtype=jnp.float32), 'gate_w': jax.random.normal(ks[1], (E, H), dtype=jnp.float32) * 0.01, 'Wg': jax.random.normal(ks[2], (E, H, I), dtype=jnp.float32) * std_h, 'Wu': jax.random.normal(ks[3], (E, H, I), dtype=jnp.float32) * std_h, 'Wd': jax.random.normal(ks[4], (E, I, H), dtype=jnp.float32) * std_i, 'sWg': jax.random.normal(ks[5], (H, I), dtype=jnp.float32) * std_h, 'sWu': jax.random.normal(ks[6], (H, I), dtype=jnp.float32) * std_h, 'sWd': jax.random.normal(ks[7], (I, H), dtype=jnp.float32) * std_i}
    _L0_ffn_all = _L0_ffn_setup()
    _L0_ffn_in = {k: v for k, v in _L0_ffn_all.items() if k in ('ln_scale', 'ln_bias', 'gate_w', 'Wg', 'Wu', 'Wd', 'sWg', 'sWu', 'sWd')}
    del _L0_ffn_all
    return {'x': x, 'ctx_1024': ctx_1024, 'mask_BxSxS2_ik1': mask_BxSxS2_ik1, 'L0_attn_Wq': _L0_attn_in['Wq'], 'L0_attn_bq': _L0_attn_in['bq'], 'L0_attn_Wk': _L0_attn_in['Wk'], 'L0_attn_bk': _L0_attn_in['bk'], 'L0_attn_Wv': _L0_attn_in['Wv'], 'L0_attn_bv': _L0_attn_in['bv'], 'L0_attn_Wo': _L0_attn_in['Wo'], 'L0_attn_bo': _L0_attn_in['bo'], 'L0_xattn_Wq': _L0_xattn_in['Wq'], 'L0_xattn_Wk': _L0_xattn_in['Wk'], 'L0_xattn_Wv': _L0_xattn_in['Wv'], 'L0_xattn_Wo': _L0_xattn_in['Wo'], 'L0_ffn_ln_scale': _L0_ffn_in['ln_scale'], 'L0_ffn_ln_bias': _L0_ffn_in['ln_bias'], 'L0_ffn_gate_w': _L0_ffn_in['gate_w'], 'L0_ffn_Wg': _L0_ffn_in['Wg'], 'L0_ffn_Wu': _L0_ffn_in['Wu'], 'L0_ffn_Wd': _L0_ffn_in['Wd'], 'L0_ffn_sWg': _L0_ffn_in['sWg'], 'L0_ffn_sWu': _L0_ffn_in['sWu'], 'L0_ffn_sWd': _L0_ffn_in['sWd']}

def reference(x, ctx_1024, mask_BxSxS2_ik1, L0_attn_Wq, L0_attn_bq, L0_attn_Wk, L0_attn_bk, L0_attn_Wv, L0_attn_bv, L0_attn_Wo, L0_attn_bo, L0_xattn_Wq, L0_xattn_Wk, L0_xattn_Wv, L0_xattn_Wo, L0_ffn_ln_scale, L0_ffn_ln_bias, L0_ffn_gate_w, L0_ffn_Wg, L0_ffn_Wu, L0_ffn_Wd, L0_ffn_sWg, L0_ffn_sWu, L0_ffn_sWd):
    import jax
    import jax.numpy as jnp

    def _L0_attn_ref(x, Wq, bq, Wk, bk, Wv, bv, Wo, bo):
        import jax, jax.numpy as jnp
        import numpy as np
        HIDDEN = 256
        NUM_HEADS = 16
        NUM_KV = 4
        HEAD_DIM = HIDDEN // NUM_HEADS
        GROUPS = NUM_HEADS // NUM_KV
        SCALE = HEAD_DIM ** 0.5
        B, N, _ = x.shape
        q = x @ Wq + bq
        k = x @ Wk + bk
        v = x @ Wv + bv
        q = q.reshape(B, N, NUM_HEADS, HEAD_DIM).transpose(0, 2, 1, 3)
        q = q.reshape(B, NUM_KV, GROUPS, N, HEAD_DIM).transpose(0, 2, 1, 3, 4)
        k = k.reshape(B, N, NUM_KV, HEAD_DIM).transpose(0, 2, 1, 3)
        v = v.reshape(B, N, NUM_KV, HEAD_DIM).transpose(0, 2, 1, 3)
        scores = jnp.einsum('bghnd,bhsd->bghns', q, k)
        attn = jax.nn.softmax(scores / SCALE, axis=-1)
        out = jnp.einsum('bghns,bhsd->bghnd', attn, v)
        out = out.transpose(0, 3, 1, 2, 4).reshape(B, N, NUM_HEADS * HEAD_DIM)
        return out @ Wo + bo

    def _L0_xattn_ref(queries, keys, values, mask, Wq, Wk, Wv, Wo):
        import jax, jax.numpy as jnp
        import numpy as np
        B, S, D = (4, 512, 256)
        H, DK, DV = (16, 64, 64)
        NEG = -10000000000.0
        q = jnp.einsum('bsd,hdk->bhsk', queries, Wq)
        k = jnp.einsum('bsd,hdk->bhsk', keys, Wk)
        v = jnp.einsum('bsd,hdv->bhsv', values, Wv)
        scores = jnp.einsum('bhsk,bhtk->bhst', q, k) / jnp.sqrt(jnp.asarray(DK, q.dtype))
        scores = jnp.where(mask[:, None, :, :] == 0, jnp.asarray(NEG, scores.dtype), scores)
        weights = jax.nn.softmax(scores, axis=-1)
        out = jnp.einsum('bhst,bhtv->bhsv', weights, v)
        out = jnp.transpose(out, (0, 2, 1, 3)).reshape(out.shape[0], out.shape[2], H * DV)
        return out @ Wo

    def _L0_ffn_ref(x, ln_scale, ln_bias, gate_w, Wg, Wu, Wd, sWg, sWu, sWd):
        import jax, jax.numpy as jnp
        import numpy as np
        EPS = 1e-05
        LN_EPS = 1e-05
        NUM_EXPERTS = 8
        TOP_K = 2
        HIDDEN = 256
        INTER = 512

        def _swiglu(x, wg, wu, wd):
            return jax.nn.silu(x @ wg) * (x @ wu) @ wd
        B, S, H = x.shape
        xf = x.reshape(-1, H)
        mu = jnp.mean(xf, axis=-1, keepdims=True)
        var = jnp.var(xf, axis=-1, keepdims=True)
        xn = (xf - mu) * jax.lax.rsqrt(var + LN_EPS) * ln_scale + ln_bias
        logits = xn @ gate_w.T
        probs = jax.nn.softmax(logits, axis=-1)
        tk_probs, tk_idx = jax.lax.top_k(probs, TOP_K)
        tk_probs = tk_probs / (jnp.sum(tk_probs, axis=-1, keepdims=True) + EPS)
        onehot = tk_idx[..., None] == jnp.arange(NUM_EXPERTS)[None, None, :]
        w = jnp.sum(tk_probs[..., None] * onehot.astype(tk_probs.dtype), axis=1)
        out = _swiglu(xf, sWg, sWu, sWd)
        for e in range(NUM_EXPERTS):
            out = out + w[:, e:e + 1] * _swiglu(xf, Wg[e], Wu[e], Wd[e])
        return out.reshape(B, S, H)
    x = x + _L0_attn_ref(_layernorm(x, axis=-1), L0_attn_Wq, L0_attn_bq, L0_attn_Wk, L0_attn_bk, L0_attn_Wv, L0_attn_bv, L0_attn_Wo, L0_attn_bo)
    x = x + _L0_xattn_ref(_layernorm(x, axis=-1), ctx_1024, ctx_1024, mask_BxSxS2_ik1, L0_xattn_Wq, L0_xattn_Wk, L0_xattn_Wv, L0_xattn_Wo)
    x = x + _L0_ffn_ref(_layernorm(x, axis=-1), L0_ffn_ln_scale, L0_ffn_ln_bias, L0_ffn_gate_w, L0_ffn_Wg, L0_ffn_Wu, L0_ffn_Wd, L0_ffn_sWg, L0_ffn_sWu, L0_ffn_sWd)
    return x

_drawn_inputs = setup_inputs


def setup_inputs(seed=0):
    import zlib

    import numpy as np

    out = dict(_drawn_inputs(seed))
    spreads = {'L0_attn_bq': (0.0, 0.8),
     'L0_attn_bk': (0.0, 0.8),
     'L0_attn_bv': (0.0, 0.1),
     'L0_attn_bo': (0.0, 0.1),
     'L0_ffn_ln_scale': (1.0, 0.2),
     'L0_ffn_ln_bias': (0.0, 0.1)}
    factors = {'L0_attn_Wq': 8.0, 'L0_attn_Wk': 7.682, 'L0_attn_Wv': 3.479}
    for name, (base, spread) in spreads.items():
        noise = np.random.default_rng([zlib.crc32(name.encode()), seed]).standard_normal(out[name].shape)
        drawn = base * np.exp(spread * noise) if base else spread * noise
        out[name] = jnp.asarray(drawn.astype(out[name].dtype))
    for name, factor in factors.items():
        out[name] = (out[name] * factor).astype(out[name].dtype)
    return out
```

```python
import concourse.bass as bass
from concourse import mybir
from contextlib import ExitStack

F32 = mybir.dt.float32
BF16 = mybir.dt.bfloat16
I32 = mybir.dt.int32
U32 = mybir.dt.uint32
ALU = mybir.AluOpType
ACT = mybir.ActivationFunctionType
AX = mybir.AxisListType

P = 128
D = 256
KD = D // P
B = 4
S = 1024
TB = S // P
NT = B * TB
LN_EPS = 1e-5
NH = 16
NKV = 4
GH = NH // NKV
HD = D // NH
NG = B * NKV
SCALE = HD ** -0.5
VW = 32
Q_PARTS = (3, 2, 1)
KQ = sum(Q_PARTS) * HD
KM = KQ + 3
HALF = 512
SLOTS = 4
TURN_AT = 4
NU = GH * TB


def phase_qkv(nc, T):
    X, ident, VA, q_parts, k_parts = T["X"], T["ident"], T["VA"], T["q_parts"], T["k_parts"]
    with ExitStack() as ctx:
        def sb(name, shape, dt=F32):
            return ctx.enter_context(nc.sbuf_tensor(name, shape, dt))

        def sem(name):
            return ctx.enter_context(nc.semaphore(name))

        wq = sb("wq_sb", [P, KD, D])
        wk = sb("wk_sb", [P, KD, NKV * HD])
        wv = sb("wv_sb", [P, KD, NKV * HD])
        bqk = sb("bqk_sb", [P, 3])
        bv = sb("bv_sb", [P, NKV * HD])
        stats = sb("stats", [P, TB, 6])
        mean_var = sb("mean_var", [P, TB, 2])
        var_eps = sb("var_eps", [P, TB])
        neg_half = sb("neg_half", [P, TB])
        rstd = sb("rstd", [P, TB])
        xn = sb("xn", [P, TB, D])
        xnT = sb("xnT", [P, KD, S])
        part = sb("part", [P, 3, 3, S], BF16)
        rest = sb("rest", [P, 3, S])
        psT = ctx.enter_context(nc.psum_tensor("psT", [P, 2, HALF], F32))
        psQ = ctx.enter_context(nc.psum_tensor("psQ", [P, 4, HALF], F32))
        psV = ctx.enter_context(nc.psum_tensor("psV", [P, 1, HALF], F32))

        x_loaded = sem("x_loaded")
        w_loaded = sem("w_loaded")
        consts = sem("consts")
        waited_pool = sem("qkv_waited_pool")
        waited_dve = sem("qkv_waited_dve")
        stats_done = sem("stats_done")
        mv_done = sem("mv_done")
        veps_done = sem("veps_done")
        rstd_done = sem("rstd_done")
        xn_done = sem("xn_done")
        tr_done = sem("tr_done")
        xnT_done = sem("xnT_done")
        proj_done = sem("proj_done")
        p1_done = sem("p1_done")
        rest_done = sem("rest_done")
        p2_done = sem("p2_done")
        p3_done = sem("p3_done")
        v_done = sem("v_done")
        va_done = sem("va_done")
        stored = sem("stored")
        MS = [(0, P), (1, P), (2, NKV * HD)]
        UNITS = [(m, rows, n) for m, rows in MS for n in range(2)]
        NUN = len(UNITS)
        NSTORE = 16 * 3 * (NKV + 1)
        block = ctx.enter_context(nc.Block())

        @block.sync
        def _(sp):
            sp.dma_start(X[:, :, :], T["x"].rearrange("b (t p) d -> p (b t) d", p=P)).then_inc(x_loaded, 16)
            sp.dma_start(wq[:, :, :], T["Wq"].rearrange("(k p) n -> p k n", p=P)).then_inc(w_loaded, 16)
            sp.dma_start(wk[:, :, :], T["Wk"].rearrange("(k p) n -> p k n", p=P)).then_inc(w_loaded, 16)
            sp.dma_start(wv[:, :, :], T["Wv"].rearrange("(k p) n -> p k n", p=P)).then_inc(w_loaded, 16)
            sp.dma_start(bqk[:, :], T["bqk"]).then_inc(w_loaded, 16)
            sp.dma_start(bv[:, :], T["bv"].rearrange("(a n) -> a n", a=1).to_broadcast([P, NKV * HD])).then_inc(w_loaded, 16)
            with sp.Fori(0, B) as b:
                sp.wait_ge(p3_done, NUN * b + NUN)
                for m in range(2):
                    for j in range(3):
                        for gg in range(2):
                            rows = slice(gg * GH * HD, (gg + 1) * GH * HD)
                            sp.dma_start(q_parts[b + (2 * m + gg) * B, j, :, :, :].rearrange("d h n -> h d n"),
                                         part[rows, j, m, :]).then_inc(stored, 16)
                for j in range(3):
                    sp.dma_start(k_parts.rearrange("(g b) j d n -> b j g d n", b=B)[b, j, :, :, :],
                                 part[0:NKV * HD, j, 2, :]).then_inc(stored, 16)
            sp.wait_ge(stored, NSTORE * B)

        @block.gpsimd
        def _(pool):
            pool.memset(ident[:, :], 0.0).then_inc(consts, 1)
            pool.wait_ge(consts, 1)
            pool.affine_select(out=ident[:, :], in_=ident[:, :], compare_op=ALU.not_equal, fill=1.0,
                               base=0, pattern=[[-1, P]], channel_multiplier=1).then_inc(consts, 1)
            pool.memset(neg_half[:, :], -0.5).then_inc(consts, 1)
            pool.memset(VA[:, :, :, :], 0.0).then_inc(consts, 1)
            pool.wait_ge(consts, 4)
            pool.memset(VA[:, :, :, HD:HD + 1], 1.0).then_inc(consts, 1)
            with pool.Fori(0, B) as b:
                pool.wait_ge(veps_done, b + 1)
                pool.tensor_tensor(rstd[:, :], var_eps[:, :], neg_half[:, :], ALU.pow).then_inc(rstd_done, 1)
                for u, (m, rows, n) in enumerate(UNITS):
                    cols = slice(n * HALF, (n + 1) * HALF)
                    pool.wait_ge(rest_done, NUN * b + u + 1)
                    pool.sem_inc(waited_pool, 1)
                    pool.tensor_copy(part[0:rows, 1, m, cols], rest[0:rows, m, cols]).then_inc(p2_done, 1)
                    pool.wait_ge(p2_done, NUN * b + u + 1)
                    pool.tensor_tensor(part[0:rows, 2, m, cols], rest[0:rows, m, cols],
                                       part[0:rows, 1, m, cols], ALU.subtract).then_inc(p3_done, 1)

        @block.vector
        def _(dve):
            dve.wait_ge(x_loaded, 16)
            dve.wait_ge(w_loaded, 16 * 5)
            dve.wait_ge(consts, 5)
            with dve.Fori(0, B) as b:
                for t in range(TB):
                    dve.bn_stats(stats[:, t, :], X[:, b * TB + t, :]).then_inc(stats_done, 1)
                dve.wait_ge(stats_done, TB * b + TB)
                dve.sem_inc(waited_dve, 1)
                for t in range(TB):
                    dve.bn_aggr(mean_var[:, t, :], stats[:, t, :]).then_inc(mv_done, 1)
                dve.wait_ge(mv_done, TB * b + TB)
                dve.tensor_scalar(var_eps[:, :], mean_var[:, :, 1], LN_EPS, None, ALU.add).then_inc(veps_done, 1)
                dve.wait_ge(rstd_done, b + 1)
                for t in range(TB):
                    dve.tensor_scalar(xn[:, t, :], X[:, b * TB + t, :], mean_var[:, t, 0:1], rstd[:, t:t + 1],
                                      ALU.subtract, ALU.mult).then_inc(xn_done, 1)
                for u, (m, rows, n) in enumerate(UNITS):
                    cols = slice(n * HALF, (n + 1) * HALF)
                    dve.wait_ge(p1_done, NUN * b + u + 1)
                    dve.scalar_tensor_tensor(rest[0:rows, m, cols], psQ[0:rows, u % 4, :], bqk[0:rows, m:m + 1],
                                             part[0:rows, 0, m, cols], ALU.add, ALU.subtract).then_inc(rest_done, 1)
                dve.wait_ge(v_done, b + 1)
                for g in range(NKV):
                    dve.tensor_tensor(VA[:, b + g * B, :, 0:HD],
                                      psV[:, 0, :].rearrange("p (t g d) -> p g t d", t=TB, g=NKV)[:, g, :, :],
                                      bv[:, g * HD:(g + 1) * HD].rearrange("p (a d) -> p a d", a=1).to_broadcast([P, TB, HD]),
                                      ALU.add).then_inc(va_done, 1)

        @block.scalar
        def _(act):
            act.wait_ge(w_loaded, 16 * 5)
            with act.Fori(0, B) as b:
                for t in range(TB):
                    act.wait_ge(tr_done, TB * b + t + 1)
                    act.activation(xnT[:, :, t * P:(t + 1) * P],
                                   psT[:, t % 2, 0:KD * P].rearrange("p (k n) -> p k n", k=KD), ACT.Copy).then_inc(xnT_done, 1)
                for u, (m, rows, n) in enumerate(UNITS):
                    act.wait_ge(proj_done, NUN * b + u + 1)
                    act.activation(part[0:rows, 0, m, n * HALF:(n + 1) * HALF], psQ[0:rows, u % 4, :], ACT.Identity,
                                   bias=bqk[0:rows, m:m + 1]).then_inc(p1_done, 1)
                act.wait_ge(stored, NSTORE * b + NSTORE)

        @block.tensor
        def _(pe):
            pe.wait_ge(w_loaded, 16 * 5)
            pe.wait_ge(consts, 5)
            with pe.Fori(0, B) as b:
                for t in range(TB):
                    pe.wait_ge(xn_done, TB * b + t + 1)
                    if t >= 2:
                        pe.wait_ge(xnT_done, TB * b + t - 1)
                    for k in range(KD):
                        tr = pe.transpose(psT[:, t % 2, k * P:(k + 1) * P], xn[:, t, k * P:(k + 1) * P], ident[:, :])
                    tr.then_inc(tr_done, 1)
                pe.wait_ge(xnT_done, TB * b + TB)
                for u, (m, rows, n) in enumerate(UNITS):
                    if u >= 4:
                        pe.wait_ge(rest_done, NUN * b + u - 3)
                    for k in range(KD):
                        w = wk[:, k, :] if m == 2 else wq[:, k, m * P:(m + 1) * P]
                        mm = pe.matmul(psQ[0:rows, u % 4, :], w, xnT[:, k, n * HALF:(n + 1) * HALF],
                                       start=(k == 0), stop=(k == KD - 1))
                    mm.then_inc(proj_done, 1)
                for t in range(TB):
                    for k in range(KD):
                        mm = pe.matmul(psV[:, 0, t * NKV * HD:(t + 1) * NKV * HD], xnT[:, k, t * P:(t + 1) * P], wv[:, k, :],
                                       start=(k == 0), stop=(k == KD - 1))
                mm.then_inc(v_done, 1)
                pe.wait_ge(va_done, NKV * b + NKV)
                pe.wait_ge(rest_done, NUN * b + NUN)


def phase_attention(nc, T):
    VA, OU, q_parts, k_parts, m_parts = T["VA"], T["OU"], T["q_parts"], T["k_parts"], T["m_parts"]
    with ExitStack() as ctx:
        def sb(name, shape, dt=F32):
            return ctx.enter_context(nc.sbuf_tensor(name, shape, dt))

        def sem(name):
            return ctx.enter_context(nc.semaphore(name))

        QS = sb("QS", [P, SLOTS, GH, S], BF16)
        KS = sb("KS", [P, SLOTS, S], BF16)
        VG = sb("VG", [P, 2, TB, VW])
        PT = sb("PT", [P, 2, GH, S])
        half_max = sb("half_max", [P, NU, 2])
        neg_max = sb("neg_max", [P, NU])
        max_rest = sb("max_rest", [P, NU])
        max_parts = sb("max_parts", [P, 3, NU], BF16)
        max_parts_t = sb("max_parts_t", [P, 3, NU], BF16)
        psA = ctx.enter_context(nc.psum_tensor("psA", [P, 2, HALF], F32))
        psB = ctx.enter_context(nc.psum_tensor("psB", [P, 2, 2, HALF], F32))
        psO = ctx.enter_context(nc.psum_tensor("psO", [P, 2, HALF], F32))

        ones_set = sem("ones_set")
        waited_pool = sem("att_waited_pool")
        loaded = [sem("loaded_even"), sem("loaded_odd")]
        v_copied = sem("v_copied")
        a_done = sem("a_done")
        max_taken = sem("max_taken")
        neg_done = sem("neg_done")
        m1_done = sem("m1_done")
        mr_done = sem("mr_done")
        m2_done = sem("m2_done")
        m3_done = sem("m3_done")
        mt_done = sem("mt_done")
        m_stored = sem("m_stored")
        rows_set = [sem("rows_set_even"), sem("rows_set_odd")]
        b_done = sem("b_done")
        exp_done = sem("exp_done")
        pv_done = sem("pv_done")
        out_copied = sem("out_copied")
        NROWS = 16
        NLOAD = 16 * 6
        block = ctx.enter_context(nc.Block())

        def count(i, per, plus):
            return i * per + plus

        @block.sync
        def _(sp):
            def load(i, e):
                if not (isinstance(i, int) and i < SLOTS):
                    sp.wait_ge(pv_done, count(i, TB, -TB * (SLOTS - 1)))
                row = 0
                for kp, nq in enumerate(Q_PARTS):
                    sp.dma_start(QS[row:row + nq * HD, i % SLOTS, :, :],
                                 q_parts[i, 0:nq, :, :, :].rearrange("a d h n -> (a d) h n")).then_inc(loaded[e], 16)
                    sp.dma_start(KS[row:row + nq * HD, i % SLOTS, :],
                                 k_parts[i, kp:kp + 1, :, :].to_broadcast([nq, HD, S])).then_inc(loaded[e], 16)
                    row += nq * HD

            def rows(i, e):
                sp.wait_ge(mt_done, count(i, 1, 1))
                for part in range(3):
                    sp.dma_start(m_parts[i, part, :].rearrange("(u k n) -> k u n", k=4, n=32),
                                 max_parts_t[:, part, :]).then_inc(m_stored, 16)
                sp.wait_ge(m_stored, count(i, 48, 48))
                sp.dma_start(QS[KQ:KM, i % SLOTS, :, :].rearrange("a h n -> a (h n)"), m_parts[i, :, :]).then_inc(rows_set[e], 16)

            load(0, 0)
            load(1, 1)
            for i in range(2):
                rows(i, i)
                load(i + 2, i)
            with sp.Fori(1, NG // 2 - 1) as j:
                for e in range(2):
                    rows(j * 2 + e, e)
                    load(j * 2 + (e + 2), e)
            for i in range(NG - 2, NG):
                rows(i, i % 2)
            for e in range(2):
                sp.wait_ge(rows_set[e], NROWS * (NG // 2))

        @block.gpsimd
        def _(pool):
            pool.memset(KS[96:P, :, :], 1.0).then_inc(ones_set, 1)
            pool.wait_ge(ones_set, 1)

            def values(i, e):
                if not (isinstance(i, int) and i < 2):
                    pool.wait_ge(pv_done, count(i, TB, -TB))
                    pool.sem_inc(waited_pool, 1)
                pool.tensor_copy(VG[:, e, :, :], VA[:, i, :, :]).then_inc(v_copied, 1)

            def maxima(i):
                pool.wait_ge(v_copied, count(i, 1, 1))
                pool.wait_ge(neg_done, count(i, 1, 1))
                if not (isinstance(i, int) and i < 1):
                    pool.wait_ge(mt_done, count(i, 1, 0))
                    pool.sem_inc(waited_pool, 1)
                pool.tensor_copy(max_parts[:, 0, :], neg_max[:, :]).then_inc(m1_done, 1)
                pool.wait_ge(m1_done, count(i, 1, 1))
                pool.tensor_tensor(max_rest[:, :], neg_max[:, :], max_parts[:, 0, :], ALU.subtract).then_inc(mr_done, 1)
                pool.wait_ge(mr_done, count(i, 1, 1))
                pool.sem_inc(waited_pool, 1)
                pool.tensor_copy(max_parts[:, 1, :], max_rest[:, :]).then_inc(m2_done, 1)
                pool.wait_ge(m2_done, count(i, 1, 1))
                pool.tensor_tensor(max_parts[:, 2, :], max_rest[:, :], max_parts[:, 1, :], ALU.subtract).then_inc(m3_done, 1)
                pool.wait_ge(m3_done, count(i, 1, 1))

            for i in range(2):
                values(i, i)
                maxima(i)
            with pool.Fori(1, NG // 2) as j:
                for e in range(2):
                    values(j * 2 + e, e)
                    maxima(j * 2 + e)

        @block.vector
        def _(dve):
            def turn_parts(i):
                dve.wait_ge(m3_done, count(i, 1, 1))
                if not (isinstance(i, int) and i < 1):
                    dve.wait_ge(m_stored, count(i, 48, 0))
                dve.transpose(max_parts_t[:, :, :], max_parts[:, :, :]).then_inc(mt_done, 1)

            def maxima(i):
                if not (isinstance(i, int) and i < 1):
                    dve.wait_ge(neg_done, count(i, 1, 0))
                for u in range(NU):
                    for n in range(2):
                        dve.wait_ge(a_done, count(i, 2 * NU, 2 * u + n + 1))
                        dve.tensor_reduce(half_max[:, u, n:n + 1], psA[:, n, :], axis=AX.X, op=ALU.max).then_inc(max_taken, 1)
                    if u == TURN_AT and not (isinstance(i, int) and i < 1):
                        turn_parts(count(i, 1, -1))
                dve.wait_ge(max_taken, count(i, 2 * NU, 2 * NU))
                if not (isinstance(i, int) and i < 1):
                    dve.wait_ge(m3_done, count(i, 1, 0))
                dve.tensor_reduce(neg_max[:, :], half_max[:, :, :], axis=AX.X, op=ALU.max, negate=True).then_inc(neg_done, 1)

            maxima(0)
            maxima(1)
            with dve.Fori(1, NG // 2) as j:
                for e in range(2):
                    maxima(j * 2 + e)
            turn_parts(NG - 1)

        @block.scalar
        def _(act):
            def take_out(i):
                act.wait_ge(pv_done, count(i, TB, TB))
                act.activation(OU[:, :, :].rearrange("p g (b n) -> p (g b) n", b=B)[:, i, :], psO[:, :, :].rearrange("p a n -> p (a n)"), ACT.Copy).then_inc(out_copied, 1)

            def exps(i):
                for c in range(TB):
                    for h in range(GH):
                        u = c * GH + h
                        act.wait_ge(b_done, count(i, NU, u + 1))
                        if c >= 2 or not (isinstance(i, int) and i < 1):
                            if h == 0:
                                act.wait_ge(pv_done, count(i, TB, c - 1))
                        act.activation(PT[:, c % 2, h, :], psB[:, u % 2, :, :].rearrange("p a n -> p (a n)"), ACT.Exp,
                                       scale=SCALE).then_inc(exp_done, 1)
                    if c == 0 and not (isinstance(i, int) and i < 1):
                        take_out(count(i, 1, -1))

            exps(0)
            exps(1)
            with act.Fori(1, NG // 2) as j:
                for e in range(2):
                    exps(j * 2 + e)
            take_out(NG - 1)

        @block.tensor
        def _(pe):
            def pass_a(i, u, n):
                h, t = divmod(u, TB)
                if not (isinstance(i, int) and i == 0 and u == 0):
                    pe.wait_ge(max_taken, count(i, 2 * NU, 2 * u + n - 1))
                pe.matmul(psA[:, n, :], QS[0:KQ, i % SLOTS, h, t * P:(t + 1) * P], KS[0:KQ, i % SLOTS, n * HALF:(n + 1) * HALF],
                          start=True, stop=True).then_inc(a_done, 1)

            def pass_b(i, u):
                c, h = divmod(u, GH)
                if not (isinstance(i, int) and i == 0 and u < 2):
                    pe.wait_ge(exp_done, count(i, NU, u - 1))
                for n in range(2):
                    mm = pe.matmul(psB[:, u % 2, n, :], KS[0:KM, i % SLOTS, c * P:(c + 1) * P],
                                   QS[0:KM, i % SLOTS, h, n * HALF:(n + 1) * HALF], start=True, stop=True)
                mm.then_inc(b_done, 1)

            def times_values(i, e, c, q):
                cols = slice(q % 2 * HALF // 2, (q % 2 + 1) * HALF // 2)
                if q == 0:
                    pe.wait_ge(exp_done, count(i, NU, (c + 1) * GH))
                if c == 0 and q == 0:
                    pe.wait_ge(v_copied, count(i, 1, 1))
                    if not (isinstance(i, int) and i < 1):
                        pe.wait_ge(out_copied, count(i, 1, 0))
                for h in range(GH):
                    mm = pe.matmul(psO[h * VW:(h + 1) * VW, q // 2, cols], VG[:, e, c, :], PT[:, c % 2, h, q * S // 4:(q + 1) * S // 4],
                                   start=(c == 0 and q % 2 == 0), stop=(c == TB - 1 and q % 2 == 1))
                if q == 3:
                    mm.then_inc(pv_done, 1)

            def group(i, e):
                pe.wait_ge(rows_set[e], count(i - e, NROWS // 2, NROWS))
                for u in range(NU):
                    ahead = 1 if u < NU // 2 else 2
                    has_a = not isinstance(i, int) or i + ahead < NG
                    if u == NU // 2 and has_a:
                        pe.wait_ge(loaded[e], count(i - e, NLOAD // 2, 2 * NLOAD))
                    if has_a:
                        pass_a(i + ahead, (u + NU // 2) % NU, 0)
                    pass_b(i, u)
                    if has_a:
                        pass_a(i + ahead, (u + NU // 2) % NU, 1)
                    c, q = divmod(u - GH - 1, 4)
                    if c >= 0:
                        times_values(i, e, c, q)
                    elif not (isinstance(i, int) and i < 1):
                        times_values(i - 1, 1 - e, c + TB, q)

            pe.wait_ge(ones_set, 1)
            pe.wait_ge(loaded[0], NLOAD)
            for u in range(NU):
                for n in range(2):
                    pass_a(0, u, n)
            pe.wait_ge(loaded[1], NLOAD)
            for u in range(NU // 2):
                for n in range(2):
                    pass_a(1, u, n)
            group(0, 0)
            group(1, 1)
            with pe.Fori(1, NG // 2 - 1) as j:
                for e in range(2):
                    group(j * 2 + e, e)
            group(NG - 2, 0)
            group(NG - 1, 1)
            for u in range(NU, NU + GH + 1):
                times_values(NG - 1, 1, *divmod(u - GH - 1, 4))


XH = 16
XD = 64
SC = 77
SCP = 96
XW = XH * XD
NPR = XH // 2
XSCALE = XD ** -0.5
NEG = -1e10
NEG_RAW = NEG / XSCALE


def at(i, per, plus):
    return i * per + plus


def peeled(i, below):
    return isinstance(i, int) and i < below


def staggered(eng, n, lags, step):
    depth = max(lags) + 1
    low = depth + 1 + (depth + 1) % 2
    for s in range(low):
        step(lambda lag, s=s: (s - lag, (s - lag) % 2) if 0 <= s - lag < n else None)
    with eng.Fori(low // 2, n // 2) as j:
        for e in range(2):
            step(lambda lag, j=j, e=e: (j * 2 + (e - lag), (e - lag) % 2))
    for s in range(n, n + depth - 1):
        step(lambda lag, s=s: (s - lag, (s - lag) % 2) if 0 <= s - lag < n else None)


def phase_self_out(nc, T):
    X, OU, ident = T["X"], T["OU"], T["ident"]
    with ExitStack() as ctx:
        def sb(name, shape, dt=F32):
            return ctx.enter_context(nc.sbuf_tensor(name, shape, dt))

        def sem(name):
            return ctx.enter_context(nc.semaphore(name))

        wo = sb("wo_sb", [P, KD, D])
        bo = sb("bo_sb", [P, D])
        OT = sb("OT", [P, 2, NKV, P])
        recip = sb("recip", [P, 2, NH])
        ON = sb("ON", [P, 2, D])
        ONT = sb("ONT", [P, 2, KD, P])
        psR = ctx.enter_context(nc.psum_tensor("psR", [P, 2, HALF], F32))
        psU = ctx.enter_context(nc.psum_tensor("psU", [P, 2, HALF], F32))
        psY = ctx.enter_context(nc.psum_tensor("psY", [P, 2, HALF], F32))
        w_in = sem("so_w_in")
        bias_added = sem("so_bias_added")
        sums_in = [sem("so_sums_in_even"), sem("so_sums_in_odd")]
        rows_done = sem("so_rows_done")
        recip_done = sem("so_recip_done")
        norm_done = sem("so_norm_done")
        turned = sem("so_turned")
        turned_in = sem("so_turned_in")
        y_done = sem("so_y_done")
        x_added = sem("so_x_added")
        block = ctx.enter_context(nc.Block())

        @block.sync
        def _(sp):
            sp.dma_start(wo[:, :, :], T["Wo"].rearrange("(k p) n -> p k n", p=P)).then_inc(w_in, 16)
            sp.dma_start(bo[:, :], T["bo"].rearrange("(a n) -> a n", a=1).to_broadcast([P, D])).then_inc(w_in, 16)

            def load(i, e):
                if not peeled(i, 2):
                    sp.wait_ge(rows_done, at(i, 1, -1))
                sp.dma_start(OT[:, e, :, :], OU[:, :, bass.ds(i * P, P)]).then_inc(sums_in[e], 16)

            load(0, 0)
            load(1, 1)
            with sp.Fori(1, NT // 2) as j:
                load(j * 2, 0)
                load(j * 2 + 1, 1)
            for e in range(2):
                sp.wait_ge(sums_in[e], 16 * (NT // 2))

        @block.gpsimd
        def _(pool):
            pool.wait_ge(w_in, 32)
            with pool.Fori(0, NT) as i:
                if True:
                    pool.tensor_tensor(X[:, i, :], X[:, i, :], bo[:, :], ALU.add).then_inc(bias_added, 1)
                pool.wait_ge(bias_added, at(i, 1, 1))

        @block.tensor
        def _(pe):
            pe.wait_ge(w_in, 32)

            def step(tile):
                if t := tile(2):
                    i, e = t
                    pe.wait_ge(turned_in, at(i, 1, 1))
                    if not peeled(i, 2):
                        pe.wait_ge(x_added, at(i, 1, -1))
                    for k in range(KD):
                        mm = pe.matmul(psY[:, e, 0:D], ONT[:, e, k, :], wo[:, k, :], start=(k == 0), stop=(k == KD - 1))
                    mm.then_inc(y_done, 1)
                if t := tile(1):
                    i, e = t
                    pe.wait_ge(norm_done, at(i, 1, 1))
                    if not peeled(i, 2):
                        pe.wait_ge(turned_in, at(i, 1, -1))
                    for k in range(KD):
                        mm = pe.transpose(psU[:, e, k * P:(k + 1) * P], ON[:, e, k * P:(k + 1) * P], ident[:, :])
                    mm.then_inc(turned, 1)
                if t := tile(0):
                    i, e = t
                    pe.wait_ge(sums_in[e], at(i - e, 8, 16))
                    if not peeled(i, 2):
                        pe.wait_ge(norm_done, at(i, 1, -1))
                    for g in range(NKV):
                        mm = pe.transpose(psR[:, e, g * P:(g + 1) * P], OT[:, e, g, :], ident[:, :])
                    mm.then_inc(rows_done, 1)

            staggered(pe, NT, (0, 1, 2), step)

        @block.vector
        def _(dve):
            def step(tile):
                if t := tile(0):
                    i, e = t
                    rows = psR[:, e, :].rearrange("p (h r) -> p h r", r=VW)
                    dve.wait_ge(rows_done, at(i, 1, 1))
                    if not peeled(i, 2):
                        dve.wait_ge(norm_done, at(i, 1, -1))
                        dve.wait_ge(turned, at(i, 1, -1))
                    dve.reciprocal(recip[:, e, :], rows[:, :, HD]).then_inc(recip_done, 1)
                    dve.wait_ge(recip_done, at(i, 1, 1))
                    dve.tensor_tensor(ON[:, e, :].rearrange("p (h d) -> p h d", d=HD), rows[:, :, 0:HD],
                                      recip[:, e, :].rearrange("p (h a) -> p h a", a=1).to_broadcast([P, NH, HD]),
                                      ALU.mult).then_inc(norm_done, 1)
                if t := tile(2):
                    i, e = t
                    dve.wait_ge(y_done, at(i, 1, 1))
                    dve.wait_ge(bias_added, at(i, 1, 1))
                    dve.tensor_tensor(X[:, i, :], psY[:, e, 0:D], X[:, i, :], ALU.add).then_inc(x_added, 1)

            staggered(dve, NT, (0, 1, 2), step)

        @block.scalar
        def _(act):
            def copy(i, e):
                act.wait_ge(turned, at(i, 1, 1))
                if not peeled(i, 2):
                    act.wait_ge(y_done, at(i, 1, -1))
                act.activation(ONT[:, e, :, :], psU[:, e, 0:D].rearrange("p (k n) -> p k n", k=KD), ACT.Copy).then_inc(turned_in, 1)

            copy(0, 0)
            copy(1, 1)
            with act.Fori(1, NT // 2) as j:
                copy(j * 2, 0)
                copy(j * 2 + 1, 1)


def phase_context(nc, T):
    ident, KX, VX = T["ident"], T["KX"], T["VX"]
    with ExitStack() as ctx:
        def sb(name, shape, dt=F32):
            return ctx.enter_context(nc.sbuf_tensor(name, shape, dt))

        def sem(name):
            return ctx.enter_context(nc.semaphore(name))

        wk = sb("wkx_sb", [P, KD, XW])
        wv = sb("wvx_sb", [P, KD, XW])
        cx = sb("cx", [SC, 2, D])
        cxT = sb("cxT", [P, KD, SC])
        psT = ctx.enter_context(nc.psum_tensor("psTc", [P, KD, P], F32))
        psK = ctx.enter_context(nc.psum_tensor("psKc", [P, 2, HALF], F32))
        psV = ctx.enter_context(nc.psum_tensor("psVc", [P, 2, HALF], F32))
        w_in = sem("cx_w_in")
        cleared = sem("cx_cleared")
        c_in = [sem("cx_in_even"), sem("cx_in_odd")]
        turned = sem("cx_turned")
        turned_in = sem("cx_turned_in")
        k_done = sem("cx_k_done")
        k_in = sem("cx_k_in")
        v_done = sem("cx_v_done")
        v_in = sem("cx_v_in")
        block = ctx.enter_context(nc.Block())

        @block.sync
        def _(sp):
            sp.dma_start(wk[:, :, :], T["Wkx"].rearrange("(k p) n -> p k n", p=P)).then_inc(w_in, 16)
            sp.dma_start(wv[:, :, :], T["Wvx"].rearrange("(k p) n -> p k n", p=P)).then_inc(w_in, 16)
            for b in range(B):
                if b >= 2:
                    sp.wait_ge(turned, b - 1)
                sp.dma_start(cx[:, b % 2, :], T["ctx"][b, :, :]).then_inc(c_in[b % 2], 16)

        @block.gpsimd
        def _(pool):
            pool.memset(KX[:, :, :, :], 0.0).then_inc(cleared, 1)
            pool.wait_ge(cleared, 1)
            pool.memset(VX[:, :, :], 0.0).then_inc(cleared, 1)

        @block.tensor
        def _(pe):
            pe.wait_ge(w_in, 32)
            for b in range(B):
                pe.wait_ge(c_in[b % 2], 16 * (b // 2 + 1))
                if b:
                    pe.wait_ge(turned_in, b)
                for k in range(KD):
                    mm = pe.transpose(psT[:, k, 0:SC], cx[:, b % 2, k * P:(k + 1) * P], ident[0:SC, 0:SC])
                mm.then_inc(turned, 1)
                pe.wait_ge(turned_in, b + 1)
                for r in range(NPR):
                    if b and r % 4 == 0:
                        pe.wait_ge(k_in, 4 * (b - 1) + 2 * (r // 4) + 2)
                    for k in range(KD):
                        mm = pe.matmul(psK[:, r // 4, (r % 4) * SC:(r % 4 + 1) * SC], wk[:, k, r * P:(r + 1) * P], cxT[:, k, :],
                                       start=(k == 0), stop=(k == KD - 1))
                    if r % 4 == 3:
                        mm.then_inc(k_done, 1)
                for n in range(2):
                    if b:
                        pe.wait_ge(v_in, 2 * (b - 1) + n + 1)
                    for k in range(KD):
                        mm = pe.matmul(psV[0:SC, n, :], cxT[:, k, :], wv[:, k, n * HALF:(n + 1) * HALF],
                                       start=(k == 0), stop=(k == KD - 1))
                    mm.then_inc(v_done, 1)

        @block.vector
        def _(dve):
            dve.wait_ge(cleared, 2)
            for b in range(B):
                for n in range(2):
                    dve.wait_ge(v_done, 2 * b + n + 1)
                    dve.tensor_copy(VX[0:SC, b, n * HALF:(n + 1) * HALF], psV[0:SC, n, :]).then_inc(v_in, 1)

        @block.scalar
        def _(act):
            act.wait_ge(cleared, 2)
            for b in range(B):
                act.wait_ge(turned, b + 1)
                if b:
                    act.wait_ge(v_done, 2 * b)
                act.activation(cxT[:, :, :], psT[:, :, 0:SC], ACT.Copy).then_inc(turned_in, 1)
                for q in range(2):
                    act.wait_ge(k_done, 2 * b + q + 1)
                    for half in range(2):
                        rows = slice(half * XD, (half + 1) * XD)
                        act.activation(KX[rows, b, 4 * q:4 * q + 4, half * SC:(half + 1) * SC],
                                       psK[rows, q, 0:4 * SC].rearrange("p (r n) -> p r n", n=SC), ACT.Copy).then_inc(k_in, 1)


def phase_cross(nc, T):
    X, ident, KX, VX = T["X"], T["ident"], T["KX"], T["VX"]
    with ExitStack() as ctx:
        def sb(name, shape, dt=F32):
            return ctx.enter_context(nc.sbuf_tensor(name, shape, dt))

        def sem(name):
            return ctx.enter_context(nc.semaphore(name))

        wq = sb("wqx_sb", [P, KD, XW])
        wo = sb("wox_sb", [P, NPR, D])
        mask = sb("mask_sb", [P, 2, SC], I32)
        stats = sb("x_stats", [P, 2, 6])
        mean_var = sb("x_mean_var", [P, 2, 2])
        var_eps = sb("x_var_eps", [P, 2])
        neg_half = sb("x_neg_half", [P, 1])
        rstd = sb("x_rstd", [P, 2])
        xn = sb("x_xn", [P, 2, D])
        xnT = sb("x_xnT", [P, 2, KD, P])
        qT = sb("x_qT", [P, 2, NPR, P])
        SX = sb("x_scores", [P, 2, XH, SCP])
        row_max = sb("x_row_max", [P, XH])
        row_sum = sb("x_row_sum", [P, 2, XH])
        recip = sb("x_recip", [P, 2, XH])
        ET = sb("x_ET", [SCP, XH, P])
        ON = sb("x_ON", [P, XH, XD])
        OT = sb("x_OT", [P, NPR, P])
        ps = ctx.enter_context(nc.psum_tensor("ps_cross", [P, 8, HALF], F32))
        Q, OTU, E, SU, XT, Y, O = 0, 2, 4, 8, 12, 13, 14
        L_LN, L_XT, L_Q, L_SM, L_E, L_O = 0, 1, 2, 3, 4, 5

        w_in = sem("x_w_in")
        mask_in = [sem("x_mask_in_even"), sem("x_mask_in_odd")]
        const = sem("x_const")
        waited_pool = sem("x_waited_pool")
        waited_dve = sem("x_waited_dve")
        filled = sem("x_filled")
        stats_done = sem("x_stats_done")
        mv_done = sem("x_mv_done")
        veps_done = sem("x_veps_done")
        rstd_done = sem("x_rstd_done")
        xn_done = sem("x_xn_done")
        xt_done, xt_in = sem("x_xt_done"), sem("x_xt_in")
        q_done, q_in = sem("x_q_done"), sem("x_q_in")
        s_done, s_in = sem("x_s_done"), sem("x_s_in")
        max_done = sem("x_max_done")
        sub_done = sem("x_sub_done")
        exp_done = sem("x_exp_done")
        sum_done = sem("x_sum_done")
        recip_done = sem("x_recip_done")
        e_done, e_in = sem("x_e_done"), sem("x_e_in")
        o_done, o_in = sem("x_o_done"), sem("x_o_in")
        ot_done, ot_in = sem("x_ot_done"), sem("x_ot_in")
        y_done, y_in = sem("x_y_done"), sem("x_y_in")
        block = ctx.enter_context(nc.Block())

        @block.sync
        def _(sp):
            sp.dma_start(wq[:, :, :], T["Wqx"].rearrange("(k p) n -> p k n", p=P)).then_inc(w_in, 16)
            sp.dma_start(wo[:, :, :], T["Wox"].rearrange("(k p) n -> p k n", p=P)).then_inc(w_in, 16)
            mk = T["mask"].rearrange("b (t p) n -> (b t) p n", p=P)
            def load(i, e):
                if not peeled(i, 2):
                    sp.wait_ge(s_in, at(i, 4, -4))
                sp.dma_start(mask[:, e, :], mk[i, :, :]).then_inc(mask_in[e], 16)

            load(0, 0)
            load(1, 1)
            with sp.Fori(1, NT // 2) as j:
                load(j * 2, 0)
                load(j * 2 + 1, 1)
            for e in range(2):
                sp.wait_ge(mask_in[e], 16 * (NT // 2))

        @block.gpsimd
        def _(pool):
            pool.memset(neg_half[:, :], -0.5).then_inc(const, 1)
            pool.wait_ge(const, 1)
            pool.memset(SX[:, :, :, :], 0.0).then_inc(const, 1)
            pool.wait_ge(const, 2)

            def step(tile):
                if t := tile(L_LN):
                    i, e = t
                    pool.wait_ge(veps_done, at(i, 1, 1))
                    pool.tensor_tensor(rstd[:, e:e + 1], var_eps[:, e:e + 1], neg_half[:, :], ALU.pow).then_inc(rstd_done, 1)
                    pool.wait_ge(rstd_done, at(i, 1, 1))
                if t := tile(L_Q):
                    i, e = t
                    if not peeled(i, 2):
                        pool.wait_ge(e_done, at(i, 4, -4))
                        pool.wait_ge(sum_done, at(i, 1, -1))
                        pool.sem_inc(waited_pool, 1)
                    pool.memset(SX[:, e, :, 0:SC], NEG_RAW).then_inc(filled, 1)
                    pool.wait_ge(filled, at(i, 1, 1))

            staggered(pool, NT, range(6), step)

        @block.tensor
        def _(pe):
            pe.wait_ge(w_in, 32)

            READ = {Q: (2, L_Q, q_in), OTU: (2, L_O, ot_in), E: (4, L_E, e_in), SU: (4, L_Q, s_in),
                    XT: (1, L_XT, xt_in), Y: (1, L_O, y_in), O: (2, L_E, o_in)}

            def unit_of(u):
                base = max(b for b in READ if b <= u)
                return (base,) + READ[base]

            def bank_free(tile, u):
                base, n, lag, read = unit_of(u)
                i, _ = tile(lag)
                if not peeled(i, 1):
                    pe.wait_ge(read, at(i, n, u - base + 1 - n))
                base, n, lag, read = unit_of((u + 8) % 16)
                t = tile(lag) if u >= 8 else tile(lag + 1)
                if t:
                    pe.wait_ge(read, at(t[0], n, (u + 8) % 16 - base + 1))

            def step(tile):
                if t := tile(L_Q):
                    i, e = t
                    pe.wait_ge(xt_in, at(i, 1, 1))
                    for n in range(2):
                        bank_free(tile, Q + n)
                        for r in range(4):
                            for k in range(KD):
                                pair = 4 * n + r
                                mm = pe.matmul(ps[:, (Q + n) % 8, r * P:(r + 1) * P], wq[:, k, pair * P:(pair + 1) * P],
                                               xnT[:, e, k, :], start=(k == 0), stop=(k == KD - 1))
                        mm.then_inc(q_done, 1)
                if t := tile(L_O):
                    i, e = t
                    for n in range(2):
                        bank_free(tile, OTU + n)
                        pe.wait_ge(o_in, at(i, 2, n + 1))
                        for r in range(4):
                            pair = 4 * n + r
                            mm = pe.transpose(ps[:, (OTU + n) % 8, r * P:(r + 1) * P], ON[:, 2 * pair:2 * pair + 2, :], ident[:, :])
                        mm.then_inc(ot_done, 1)
                if t := tile(L_E):
                    i, e = t
                    pe.wait_ge(exp_done, at(i, 1, 1))
                    for n in range(4):
                        bank_free(tile, E + n)
                        for h in range(4):
                            mm = pe.transpose(ps[0:SCP, (E + n) % 8, h * P:(h + 1) * P], SX[:, e, 4 * n + h, :], ident[:, :])
                        mm.then_inc(e_done, 1)
                if t := tile(L_Q):
                    i, e = t
                    for n in range(4):
                        bank_free(tile, SU + n)
                        for r in range(2):
                            pair = 2 * n + r
                            mm = pe.matmul(ps[:, (SU + n) % 8, r * 2 * SC:(r + 1) * 2 * SC], qT[:, e, pair, :],
                                           KX[:, i // TB, pair, :], start=True, stop=True)
                        mm.then_inc(s_done, 1)
                if t := tile(L_XT):
                    i, e = t
                    bank_free(tile, XT)
                    pe.wait_ge(xn_done, at(i, 1, 1))
                    for k in range(KD):
                        mm = pe.transpose(ps[:, XT % 8, k * P:(k + 1) * P], xn[:, e, k * P:(k + 1) * P], ident[:, :])
                    mm.then_inc(xt_done, 1)
                if t := tile(L_O):
                    i, e = t
                    bank_free(tile, Y)
                    pe.wait_ge(ot_in, at(i, 2, 2))
                    for k in range(NPR):
                        mm = pe.matmul(ps[:, Y % 8, 0:D], OT[:, k, :], wo[:, k, :], start=(k == 0), stop=(k == NPR - 1))
                    mm.then_inc(y_done, 1)
                if t := tile(L_E):
                    i, e = t
                    for n in range(2):
                        bank_free(tile, O + n)
                        for h in range(8):
                            head = 8 * n + h
                            mm = pe.matmul(ps[:, (O + n) % 8, h * XD:(h + 1) * XD], ET[:, head, :],
                                           VX[:, i // TB, head * XD:(head + 1) * XD], start=True, stop=True)
                        mm.then_inc(o_done, 1)

            staggered(pe, NT, range(6), step)

        @block.vector
        def _(dve):
            dve.wait_ge(const, 2)

            def step(tile):
                if t := tile(L_O):
                    i, e = t
                    dve.wait_ge(recip_done, at(i, 1, 1))
                    for n in range(2):
                        dve.wait_ge(o_done, at(i, 2, n + 1))
                        if not peeled(i, 1):
                            dve.wait_ge(ot_done, at(i, 2, n - 1))
                        dve.tensor_tensor(ON[:, 8 * n:8 * n + 8, :], ps[:, (O + n) % 8, :].rearrange("p (h d) -> p h d", d=XD),
                                          recip[:, e, 8 * n:8 * n + 8].rearrange("p (h a) -> p h a", a=1).to_broadcast([P, 8, XD]),
                                          ALU.mult).then_inc(o_in, 1)
                if t := tile(L_E):
                    i, e = t
                    dve.wait_ge(exp_done, at(i, 1, 1))
                    dve.tensor_reduce(row_sum[:, e, :], SX[:, e, :, 0:SC], axis=AX.X, op=ALU.add).then_inc(sum_done, 1)
                    dve.wait_ge(sum_done, at(i, 1, 1))
                    dve.reciprocal(recip[:, e, :], row_sum[:, e, :]).then_inc(recip_done, 1)
                if t := tile(L_SM):
                    i, e = t
                    dve.wait_ge(s_in, at(i, 4, 4))
                    dve.tensor_reduce(row_max[:, :], SX[:, e, :, 0:SC], axis=AX.X, op=ALU.max).then_inc(max_done, 1)
                    dve.wait_ge(max_done, at(i, 1, 1))
                    dve.tensor_tensor(SX[:, e, :, 0:SC], SX[:, e, :, 0:SC],
                                      row_max[:, :].rearrange("p (h a) -> p h a", a=1).to_broadcast([P, XH, SC]),
                                      ALU.subtract).then_inc(sub_done, 1)
                if t := tile(L_LN):
                    i, e = t
                    dve.bn_stats(stats[:, e, :], X[:, i, :]).then_inc(stats_done, 1)
                    dve.wait_ge(stats_done, at(i, 1, 1))
                    dve.sem_inc(waited_dve, 1)
                    dve.bn_aggr(mean_var[:, e, :], stats[:, e, :]).then_inc(mv_done, 1)
                    dve.wait_ge(mv_done, at(i, 1, 1))
                    dve.tensor_scalar(var_eps[:, e:e + 1], mean_var[:, e, 1:2], LN_EPS, None, ALU.add).then_inc(veps_done, 1)
                if t := tile(L_Q):
                    i, e = t
                    dve.wait_ge(filled, at(i, 1, 1))
                    dve.wait_ge(mask_in[e], at(i - e, 8, 16))
                    for n in range(4):
                        dve.wait_ge(s_done, at(i, 4, n + 1))
                        dve.sem_inc(waited_dve, 1)
                        dve.copy_predicated(SX[:, e, 4 * n:4 * n + 4, 0:SC], mask[:, e, :].rearrange("p (a n) -> p a n", a=1).to_broadcast([P, 4, SC]),
                                            ps[:, (SU + n) % 8, 0:4 * SC].rearrange("p (h n) -> p h n", n=SC)).then_inc(s_in, 1)
                if t := tile(L_LN):
                    i, e = t
                    dve.wait_ge(rstd_done, at(i, 1, 1))
                    if not peeled(i, 2):
                        dve.wait_ge(xt_done, at(i, 1, -1))
                    dve.tensor_scalar(xn[:, e, :], X[:, i, :], mean_var[:, e, 0:1], rstd[:, e:e + 1],
                                      ALU.subtract, ALU.mult).then_inc(xn_done, 1)
                if t := tile(L_O):
                    i, e = t
                    dve.wait_ge(y_done, at(i, 1, 1))
                    dve.tensor_tensor(X[:, i, :], ps[:, Y % 8, 0:D], X[:, i, :], ALU.add).then_inc(y_in, 1)

            staggered(dve, NT, range(6), step)

        @block.scalar
        def _(act):
            def step(tile):
                if t := tile(L_Q):
                    i, e = t
                    for n in range(2):
                        act.wait_ge(q_done, at(i, 2, n + 1))
                        if not peeled(i, 2):
                            act.wait_ge(s_done, at(i, 4, -4))
                        act.activation(qT[:, e, 4 * n:4 * n + 4, :], ps[:, (Q + n) % 8, :].rearrange("p (r n) -> p r n", n=P),
                                       ACT.Copy).then_inc(q_in, 1)
                if t := tile(L_O):
                    i, e = t
                    for n in range(2):
                        act.wait_ge(ot_done, at(i, 2, n + 1))
                        if not peeled(i, 1):
                            act.wait_ge(y_done, at(i, 1, 0))
                        act.activation(OT[:, 4 * n:4 * n + 4, :], ps[:, (OTU + n) % 8, :].rearrange("p (r n) -> p r n", n=P),
                                       ACT.Copy).then_inc(ot_in, 1)
                if t := tile(L_E):
                    i, e = t
                    for n in range(4):
                        act.wait_ge(e_done, at(i, 4, n + 1))
                        if not peeled(i, 1):
                            act.wait_ge(o_done, at(i, 2, n // 2 - 1))
                        act.activation(ET[:, 4 * n:4 * n + 4, :], ps[0:SCP, (E + n) % 8, :].rearrange("p (h n) -> p h n", n=P),
                                       ACT.Copy).then_inc(e_in, 1)
                if t := tile(L_SM):
                    i, e = t
                    act.wait_ge(sub_done, at(i, 1, 1))
                    act.activation(SX[:, e, :, 0:SC], SX[:, e, :, 0:SC], ACT.Exp, scale=XSCALE).then_inc(exp_done, 1)
                if t := tile(L_XT):
                    i, e = t
                    act.wait_ge(xt_done, at(i, 1, 1))
                    if not peeled(i, 2):
                        act.wait_ge(q_done, at(i, 2, -2))
                    act.activation(xnT[:, e, :, :], ps[:, XT % 8, 0:D].rearrange("p (k n) -> p k n", n=P), ACT.Copy).then_inc(xt_in, 1)

            staggered(act, NT, range(6), step)


NE = 8
TOP = 2
FI = 512
KF = FI // P
TOPK_EPS = 1e-5
NTM = (TOP * B * S + NE * (P - 1)) // P
NTM += NTM % 2
NSLOT = NTM * P


def phase_shared(nc, T):
    X, XF, LG, ident = T["X"], T["XF"], T["LG"], T["ident"]
    WG, WU, WD = T["WG"], T["WU"], T["WD"]
    with ExitStack() as ctx:
        def sb(name, shape, dt=F32):
            return ctx.enter_context(nc.sbuf_tensor(name, shape, dt))

        def sem(name):
            return ctx.enter_context(nc.semaphore(name))

        wg = sb("swg_sb", [P, KD, FI])
        wu = sb("swu_sb", [P, KD, FI])
        wd = sb("swd_sb", [P, KF, D])
        gate = sb("gate_sb", [P, KD, NE])
        affine = sb("affine_sb", [P, 2, KD])
        stats = sb("f_stats", [P, 2, 2, 6])
        mean_var = sb("f_mean_var", [P, 2, 2, 2])
        var_eps = sb("f_var_eps", [P, 2, 2])
        neg_half = sb("f_neg_half", [P, 1])
        rstd = sb("f_rstd", [P, 2, 2])
        xf = sb("f_xf", [P, 2, D])
        xr = sb("f_xr", [P, 2, D])
        xfT = sb("f_xfT", [P, 2, KD, P])
        xrT = sb("f_xrT", [P, 2, KD, P])
        SG = sb("f_silu", [P, 2, FI])
        H = sb("f_h", [P, 2, FI])
        HT = sb("f_hT", [P, 2, KF, P])
        psG = ctx.enter_context(nc.psum_tensor("f_psG", [P, 2, HALF], F32))
        psU = ctx.enter_context(nc.psum_tensor("f_psU", [P, 2, HALF], F32))
        psT = ctx.enter_context(nc.psum_tensor("f_psT", [P, 1, HALF], F32))
        psL = ctx.enter_context(nc.psum_tensor("f_psL", [P, 1, HALF], F32))
        psH = ctx.enter_context(nc.psum_tensor("f_psH", [P, 1, HALF], F32))
        psY = ctx.enter_context(nc.psum_tensor("f_psY", [P, 1, HALF], F32))
        w_in = sem("f_w_in")
        const = sem("f_const")
        waited_dve = sem("f_waited_dve")
        experts_in = sem("f_experts_in")
        stats_done = [sem("f_stats1"), sem("f_stats2")]
        mv_done = [sem("f_mv1"), sem("f_mv2")]
        veps_done = [sem("f_veps1"), sem("f_veps2")]
        rstd_done = [sem("f_rstd1"), sem("f_rstd2")]
        xf_done = sem("f_xf_done")
        xf_kept = sem("f_xf_kept")
        xr_done = sem("f_xr_done")
        t_done, xf_in, xr_in = sem("f_t_done"), sem("f_xf_in"), sem("f_xr_in")
        g_done, u_done, l_done = sem("f_g_done"), sem("f_u_done"), sem("f_l_done")
        silu_done, h_done, l_in = sem("f_silu_done"), sem("f_h_done"), sem("f_l_in")
        ht_done, ht_in = sem("f_ht_done"), sem("f_ht_in")
        y_done, y_in = sem("f_y_done"), sem("f_y_in")
        block = ctx.enter_context(nc.Block())

        @block.sync
        def _(sp):
            sp.dma_start(wg[:, :, :], T["sWg"].rearrange("(k p) n -> p k n", p=P)).then_inc(w_in, 16)
            sp.dma_start(wu[:, :, :], T["sWu"].rearrange("(k p) n -> p k n", p=P)).then_inc(w_in, 16)
            sp.dma_start(wd[:, :, :], T["sWd"].rearrange("(k p) n -> p k n", p=P)).then_inc(w_in, 16)
            sp.dma_start(gate[:, :, :], T["gateT"].rearrange("(k p) n -> p k n", p=P)).then_inc(w_in, 16)
            sp.dma_start(affine[:, :, :], T["affine"]).then_inc(w_in, 16)
            for x in range(NE):
                sp.dma_start(WG[:, x, :, :], T["Wg"][x, :, :].rearrange("(k p) n -> p k n", p=P)).then_inc(experts_in, 16)
                sp.dma_start(WU[:, x, :, :], T["Wu"][x, :, :].rearrange("(k p) n -> p k n", p=P)).then_inc(experts_in, 16)
                sp.dma_start(WD[:, x, :, :], T["Wd"][x, :, :].rearrange("(k p) n -> p k n", p=P)).then_inc(experts_in, 16)
            sp.wait_ge(experts_in, 16 * 3 * NE)

        @block.gpsimd
        def _(pool):
            pool.memset(neg_half[:, :], -0.5).then_inc(const, 1)
            pool.wait_ge(const, 1)

            def step(tile):
                for which in range(2):
                    if t := tile(which):
                        i, e = t
                        pool.wait_ge(veps_done[which], at(i, 1, 1))
                        pool.tensor_tensor(rstd[:, which, e:e + 1], var_eps[:, which, e:e + 1], neg_half[:, :],
                                           ALU.pow).then_inc(rstd_done[which], 1)
                        pool.wait_ge(rstd_done[which], at(i, 1, 1))

            staggered(pool, NT, range(5), step)

        @block.tensor
        def _(pe):
            pe.wait_ge(w_in, 16 * 5)

            def step(tile):
                if t := tile(3):
                    i, e = t
                    pe.wait_ge(xf_in, at(i, 1, 1))
                    for w, psum, done, read in ((wg, psG, g_done, silu_done), (wu, psU, u_done, h_done)):
                        if not peeled(i, 2):
                            pe.wait_ge(read, at(i, 1, -1))
                        for k in range(KD):
                            mm = pe.matmul(psum[:, e, :], xfT[:, e, k, :], w[:, k, :], start=(k == 0), stop=(k == KD - 1))
                        mm.then_inc(done, 1)
                    pe.wait_ge(xr_in, at(i, 1, 1))
                    if not peeled(i, 1):
                        pe.wait_ge(l_in, at(i, 1, 0))
                    for k in range(KD):
                        mm = pe.matmul(psL[:, 0, 0:NE], xrT[:, e, k, :], gate[:, k, :], start=(k == 0), stop=(k == KD - 1))
                    mm.then_inc(l_done, 1)
                if t := tile(4):
                    i, e = t
                    pe.wait_ge(h_done, at(i, 1, 1))
                    if not peeled(i, 1):
                        pe.wait_ge(ht_in, at(i, 1, 0))
                    for k in range(KF):
                        mm = pe.transpose(psH[:, 0, k * P:(k + 1) * P], H[:, e, k * P:(k + 1) * P], ident[:, :])
                    mm.then_inc(ht_done, 1)
                if t := tile(2):
                    i, e = t
                    pe.wait_ge(xr_done, at(i, 1, 1))
                    if not peeled(i, 1):
                        pe.wait_ge(xf_in, at(i, 1, 0))
                        pe.wait_ge(xr_in, at(i, 1, 0))
                    for k in range(KD):
                        pe.transpose(psT[:, 0, k * P:(k + 1) * P], xf[:, e, k * P:(k + 1) * P], ident[:, :])
                    for k in range(KD):
                        mm = pe.transpose(psT[:, 0, (KD + k) * P:(KD + k + 1) * P], xr[:, e, k * P:(k + 1) * P], ident[:, :])
                    mm.then_inc(t_done, 1)
                if t := tile(4):
                    i, e = t
                    pe.wait_ge(ht_in, at(i, 1, 1))
                    if not peeled(i, 1):
                        pe.wait_ge(y_in, at(i, 1, 0))
                    for k in range(KF):
                        mm = pe.matmul(psY[:, 0, 0:D], HT[:, e, k, :], wd[:, k, :], start=(k == 0), stop=(k == KF - 1))
                    mm.then_inc(y_done, 1)

            staggered(pe, NT, range(5), step)

        @block.vector
        def _(dve):
            def statistics(i, e, which, source):
                dve.bn_stats(stats[:, which, e, :], source).then_inc(stats_done[which], 1)
                dve.wait_ge(stats_done[which], at(i, 1, 1))
                dve.sem_inc(waited_dve, 1)
                dve.bn_aggr(mean_var[:, which, e, :], stats[:, which, e, :]).then_inc(mv_done[which], 1)
                dve.wait_ge(mv_done[which], at(i, 1, 1))
                dve.tensor_scalar(var_eps[:, which, e:e + 1], mean_var[:, which, e, 1:2], LN_EPS, None,
                                  ALU.add).then_inc(veps_done[which], 1)

            def step(tile):
                if t := tile(2):
                    i, e = t
                    dve.wait_ge(rstd_done[1], at(i, 1, 1))
                    if not peeled(i, 2):
                        dve.wait_ge(t_done, at(i, 1, -1))
                    dve.tensor_scalar(xr[:, e, :], xf[:, e, :], mean_var[:, 1, e, 0:1], rstd[:, 1, e:e + 1],
                                      ALU.subtract, ALU.mult).then_inc(xr_done, 1)
                if t := tile(0):
                    i, e = t
                    statistics(i, e, 0, X[:, i, :])
                if t := tile(1):
                    i, e = t
                    dve.wait_ge(rstd_done[0], at(i, 1, 1))
                    if not peeled(i, 2):
                        dve.wait_ge(t_done, at(i, 1, -1))
                        dve.wait_ge(xf_kept, at(i, 1, -1))
                    dve.tensor_scalar(xf[:, e, :], X[:, i, :], mean_var[:, 0, e, 0:1], rstd[:, 0, e:e + 1],
                                      ALU.subtract, ALU.mult).then_inc(xf_done, 1)
                    dve.wait_ge(xf_done, at(i, 1, 1))
                    statistics(i, e, 1, xf[:, e, :])
                if t := tile(3):
                    i, e = t
                    dve.wait_ge(silu_done, at(i, 1, 1))
                    dve.wait_ge(u_done, at(i, 1, 1))
                    if not peeled(i, 2):
                        dve.wait_ge(ht_done, at(i, 1, -1))
                    dve.tensor_tensor(H[:, e, :], psU[:, e, :], SG[:, e, :], ALU.mult).then_inc(h_done, 1)
                    dve.wait_ge(l_done, at(i, 1, 1))
                    dve.tensor_copy(LG[:, i, :], psL[:, 0, 0:NE]).then_inc(l_in, 1)
                if t := tile(4):
                    i, e = t
                    dve.wait_ge(y_done, at(i, 1, 1))
                    dve.tensor_tensor(X[:, i, :], psY[:, 0, 0:D], X[:, i, :], ALU.add).then_inc(y_in, 1)

            staggered(dve, NT, range(5), step)

        @block.scalar
        def _(act):
            act.wait_ge(w_in, 16 * 5)

            def step(tile):
                if t := tile(3):
                    i, e = t
                    act.wait_ge(g_done, at(i, 1, 1))
                    if not peeled(i, 2):
                        act.wait_ge(h_done, at(i, 1, -1))
                    act.activation(SG[:, e, :], psG[:, e, :], ACT.Silu).then_inc(silu_done, 1)
                if t := tile(4):
                    i, e = t
                    act.wait_ge(ht_done, at(i, 1, 1))
                    if not peeled(i, 2):
                        act.wait_ge(y_done, at(i, 1, -1))
                    act.activation(HT[:, e, :, :], psH[:, 0, :].rearrange("p (k n) -> p k n", n=P), ACT.Copy).then_inc(ht_in, 1)
                if t := tile(2):
                    i, e = t
                    act.wait_ge(t_done, at(i, 1, 1))
                    if not peeled(i, 2):
                        act.wait_ge(u_done, at(i, 1, -1))
                    act.activation(xfT[:, e, :, :], psT[:, 0, 0:D].rearrange("p (k n) -> p k n", n=P), ACT.Copy).then_inc(xf_in, 1)
                    if not peeled(i, 2):
                        act.wait_ge(l_done, at(i, 1, -1))
                    for k in range(KD):
                        ins = act.activation(xrT[:, e, k, :], psT[:, 0, (KD + k) * P:(KD + k + 1) * P], ACT.Identity,
                                             scale=affine[:, 0, k:k + 1], bias=affine[:, 1, k:k + 1])
                    ins.then_inc(xr_in, 1)
                if t := tile(1):
                    i, e = t
                    act.wait_ge(xf_done, at(i, 1, 1))
                    act.activation(XF[:, i, :], xf[:, e, :], ACT.Copy).then_inc(xf_kept, 1)

            staggered(act, NT, range(5), step)


def phase_route(nc, T):
    LG, XF, W12, POS = T["LG"], T["XF"], T["W12"], T["POS"]
    tile_expert, xs = T["tile_expert"], T["xs"]
    with ExitStack() as ctx:
        def sb(name, shape, dt=F32):
            return ctx.enter_context(nc.sbuf_tensor(name, shape, dt))

        def sem(name):
            return ctx.enter_context(nc.semaphore(name))

        A3 = [P, NT, NE]
        top = sb("r_top", [P, NT])
        ex = sb("r_ex", A3)
        total = sb("r_total", [P, NT])
        probs = sb("r_probs", A3)
        order = sb("r_order", [P, NE])
        value = sb("r_value", A3)
        best = sb("r_best", [P, 2, NT])
        pick = sb("r_pick", [P, NT])
        chosen = sb("r_chosen", [P, 2, NT, NE])
        both = sb("r_both", A3)
        den = sb("r_den", [P, NT])
        before = sb("r_before", [P, P])
        ones = sb("r_ones", [P, P])
        sums = sb("r_sums", [P, 2, NT, NE])
        counts = sb("r_counts", [P, NE])
        counts_i = sb("r_counts_i", [P, NE], I32)
        tiles = sb("r_tiles", [P, NE])
        ends = sb("r_ends", [P, 2, NE])
        slot = sb("r_slot", A3)
        slot_of = sb("r_slot_of", [P, 2, NT])
        tile_no = sb("r_tile_no", [P, NTM])
        expert = sb("r_expert", [P, NTM])
        ps = ctx.enter_context(nc.psum_tensor("r_ps", [P, 2, NT, NE], F32))
        const = sem("r_const")
        step_done = sem("r_step_done")
        max_off = sem("r_max_off")
        exp_done = sem("r_exp_done")
        chosen_done = sem("r_chosen_done")
        counted = sem("r_counted")
        slots_done = sem("r_slots_done")
        scattered = sem("r_scattered")
        block = ctx.enter_context(nc.Block())

        def over_e(ap):
            return ap.rearrange("p (t a) -> p t a", a=1).to_broadcast(A3)

        def over_t(ap):
            return ap.rearrange("p (a e) -> p a e", a=1).to_broadcast(A3)

        @block.gpsimd
        def _(pool):
            pool.memset(ones[:, :], 1.0).then_inc(const, 1)
            pool.wait_ge(const, 1)
            pool.affine_select(out=before[:, :], in_=ones[:, :], compare_op=ALU.is_gt, fill=0.0,
                               base=0, pattern=[[1, P]], channel_multiplier=-1).then_inc(const, 1)
            pool.wait_ge(const, 2)
            pool.iota(order[:, :], [[-1, NE]], base=NE, channel_multiplier=0,
                      allow_small_or_imprecise_dtypes=True).then_inc(const, 1)
            pool.wait_ge(const, 3)
            pool.iota(tile_no[:, :], [[1, NTM]], base=0, channel_multiplier=0,
                      allow_small_or_imprecise_dtypes=True).then_inc(const, 1)
            pool.wait_ge(slots_done, 1)
            for t in range(NT):
                for c in range(TOP):
                    pool.indirect_dma_start(out=xs, out_offset=bass.IndirectOffsetOnAxis(ap=POS[:, c, t:t + 1], axis=0),
                                            in_=XF[:, t, :], in_offset=None).then_inc(scattered, 16)
            pool.wait_ge(scattered, 16 * TOP * NT)

        @block.scalar
        def _(act):
            act.wait_ge(max_off, 1)
            act.activation(ex[:, :, :], ex[:, :, :], ACT.Exp).then_inc(exp_done, 1)

        @block.tensor
        def _(pe):
            pe.wait_ge(const, 2)
            pe.wait_ge(chosen_done, 1)
            flat = both[:, :, :].rearrange("p t e -> p (t e)")
            pe.matmul(ps[:, 0, :, :].rearrange("p t e -> p (t e)"), before[:, :], flat, start=True, stop=True)
            pe.matmul(ps[:, 1, :, :].rearrange("p t e -> p (t e)"), ones[:, :], flat, start=True, stop=True).then_inc(counted, 1)

        @block.vector
        def _(dve):
            n = [0]

            def link(ins):
                n[0] += 1
                ins.then_inc(step_done, 1)
                dve.wait_ge(step_done, n[0])

            dve.wait_ge(const, 4)
            link(dve.tensor_reduce(top[:, :], LG[:, :, :], axis=AX.X, op=ALU.max))
            dve.tensor_tensor(ex[:, :, :], LG[:, :, :], over_e(top[:, :]), ALU.subtract).then_inc(max_off, 1)
            dve.wait_ge(exp_done, 1)
            link(dve.tensor_reduce(total[:, :], ex[:, :, :], axis=AX.X, op=ALU.add))
            link(dve.reciprocal(total[:, :], total[:, :]))
            link(dve.tensor_tensor(probs[:, :, :], ex[:, :, :], over_e(total[:, :]), ALU.mult))
            for c in range(TOP):
                link(dve.tensor_reduce(best[:, c, :], probs[:, :, :], axis=AX.X, op=ALU.max))
                link(dve.tensor_tensor(value[:, :, :], probs[:, :, :], over_e(best[:, c, :]), ALU.is_equal))
                link(dve.tensor_tensor(value[:, :, :], value[:, :, :], over_t(order[:, :]), ALU.mult))
                link(dve.tensor_reduce(pick[:, :], value[:, :, :], axis=AX.X, op=ALU.max))
                link(dve.tensor_tensor(chosen[:, c, :, :], value[:, :, :], over_e(pick[:, :]), ALU.is_equal))
                if c == 0:
                    link(dve.scalar_tensor_tensor(probs[:, :, :], chosen[:, 0, :, :], -2.0, probs[:, :, :], ALU.mult, ALU.add))
            dve.tensor_tensor(both[:, :, :], chosen[:, 0, :, :], chosen[:, 1, :, :], ALU.add).then_inc(chosen_done, 1)
            link(dve.tensor_tensor(den[:, :], best[:, 0, :], best[:, 1, :], ALU.add))
            link(dve.tensor_scalar(den[:, :], den[:, :], TOPK_EPS, None, ALU.add))
            link(dve.reciprocal(den[:, :], den[:, :]))
            for c in range(TOP):
                link(dve.tensor_tensor(W12[:, c, :], best[:, c, :], den[:, :], ALU.mult))
            dve.wait_ge(counted, 1)
            link(dve.tensor_copy(sums[:, 0, :, :], ps[:, 1, :, :]))
            a, shift = 0, 1
            while shift < NT:
                link(dve.tensor_copy(sums[:, 1 - a, 0:shift, :], sums[:, a, 0:shift, :]))
                link(dve.tensor_tensor(sums[:, 1 - a, shift:NT, :], sums[:, a, shift:NT, :], sums[:, a, 0:NT - shift, :], ALU.add))
                a, shift = 1 - a, 2 * shift
            link(dve.tensor_scalar(counts[:, :], sums[:, a, NT - 1, :], float(P - 1), None, ALU.add))
            link(dve.tensor_copy(counts_i[:, :], counts[:, :]))
            link(dve.tensor_scalar(counts_i[:, :], counts_i[:, :], P.bit_length() - 1, None, ALU.logical_shift_right))
            link(dve.tensor_copy(tiles[:, :], counts_i[:, :]))
            link(dve.tensor_copy(ends[:, 0, :], tiles[:, :]))
            c, shift = 0, 1
            while shift < NE:
                link(dve.tensor_copy(ends[:, 1 - c, 0:shift], ends[:, c, 0:shift]))
                link(dve.tensor_tensor(ends[:, 1 - c, shift:NE], ends[:, c, shift:NE], ends[:, c, 0:NE - shift], ALU.add))
                c, shift = 1 - c, 2 * shift
            link(dve.tensor_tensor(tiles[:, :], ends[:, c, :], tiles[:, :], ALU.subtract))
            link(dve.tensor_scalar(tiles[:, :], tiles[:, :], float(P), None, ALU.mult))
            link(dve.tensor_tensor(slot[:, :, :], ps[:, 0, :, :], sums[:, a, :, :], ALU.add))
            link(dve.tensor_tensor(slot[:, :, :], slot[:, :, :], over_t(tiles[:, :]), ALU.add))
            link(dve.tensor_tensor(slot[:, :, :], ps[:, 1, :, :], slot[:, :, :], ALU.subtract))
            for k in range(TOP):
                link(dve.tensor_tensor(value[:, :, :], chosen[:, k, :, :], slot[:, :, :], ALU.mult))
                link(dve.tensor_reduce(slot_of[:, k, :], value[:, :, :], axis=AX.X, op=ALU.add, negate=True))
            link(dve.tensor_copy(POS[:, :, :], slot_of[:, :, :]))
            link(dve.tensor_scalar(expert[:, :], tile_no[:, :], ends[:, c, 0:1], None, ALU.is_ge))
            for x in range(1, NE - 1):
                link(dve.scalar_tensor_tensor(expert[:, :], tile_no[:, :], ends[:, c, x:x + 1], expert[:, :], ALU.is_ge, ALU.add))
            dve.tensor_copy(tile_expert[:, :], expert[:, :]).then_inc(slots_done, 1)


def phase_experts(nc, T):
    ident, WG, WU, WD, tile_expert, xs, ys = (T[k] for k in ("ident", "WG", "WU", "WD", "tile_expert", "xs", "ys"))
    with ExitStack() as ctx:
        def sb(name, shape, dt=F32):
            return ctx.enter_context(nc.sbuf_tensor(name, shape, dt))

        def sem(name):
            return ctx.enter_context(nc.semaphore(name))

        xt = sb("m_x", [P, 2, D])
        xT = sb("m_xT", [P, 2, KD, P])
        SG = sb("m_silu", [P, 2, FI])
        H = sb("m_h", [P, 2, FI])
        HT = sb("m_hT", [P, 2, KF, P])
        yt = sb("m_y", [P, 2, D])
        psG = ctx.enter_context(nc.psum_tensor("m_psG", [P, 2, HALF], F32))
        psU = ctx.enter_context(nc.psum_tensor("m_psU", [P, 2, HALF], F32))
        psT = ctx.enter_context(nc.psum_tensor("m_psT", [P, 1, HALF], F32))
        psH = ctx.enter_context(nc.psum_tensor("m_psH", [P, 1, HALF], F32))
        psY = ctx.enter_context(nc.psum_tensor("m_psY", [P, 2, HALF], F32))
        x_in = [sem("m_x_in_even"), sem("m_x_in_odd")]
        t_done, t_in = sem("m_t_done"), sem("m_t_in")
        g_done, u_done = sem("m_g_done"), sem("m_u_done")
        silu_done, h_done = sem("m_silu_done"), sem("m_h_done")
        ht_done, ht_in = sem("m_ht_done"), sem("m_ht_in")
        y_done, y_in = sem("m_y_done"), sem("m_y_in")
        y_out = [sem("m_y_out_even"), sem("m_y_out_odd")]
        block = ctx.enter_context(nc.Block())
        xs_t = xs.rearrange("(t p) d -> t p d", p=P)
        ys_t = ys.rearrange("(t p) d -> t p d", p=P)

        @block.sync
        def _(sp):
            def load(i, e):
                if not peeled(i, 2):
                    sp.wait_ge(t_done, at(i, 1, -1))
                sp.dma_start(xt[:, e, :], xs_t[i, :, :]).then_inc(x_in[e], 16)

            load(0, 0)
            load(1, 1)
            with sp.Fori(1, NTM // 2) as j:
                load(j * 2, 0)
                load(j * 2 + 1, 1)
            for e in range(2):
                sp.wait_ge(x_in[e], 16 * (NTM // 2))

        @block.gpsimd
        def _(pool):
            def store(i, e):
                pool.wait_ge(y_in, at(i, 1, 1))
                pool.dma_start(ys_t[i, :, :], yt[:, e, :]).then_inc(y_out[e], 16)

            with pool.Fori(0, NTM // 2) as j:
                store(j * 2, 0)
                store(j * 2 + 1, 1)
            for e in range(2):
                pool.wait_ge(y_out[e], 16 * (NTM // 2))

        @block.tensor
        def _(pe):
            def expert_of(i):
                return pe.value_load(tile_expert[0:1, bass.ds(i, 1)], min_val=0, max_val=NE - 1)

            def step(tile):
                if t := tile(1):
                    i, e = t
                    x = expert_of(i)
                    pe.wait_ge(t_in, at(i, 1, 1))
                    for w, psum, done, read in ((WG, psG, g_done, silu_done), (WU, psU, u_done, h_done)):
                        if not peeled(i, 2):
                            pe.wait_ge(read, at(i, 1, -1))
                        for k in range(KD):
                            mm = pe.matmul(psum[:, e, :], xT[:, e, k, :], w[:, x, k, :], start=(k == 0), stop=(k == KD - 1))
                        mm.then_inc(done, 1)
                if t := tile(2):
                    i, e = t
                    pe.wait_ge(h_done, at(i, 1, 1))
                    if not peeled(i, 1):
                        pe.wait_ge(ht_in, at(i, 1, 0))
                    for k in range(KF):
                        mm = pe.transpose(psH[:, 0, k * P:(k + 1) * P], H[:, e, k * P:(k + 1) * P], ident[:, :])
                    mm.then_inc(ht_done, 1)
                if t := tile(0):
                    i, e = t
                    pe.wait_ge(x_in[e], at(i - e, 8, 16))
                    if not peeled(i, 1):
                        pe.wait_ge(t_in, at(i, 1, 0))
                    for k in range(KD):
                        mm = pe.transpose(psT[:, 0, k * P:(k + 1) * P], xt[:, e, k * P:(k + 1) * P], ident[:, :])
                    mm.then_inc(t_done, 1)
                if t := tile(2):
                    i, e = t
                    x = expert_of(i)
                    pe.wait_ge(ht_in, at(i, 1, 1))
                    if not peeled(i, 2):
                        pe.wait_ge(y_in, at(i, 1, -1))
                    for k in range(KF):
                        mm = pe.matmul(psY[:, e, 0:D], HT[:, e, k, :], WD[:, x, k, :], start=(k == 0), stop=(k == KF - 1))
                    mm.then_inc(y_done, 1)

            staggered(pe, NTM, range(3), step)

        @block.vector
        def _(dve):
            def step(tile):
                if t := tile(1):
                    i, e = t
                    dve.wait_ge(silu_done, at(i, 1, 1))
                    dve.wait_ge(u_done, at(i, 1, 1))
                    if not peeled(i, 2):
                        dve.wait_ge(ht_done, at(i, 1, -1))
                    dve.tensor_tensor(H[:, e, :], psU[:, e, :], SG[:, e, :], ALU.mult).then_inc(h_done, 1)
                if t := tile(2):
                    i, e = t
                    dve.wait_ge(y_done, at(i, 1, 1))
                    if not peeled(i, 2):
                        dve.wait_ge(y_out[e], at(i - e, 8, 0))
                    dve.tensor_copy(yt[:, e, :], psY[:, e, 0:D]).then_inc(y_in, 1)

            staggered(dve, NTM, range(3), step)

        @block.scalar
        def _(act):
            def step(tile):
                if t := tile(1):
                    i, e = t
                    act.wait_ge(g_done, at(i, 1, 1))
                    if not peeled(i, 2):
                        act.wait_ge(h_done, at(i, 1, -1))
                    act.activation(SG[:, e, :], psG[:, e, :], ACT.Silu).then_inc(silu_done, 1)
                if t := tile(2):
                    i, e = t
                    act.wait_ge(ht_done, at(i, 1, 1))
                    if not peeled(i, 2):
                        act.wait_ge(y_done, at(i, 1, -1))
                    act.activation(HT[:, e, :, :], psH[:, 0, :].rearrange("p (k n) -> p k n", n=P), ACT.Copy).then_inc(ht_in, 1)
                if t := tile(0):
                    i, e = t
                    act.wait_ge(t_done, at(i, 1, 1))
                    if not peeled(i, 2):
                        act.wait_ge(u_done, at(i, 1, -1))
                    act.activation(xT[:, e, :, :], psT[:, 0, 0:D].rearrange("p (k n) -> p k n", n=P), ACT.Copy).then_inc(t_in, 1)

            staggered(act, NTM, range(3), step)


def phase_combine(nc, T):
    X, W12, POS, ys, out = T["X"], T["W12"], T["POS"], T["ys"], T["out"]
    with ExitStack() as ctx:
        def sem(name):
            return ctx.enter_context(nc.semaphore(name))

        NB = 4
        rows = ctx.enter_context(nc.sbuf_tensor("c_rows", [P, TOP, NB, D], F32))
        gathered = [sem(f"c_gathered{n}") for n in range(NB)]
        added = sem("c_added")
        first = sem("c_first")
        stored = sem("c_stored")
        block = ctx.enter_context(nc.Block())
        out_t = out.rearrange("b (t p) d -> p (b t) d", p=P)

        @block.gpsimd
        def _(pool):
            for t in range(NT):
                if t >= NB:
                    pool.wait_ge(added, t - NB + 1)
                for c in range(TOP):
                    pool.indirect_dma_start(out=rows[:, c, t % NB, :], out_offset=None, in_=ys,
                                            in_offset=bass.IndirectOffsetOnAxis(ap=POS[:, c, t:t + 1], axis=0),
                                            ).then_inc(gathered[t % NB], 16)

        @block.vector
        def _(dve):
            for t in range(NT):
                dve.wait_ge(gathered[t % NB], 32 * (t // NB + 1))
                dve.scalar_tensor_tensor(X[:, t, :], rows[:, 0, t % NB, :], W12[:, 0, t:t + 1], X[:, t, :],
                                         ALU.mult, ALU.add).then_inc(first, 1)
                dve.wait_ge(first, t + 1)
                dve.scalar_tensor_tensor(X[:, t, :], rows[:, 1, t % NB, :], W12[:, 1, t:t + 1], X[:, t, :],
                                         ALU.mult, ALU.add).then_inc(added, 1)

        @block.sync
        def _(sp):
            with sp.Fori(0, NT // 4) as j:
                sp.wait_ge(added, at(j, 4, 4))
                sp.dma_start(out_t[:, bass.ds(j * 4, 4), :], X[:, bass.ds(j * 4, 4), :]).then_inc(stored, 16)
            sp.wait_ge(stored, 16 * (NT // 4))


def phase_scratch(nc, T):
    with ExitStack() as ctx:
        zero = ctx.enter_context(nc.sbuf_tensor("zero_row", [P, 1, D], F32))
        zeroed = ctx.enter_context(nc.semaphore("zeroed"))
        xs_cleared = ctx.enter_context(nc.semaphore("xs_cleared"))
        block = ctx.enter_context(nc.Block())

        @block.vector
        def _(dve):
            dve.memset(zero[:, :, :], 0.0).then_inc(zeroed, 1)

        @block.sync
        def _(sp):
            sp.wait_ge(zeroed, 1)
            sp.dma_start(T["xs"].rearrange("(t p) d -> p t d", p=P),
                         zero[:, :, :].to_broadcast([P, NTM, D])).then_inc(xs_cleared, 16)
            sp.wait_ge(xs_cleared, 16)


def decoder_layer(nc, T):
    with ExitStack() as ctx:
        def dram(name, shape, dt):
            return nc.dram_tensor(name, shape, dt, kind="Internal").ap()

        def sb(stack, name, shape, dt=F32):
            T[name] = stack.enter_context(nc.sbuf_tensor(name, shape, dt))

        T["q_parts"] = dram("q_parts", [NG, 3, HD, GH, S], BF16)
        T["k_parts"] = dram("k_parts", [NG, 3, HD, S], BF16)
        T["m_parts"] = dram("m_parts", [NG, 3, GH * S], BF16)
        T["xs"] = dram("xs", [NSLOT, D], F32)
        T["ys"] = dram("ys", [NSLOT, D], F32)
        sb(ctx, "X", [P, NT, D])
        sb(ctx, "ident", [P, P])
        phase_scratch(nc, T)
        with ExitStack() as attention:
            sb(attention, "VA", [P, NG, TB, VW])
            sb(attention, "OU", [P, NKV, B * S])
            phase_qkv(nc, T)
            phase_attention(nc, T)
            phase_self_out(nc, T)
        with ExitStack() as cross:
            sb(cross, "KX", [P, B, NPR, 2 * SC])
            sb(cross, "VX", [SCP, B, XW])
            phase_context(nc, T)
            phase_cross(nc, T)
        sb(ctx, "XF", [P, NT, D])
        sb(ctx, "LG", [P, NT, NE])
        sb(ctx, "W12", [P, TOP, NT])
        sb(ctx, "POS", [P, TOP, NT], U32)
        sb(ctx, "tile_expert", [P, NTM], I32)
        sb(ctx, "WG", [P, NE, KD, FI])
        sb(ctx, "WU", [P, NE, KD, FI])
        sb(ctx, "WD", [P, NE, KF, D])
        phase_shared(nc, T)
        phase_route(nc, T)
        phase_experts(nc, T)
        phase_combine(nc, T)


def kernel(**inputs):
    import numpy as np
    import concourse.bacc as bacc
    from concourse.bass_utils import run_bass_kernel_spmd

    def rows(name):
        return np.ascontiguousarray(inputs[name])

    def per_head(name):
        w = np.asarray(inputs[name])
        return np.ascontiguousarray(w.transpose(1, 0, 2).reshape(w.shape[1], -1))

    def columns(*vectors):
        v = np.concatenate([np.asarray(x) for x in vectors])
        v = np.concatenate([v, np.zeros(-len(v) % P, v.dtype)])
        return np.ascontiguousarray(v.reshape(-1, P).T)

    wo = np.asarray(inputs["L0_attn_Wo"]).reshape(GH, NKV, HD, D).transpose(1, 0, 2, 3)
    arrays = {
        "x": rows("x"), "ctx": rows("ctx_1024"), "mask": rows("mask_BxSxS2_ik1"),
        "Wq": rows("L0_attn_Wq"), "Wk": rows("L0_attn_Wk"), "Wv": rows("L0_attn_Wv"),
        "bqk": columns(inputs["L0_attn_bq"], inputs["L0_attn_bk"]), "bv": rows("L0_attn_bv"),
        "Wo": np.ascontiguousarray(wo.reshape(D, D)), "bo": rows("L0_attn_bo"),
        "Wqx": per_head("L0_xattn_Wq"), "Wkx": per_head("L0_xattn_Wk"), "Wvx": per_head("L0_xattn_Wv"),
        "Wox": rows("L0_xattn_Wo"),
        "sWg": rows("L0_ffn_sWg"), "sWu": rows("L0_ffn_sWu"), "sWd": rows("L0_ffn_sWd"),
        "gateT": np.ascontiguousarray(np.asarray(inputs["L0_ffn_gate_w"]).T),
        "affine": np.ascontiguousarray(np.stack([columns(inputs["L0_ffn_ln_scale"]), columns(inputs["L0_ffn_ln_bias"])], 1)),
        "Wg": rows("L0_ffn_Wg"), "Wu": rows("L0_ffn_Wu"), "Wd": rows("L0_ffn_Wd"),
    }
    nc = bacc.Bacc("TRN2", target_bir_lowering=False, num_devices=1)
    T = {name: nc.dram_tensor(f"in_{name}", a.shape, mybir.dt.from_np(a.dtype), kind="ExternalInput").ap()
         for name, a in arrays.items()}
    T["out"] = nc.dram_tensor("out", (B, S, D), F32, kind="ExternalOutput").ap()
    decoder_layer(nc, T)
    r = run_bass_kernel_spmd(nc, [{f"in_{name}": a for name, a in arrays.items()}], core_ids=[0])
    return r.results[0]["out"]
```

```python
import concourse.bass as bass
from concourse import mybir
from contextlib import ExitStack

F32 = mybir.dt.float32
BF16 = mybir.dt.bfloat16
I32 = mybir.dt.int32
U32 = mybir.dt.uint32
ALU = mybir.AluOpType
ACT = mybir.ActivationFunctionType
AX = mybir.AxisListType

P = 128
D = 256
KD = D // P
B = 4
S = 1024
TB = S // P
NT = B * TB
LN_EPS = 1e-5
NH = 16
NKV = 4
GH = NH // NKV
HD = D // NH
NG = B * NKV
SCALE = HD ** -0.5
VW = 32
Q_PARTS = (3, 2, 1)
KQ = sum(Q_PARTS) * HD
KM = KQ + 3
HALF = 512
SLOTS = 4
TURN_AT = 4
NU = GH * TB


def phase_qkv(nc, T):
    X, ident, VA, q_parts, k_parts = T["X"], T["ident"], T["VA"], T["q_parts"], T["k_parts"]
    with ExitStack() as ctx:
        def sb(name, shape, dt=F32):
            return ctx.enter_context(nc.sbuf_tensor(name, shape, dt))

        def sem(name):
            return ctx.enter_context(nc.semaphore(name))

        wq = sb("wq_sb", [P, KD, D])
        wk = sb("wk_sb", [P, KD, NKV * HD])
        wv = sb("wv_sb", [P, KD, NKV * HD])
        bqk = sb("bqk_sb", [P, 3])
        bv = sb("bv_sb", [P, NKV * HD])
        stats = sb("stats", [P, TB, 6])
        mean_var = sb("mean_var", [P, TB, 2])
        var_eps = sb("var_eps", [P, TB])
        neg_half = sb("neg_half", [P, TB])
        rstd = sb("rstd", [P, TB])
        xn = sb("xn", [P, TB, D])
        xnT = sb("xnT", [P, KD, S])
        part = sb("part", [P, 3, 3, S], BF16)
        rest = sb("rest", [P, 3, S])
        psT = ctx.enter_context(nc.psum_tensor("psT", [P, 2, HALF], F32))
        psQ = ctx.enter_context(nc.psum_tensor("psQ", [P, 4, HALF], F32))
        psV = ctx.enter_context(nc.psum_tensor("psV", [P, 1, HALF], F32))

        x_loaded = sem("x_loaded")
        w_loaded = sem("w_loaded")
        consts = sem("consts")
        waited_pool = sem("qkv_waited_pool")
        waited_dve = sem("qkv_waited_dve")
        stats_done = sem("stats_done")
        mv_done = sem("mv_done")
        veps_done = sem("veps_done")
        rstd_done = sem("rstd_done")
        xn_done = sem("xn_done")
        tr_done = sem("tr_done")
        xnT_done = sem("xnT_done")
        proj_done = sem("proj_done")
        p1_done = sem("p1_done")
        rest_done = sem("rest_done")
        p2_done = sem("p2_done")
        p3_done = sem("p3_done")
        v_done = sem("v_done")
        va_done = sem("va_done")
        stored = sem("stored")
        MS = [(0, P), (1, P), (2, NKV * HD)]
        UNITS = [(m, rows, n) for m, rows in MS for n in range(2)]
        NUN = len(UNITS)
        NSTORE = 16 * 3 * (NKV + 1)
        block = ctx.enter_context(nc.Block())

        @block.sync
        def _(sp):
            sp.dma_start(X[:, :, :], T["x"].rearrange("b (t p) d -> p (b t) d", p=P)).then_inc(x_loaded, 16)
            sp.dma_start(wq[:, :, :], T["Wq"].rearrange("(k p) n -> p k n", p=P)).then_inc(w_loaded, 16)
            sp.dma_start(wk[:, :, :], T["Wk"].rearrange("(k p) n -> p k n", p=P)).then_inc(w_loaded, 16)
            sp.dma_start(wv[:, :, :], T["Wv"].rearrange("(k p) n -> p k n", p=P)).then_inc(w_loaded, 16)
            sp.dma_start(bqk[:, :], T["bqk"]).then_inc(w_loaded, 16)
            sp.dma_start(bv[:, :], T["bv"].rearrange("(a n) -> a n", a=1).to_broadcast([P, NKV * HD])).then_inc(w_loaded, 16)
            with sp.Fori(0, B) as b:
                sp.wait_ge(p3_done, NUN * b + NUN)
                for m in range(2):
                    for j in range(3):
                        for gg in range(2):
                            rows = slice(gg * GH * HD, (gg + 1) * GH * HD)
                            sp.dma_start(q_parts[b + (2 * m + gg) * B, j, :, :, :].rearrange("d h n -> h d n"),
                                         part[rows, j, m, :]).then_inc(stored, 16)
                for j in range(3):
                    sp.dma_start(k_parts.rearrange("(g b) j d n -> b j g d n", b=B)[b, j, :, :, :],
                                 part[0:NKV * HD, j, 2, :]).then_inc(stored, 16)
            sp.wait_ge(stored, NSTORE * B)

        @block.gpsimd
        def _(pool):
            pool.memset(ident[:, :], 0.0).then_inc(consts, 1)
            pool.wait_ge(consts, 1)
            pool.affine_select(out=ident[:, :], in_=ident[:, :], compare_op=ALU.not_equal, fill=1.0,
                               base=0, pattern=[[-1, P]], channel_multiplier=1).then_inc(consts, 1)
            pool.memset(neg_half[:, :], -0.5).then_inc(consts, 1)
            pool.memset(VA[:, :, :, :], 0.0).then_inc(consts, 1)
            pool.wait_ge(consts, 4)
            pool.memset(VA[:, :, :, HD:HD + 1], 1.0).then_inc(consts, 1)
            with pool.Fori(0, B) as b:
                pool.wait_ge(veps_done, b + 1)
                pool.tensor_tensor(rstd[:, :], var_eps[:, :], neg_half[:, :], ALU.pow).then_inc(rstd_done, 1)
                for u, (m, rows, n) in enumerate(UNITS):
                    cols = slice(n * HALF, (n + 1) * HALF)
                    pool.wait_ge(rest_done, NUN * b + u + 1)
                    pool.sem_inc(waited_pool, 1)
                    pool.tensor_copy(part[0:rows, 1, m, cols], rest[0:rows, m, cols]).then_inc(p2_done, 1)
                    pool.wait_ge(p2_done, NUN * b + u + 1)
                    pool.tensor_tensor(part[0:rows, 2, m, cols], rest[0:rows, m, cols],
                                       part[0:rows, 1, m, cols], ALU.subtract).then_inc(p3_done, 1)

        @block.vector
        def _(dve):
            dve.wait_ge(x_loaded, 16)
            dve.wait_ge(w_loaded, 16 * 5)
            dve.wait_ge(consts, 5)
            with dve.Fori(0, B) as b:
                for t in range(TB):
                    dve.bn_stats(stats[:, t, :], X[:, b * TB + t, :]).then_inc(stats_done, 1)
                dve.wait_ge(stats_done, TB * b + TB)
                dve.sem_inc(waited_dve, 1)
                for t in range(TB):
                    dve.bn_aggr(mean_var[:, t, :], stats[:, t, :]).then_inc(mv_done, 1)
                dve.wait_ge(mv_done, TB * b + TB)
                dve.tensor_scalar(var_eps[:, :], mean_var[:, :, 1], LN_EPS, None, ALU.add).then_inc(veps_done, 1)
                dve.wait_ge(rstd_done, b + 1)
                for t in range(TB):
                    dve.tensor_scalar(xn[:, t, :], X[:, b * TB + t, :], mean_var[:, t, 0:1], rstd[:, t:t + 1],
                                      ALU.subtract, ALU.mult).then_inc(xn_done, 1)
                for u, (m, rows, n) in enumerate(UNITS):
                    cols = slice(n * HALF, (n + 1) * HALF)
                    dve.wait_ge(p1_done, NUN * b + u + 1)
                    dve.scalar_tensor_tensor(rest[0:rows, m, cols], psQ[0:rows, u % 4, :], bqk[0:rows, m:m + 1],
                                             part[0:rows, 0, m, cols], ALU.add, ALU.subtract).then_inc(rest_done, 1)
                dve.wait_ge(v_done, b + 1)
                for g in range(NKV):
                    dve.tensor_tensor(VA[:, b + g * B, :, 0:HD],
                                      psV[:, 0, :].rearrange("p (t g d) -> p g t d", t=TB, g=NKV)[:, g, :, :],
                                      bv[:, g * HD:(g + 1) * HD].rearrange("p (a d) -> p a d", a=1).to_broadcast([P, TB, HD]),
                                      ALU.add).then_inc(va_done, 1)

        @block.scalar
        def _(act):
            act.wait_ge(w_loaded, 16 * 5)
            with act.Fori(0, B) as b:
                for t in range(TB):
                    act.wait_ge(tr_done, TB * b + t + 1)
                    act.activation(xnT[:, :, t * P:(t + 1) * P],
                                   psT[:, t % 2, 0:KD * P].rearrange("p (k n) -> p k n", k=KD), ACT.Copy).then_inc(xnT_done, 1)
                for u, (m, rows, n) in enumerate(UNITS):
                    act.wait_ge(proj_done, NUN * b + u + 1)
                    act.activation(part[0:rows, 0, m, n * HALF:(n + 1) * HALF], psQ[0:rows, u % 4, :], ACT.Identity,
                                   bias=bqk[0:rows, m:m + 1]).then_inc(p1_done, 1)
                act.wait_ge(stored, NSTORE * b + NSTORE)

        @block.tensor
        def _(pe):
            pe.wait_ge(w_loaded, 16 * 5)
            pe.wait_ge(consts, 5)
            with pe.Fori(0, B) as b:
                for t in range(TB):
                    pe.wait_ge(xn_done, TB * b + t + 1)
                    if t >= 2:
                        pe.wait_ge(xnT_done, TB * b + t - 1)
                    for k in range(KD):
                        tr = pe.transpose(psT[:, t % 2, k * P:(k + 1) * P], xn[:, t, k * P:(k + 1) * P], ident[:, :])
                    tr.then_inc(tr_done, 1)
                pe.wait_ge(xnT_done, TB * b + TB)
                for u, (m, rows, n) in enumerate(UNITS):
                    if u >= 4:
                        pe.wait_ge(rest_done, NUN * b + u - 3)
                    for k in range(KD):
                        w = wk[:, k, :] if m == 2 else wq[:, k, m * P:(m + 1) * P]
                        mm = pe.matmul(psQ[0:rows, u % 4, :], w, xnT[:, k, n * HALF:(n + 1) * HALF],
                                       start=(k == 0), stop=(k == KD - 1))
                    mm.then_inc(proj_done, 1)
                for t in range(TB):
                    for k in range(KD):
                        mm = pe.matmul(psV[:, 0, t * NKV * HD:(t + 1) * NKV * HD], xnT[:, k, t * P:(t + 1) * P], wv[:, k, :],
                                       start=(k == 0), stop=(k == KD - 1))
                mm.then_inc(v_done, 1)
                pe.wait_ge(va_done, NKV * b + NKV)
                pe.wait_ge(rest_done, NUN * b + NUN)


def phase_attention(nc, T):
    VA, OU, q_parts, k_parts, m_parts = T["VA"], T["OU"], T["q_parts"], T["k_parts"], T["m_parts"]
    with ExitStack() as ctx:
        def sb(name, shape, dt=F32):
            return ctx.enter_context(nc.sbuf_tensor(name, shape, dt))

        def sem(name):
            return ctx.enter_context(nc.semaphore(name))

        QS = sb("QS", [P, SLOTS, GH, S], BF16)
        KS = sb("KS", [P, SLOTS, S], BF16)
        VG = sb("VG", [P, 2, TB, VW])
        PT = sb("PT", [P, 2, GH, S])
        half_max = sb("half_max", [P, NU, 2])
        neg_max = sb("neg_max", [P, NU])
        max_rest = sb("max_rest", [P, NU])
        max_parts = sb("max_parts", [P, 3, NU], BF16)
        max_parts_t = sb("max_parts_t", [P, 3, NU], BF16)
        psA = ctx.enter_context(nc.psum_tensor("psA", [P, 2, HALF], F32))
        psB = ctx.enter_context(nc.psum_tensor("psB", [P, 2, 2, HALF], F32))
        psO = ctx.enter_context(nc.psum_tensor("psO", [P, 2, HALF], F32))

        ones_set = sem("ones_set")
        waited_pool = sem("att_waited_pool")
        loaded = [sem("loaded_even"), sem("loaded_odd")]
        v_copied = sem("v_copied")
        a_done = sem("a_done")
        max_taken = sem("max_taken")
        neg_done = sem("neg_done")
        m1_done = sem("m1_done")
        mr_done = sem("mr_done")
        m2_done = sem("m2_done")
        m3_done = sem("m3_done")
        mt_done = sem("mt_done")
        m_stored = sem("m_stored")
        rows_set = [sem("rows_set_even"), sem("rows_set_odd")]
        b_done = sem("b_done")
        exp_done = sem("exp_done")
        pv_done = sem("pv_done")
        out_copied = sem("out_copied")
        NROWS = 16
        NLOAD = 16 * 6
        block = ctx.enter_context(nc.Block())

        def count(i, per, plus):
            return i * per + plus

        @block.sync
        def _(sp):
            def load(i, e):
                if not (isinstance(i, int) and i < SLOTS):
                    sp.wait_ge(pv_done, count(i, TB, -TB * (SLOTS - 1)))
                row = 0
                for kp, nq in enumerate(Q_PARTS):
                    sp.dma_start(QS[row:row + nq * HD, i % SLOTS, :, :],
                                 q_parts[i, 0:nq, :, :, :].rearrange("a d h n -> (a d) h n")).then_inc(loaded[e], 16)
                    sp.dma_start(KS[row:row + nq * HD, i % SLOTS, :],
                                 k_parts[i, kp:kp + 1, :, :].to_broadcast([nq, HD, S])).then_inc(loaded[e], 16)
                    row += nq * HD

            def rows(i, e):
                sp.wait_ge(mt_done, count(i, 1, 1))
                for part in range(3):
                    sp.dma_start(m_parts[i, part, :].rearrange("(u k n) -> k u n", k=4, n=32),
                                 max_parts_t[:, part, :]).then_inc(m_stored, 16)
                sp.wait_ge(m_stored, count(i, 48, 48))
                sp.dma_start(QS[KQ:KM, i % SLOTS, :, :].rearrange("a h n -> a (h n)"), m_parts[i, :, :]).then_inc(rows_set[e], 16)

            load(0, 0)
            load(1, 1)
            for i in range(2):
                rows(i, i)
                load(i + 2, i)
            with sp.Fori(1, NG // 2 - 1) as j:
                for e in range(2):
                    rows(j * 2 + e, e)
                    load(j * 2 + (e + 2), e)
            for i in range(NG - 2, NG):
                rows(i, i % 2)
            for e in range(2):
                sp.wait_ge(rows_set[e], NROWS * (NG // 2))

        @block.gpsimd
        def _(pool):
            pool.memset(KS[96:P, :, :], 1.0).then_inc(ones_set, 1)
            pool.wait_ge(ones_set, 1)

            def values(i, e):
                if not (isinstance(i, int) and i < 2):
                    pool.wait_ge(pv_done, count(i, TB, -TB))
                    pool.sem_inc(waited_pool, 1)
                pool.tensor_copy(VG[:, e, :, :], VA[:, i, :, :]).then_inc(v_copied, 1)

            def maxima(i):
                pool.wait_ge(v_copied, count(i, 1, 1))
                pool.wait_ge(neg_done, count(i, 1, 1))
                if not (isinstance(i, int) and i < 1):
                    pool.wait_ge(mt_done, count(i, 1, 0))
                    pool.sem_inc(waited_pool, 1)
                pool.tensor_copy(max_parts[:, 0, :], neg_max[:, :]).then_inc(m1_done, 1)
                pool.wait_ge(m1_done, count(i, 1, 1))
                pool.tensor_tensor(max_rest[:, :], neg_max[:, :], max_parts[:, 0, :], ALU.subtract).then_inc(mr_done, 1)
                pool.wait_ge(mr_done, count(i, 1, 1))
                pool.sem_inc(waited_pool, 1)
                pool.tensor_copy(max_parts[:, 1, :], max_rest[:, :]).then_inc(m2_done, 1)
                pool.wait_ge(m2_done, count(i, 1, 1))
                pool.tensor_tensor(max_parts[:, 2, :], max_rest[:, :], max_parts[:, 1, :], ALU.subtract).then_inc(m3_done, 1)
                pool.wait_ge(m3_done, count(i, 1, 1))

            for i in range(2):
                values(i, i)
                maxima(i)
            with pool.Fori(1, NG // 2) as j:
                for e in range(2):
                    values(j * 2 + e, e)
                    maxima(j * 2 + e)

        @block.vector
        def _(dve):
            def turn_parts(i):
                dve.wait_ge(m3_done, count(i, 1, 1))
                if not (isinstance(i, int) and i < 1):
                    dve.wait_ge(m_stored, count(i, 48, 0))
                dve.transpose(max_parts_t[:, :, :], max_parts[:, :, :]).then_inc(mt_done, 1)

            def maxima(i):
                if not (isinstance(i, int) and i < 1):
                    dve.wait_ge(neg_done, count(i, 1, 0))
                for u in range(NU):
                    for n in range(2):
                        dve.wait_ge(a_done, count(i, 2 * NU, 2 * u + n + 1))
                        dve.tensor_reduce(half_max[:, u, n:n + 1], psA[:, n, :], axis=AX.X, op=ALU.max).then_inc(max_taken, 1)
                    if u == TURN_AT and not (isinstance(i, int) and i < 1):
                        turn_parts(count(i, 1, -1))
                dve.wait_ge(max_taken, count(i, 2 * NU, 2 * NU))
                if not (isinstance(i, int) and i < 1):
                    dve.wait_ge(m3_done, count(i, 1, 0))
                dve.tensor_reduce(neg_max[:, :], half_max[:, :, :], axis=AX.X, op=ALU.max, negate=True).then_inc(neg_done, 1)

            maxima(0)
            maxima(1)
            with dve.Fori(1, NG // 2) as j:
                for e in range(2):
                    maxima(j * 2 + e)
            turn_parts(NG - 1)

        @block.scalar
        def _(act):
            def take_out(i):
                act.wait_ge(pv_done, count(i, TB, TB))
                act.activation(OU[:, :, :].rearrange("p g (b n) -> p (g b) n", b=B)[:, i, :], psO[:, :, :].rearrange("p a n -> p (a n)"), ACT.Copy).then_inc(out_copied, 1)

            def exps(i):
                for c in range(TB):
                    for h in range(GH):
                        u = c * GH + h
                        act.wait_ge(b_done, count(i, NU, u + 1))
                        if c >= 2 or not (isinstance(i, int) and i < 1):
                            if h == 0:
                                act.wait_ge(pv_done, count(i, TB, c - 1))
                        act.activation(PT[:, c % 2, h, :], psB[:, u % 2, :, :].rearrange("p a n -> p (a n)"), ACT.Exp,
                                       scale=SCALE).then_inc(exp_done, 1)
                    if c == 0 and not (isinstance(i, int) and i < 1):
                        take_out(count(i, 1, -1))

            exps(0)
            exps(1)
            with act.Fori(1, NG // 2) as j:
                for e in range(2):
                    exps(j * 2 + e)
            take_out(NG - 1)

        @block.tensor
        def _(pe):
            def pass_a(i, u, n):
                h, t = divmod(u, TB)
                if not (isinstance(i, int) and i == 0 and u == 0):
                    pe.wait_ge(max_taken, count(i, 2 * NU, 2 * u + n - 1))
                pe.matmul(psA[:, n, :], QS[0:KQ, i % SLOTS, h, t * P:(t + 1) * P], KS[0:KQ, i % SLOTS, n * HALF:(n + 1) * HALF],
                          start=True, stop=True).then_inc(a_done, 1)

            def pass_b(i, u):
                c, h = divmod(u, GH)
                if not (isinstance(i, int) and i == 0 and u < 2):
                    pe.wait_ge(exp_done, count(i, NU, u - 1))
                for n in range(2):
                    mm = pe.matmul(psB[:, u % 2, n, :], KS[0:KM, i % SLOTS, c * P:(c + 1) * P],
                                   QS[0:KM, i % SLOTS, h, n * HALF:(n + 1) * HALF], start=True, stop=True)
                mm.then_inc(b_done, 1)

            def times_values(i, e, c, q):
                cols = slice(q % 2 * HALF // 2, (q % 2 + 1) * HALF // 2)
                if q == 0:
                    pe.wait_ge(exp_done, count(i, NU, (c + 1) * GH))
                if c == 0 and q == 0:
                    pe.wait_ge(v_copied, count(i, 1, 1))
                    if not (isinstance(i, int) and i < 1):
                        pe.wait_ge(out_copied, count(i, 1, 0))
                for h in range(GH):
                    mm = pe.matmul(psO[h * VW:(h + 1) * VW, q // 2, cols], VG[:, e, c, :], PT[:, c % 2, h, q * S // 4:(q + 1) * S // 4],
                                   start=(c == 0 and q % 2 == 0), stop=(c == TB - 1 and q % 2 == 1))
                if q == 3:
                    mm.then_inc(pv_done, 1)

            def group(i, e):
                pe.wait_ge(rows_set[e], count(i - e, NROWS // 2, NROWS))
                for u in range(NU):
                    ahead = 1 if u < NU // 2 else 2
                    has_a = not isinstance(i, int) or i + ahead < NG
                    if u == NU // 2 and has_a:
                        pe.wait_ge(loaded[e], count(i - e, NLOAD // 2, 2 * NLOAD))
                    if has_a:
                        pass_a(i + ahead, (u + NU // 2) % NU, 0)
                    pass_b(i, u)
                    if has_a:
                        pass_a(i + ahead, (u + NU // 2) % NU, 1)
                    c, q = divmod(u - GH - 1, 4)
                    if c >= 0:
                        times_values(i, e, c, q)
                    elif not (isinstance(i, int) and i < 1):
                        times_values(i - 1, 1 - e, c + TB, q)

            pe.wait_ge(ones_set, 1)
            pe.wait_ge(loaded[0], NLOAD)
            for u in range(NU):
                for n in range(2):
                    pass_a(0, u, n)
            pe.wait_ge(loaded[1], NLOAD)
            for u in range(NU // 2):
                for n in range(2):
                    pass_a(1, u, n)
            group(0, 0)
            group(1, 1)
            with pe.Fori(1, NG // 2 - 1) as j:
                for e in range(2):
                    group(j * 2 + e, e)
            group(NG - 2, 0)
            group(NG - 1, 1)
            for u in range(NU, NU + GH + 1):
                times_values(NG - 1, 1, *divmod(u - GH - 1, 4))


XH = 16
XD = 64
SC = 77
SCP = 96
XW = XH * XD
NPR = XH // 2
XSCALE = XD ** -0.5
NEG = -1e10
NEG_RAW = NEG / XSCALE


def at(i, per, plus):
    return i * per + plus


def peeled(i, below):
    return isinstance(i, int) and i < below


def staggered(eng, n, lags, step):
    depth = max(lags) + 1
    low = depth + 1 + (depth + 1) % 2
    for s in range(low):
        step(lambda lag, s=s: (s - lag, (s - lag) % 2) if 0 <= s - lag < n else None)
    with eng.Fori(low // 2, n // 2) as j:
        for e in range(2):
            step(lambda lag, j=j, e=e: (j * 2 + (e - lag), (e - lag) % 2))
    for s in range(n, n + depth - 1):
        step(lambda lag, s=s: (s - lag, (s - lag) % 2) if 0 <= s - lag < n else None)


def phase_self_out(nc, T):
    X, OU, ident = T["X"], T["OU"], T["ident"]
    with ExitStack() as ctx:
        def sb(name, shape, dt=F32):
            return ctx.enter_context(nc.sbuf_tensor(name, shape, dt))

        def sem(name):
            return ctx.enter_context(nc.semaphore(name))

        wo = sb("wo_sb", [P, KD, D])
        bo = sb("bo_sb", [P, D])
        OT = sb("OT", [P, 2, NKV, P])
        recip = sb("recip", [P, 2, NH])
        ON = sb("ON", [P, 2, D])
        ONT = sb("ONT", [P, 2, KD, P])
        psR = ctx.enter_context(nc.psum_tensor("psR", [P, 2, HALF], F32))
        psU = ctx.enter_context(nc.psum_tensor("psU", [P, 2, HALF], F32))
        psY = ctx.enter_context(nc.psum_tensor("psY", [P, 2, HALF], F32))
        w_in = sem("so_w_in")
        bias_added = sem("so_bias_added")
        sums_in = [sem("so_sums_in_even"), sem("so_sums_in_odd")]
        rows_done = sem("so_rows_done")
        recip_done = sem("so_recip_done")
        norm_done = sem("so_norm_done")
        turned = sem("so_turned")
        turned_in = sem("so_turned_in")
        y_done = sem("so_y_done")
        x_added = sem("so_x_added")
        block = ctx.enter_context(nc.Block())

        @block.sync
        def _(sp):
            sp.dma_start(wo[:, :, :], T["Wo"].rearrange("(k p) n -> p k n", p=P)).then_inc(w_in, 16)
            sp.dma_start(bo[:, :], T["bo"].rearrange("(a n) -> a n", a=1).to_broadcast([P, D])).then_inc(w_in, 16)

            def load(i, e):
                if not peeled(i, 2):
                    sp.wait_ge(rows_done, at(i, 1, -1))
                sp.dma_start(OT[:, e, :, :], OU[:, :, bass.ds(i * P, P)]).then_inc(sums_in[e], 16)

            load(0, 0)
            load(1, 1)
            with sp.Fori(1, NT // 2) as j:
                load(j * 2, 0)
                load(j * 2 + 1, 1)
            for e in range(2):
                sp.wait_ge(sums_in[e], 16 * (NT // 2))

        @block.gpsimd
        def _(pool):
            pool.wait_ge(w_in, 32)
            with pool.Fori(0, NT) as i:
                if True:
                    pool.tensor_tensor(X[:, i, :], X[:, i, :], bo[:, :], ALU.add).then_inc(bias_added, 1)
                pool.wait_ge(bias_added, at(i, 1, 1))

        @block.tensor
        def _(pe):
            pe.wait_ge(w_in, 32)

            def step(tile):
                if t := tile(2):
                    i, e = t
                    pe.wait_ge(turned_in, at(i, 1, 1))
                    if not peeled(i, 2):
                        pe.wait_ge(x_added, at(i, 1, -1))
                    for k in range(KD):
                        mm = pe.matmul(psY[:, e, 0:D], ONT[:, e, k, :], wo[:, k, :], start=(k == 0), stop=(k == KD - 1))
                    mm.then_inc(y_done, 1)
                if t := tile(1):
                    i, e = t
                    pe.wait_ge(norm_done, at(i, 1, 1))
                    if not peeled(i, 2):
                        pe.wait_ge(turned_in, at(i, 1, -1))
                    for k in range(KD):
                        mm = pe.transpose(psU[:, e, k * P:(k + 1) * P], ON[:, e, k * P:(k + 1) * P], ident[:, :])
                    mm.then_inc(turned, 1)
                if t := tile(0):
                    i, e = t
                    pe.wait_ge(sums_in[e], at(i - e, 8, 16))
                    if not peeled(i, 2):
                        pe.wait_ge(norm_done, at(i, 1, -1))
                    for g in range(NKV):
                        mm = pe.transpose(psR[:, e, g * P:(g + 1) * P], OT[:, e, g, :], ident[:, :])
                    mm.then_inc(rows_done, 1)

            staggered(pe, NT, (0, 1, 2), step)

        @block.vector
        def _(dve):
            def step(tile):
                if t := tile(0):
                    i, e = t
                    rows = psR[:, e, :].rearrange("p (h r) -> p h r", r=VW)
                    dve.wait_ge(rows_done, at(i, 1, 1))
                    if not peeled(i, 2):
                        dve.wait_ge(norm_done, at(i, 1, -1))
                        dve.wait_ge(turned, at(i, 1, -1))
                    dve.reciprocal(recip[:, e, :], rows[:, :, HD]).then_inc(recip_done, 1)
                    dve.wait_ge(recip_done, at(i, 1, 1))
                    dve.tensor_tensor(ON[:, e, :].rearrange("p (h d) -> p h d", d=HD), rows[:, :, 0:HD],
                                      recip[:, e, :].rearrange("p (h a) -> p h a", a=1).to_broadcast([P, NH, HD]),
                                      ALU.mult).then_inc(norm_done, 1)
                if t := tile(2):
                    i, e = t
                    dve.wait_ge(y_done, at(i, 1, 1))
                    dve.wait_ge(bias_added, at(i, 1, 1))
                    dve.tensor_tensor(X[:, i, :], psY[:, e, 0:D], X[:, i, :], ALU.add).then_inc(x_added, 1)

            staggered(dve, NT, (0, 1, 2), step)

        @block.scalar
        def _(act):
            def copy(i, e):
                act.wait_ge(turned, at(i, 1, 1))
                if not peeled(i, 2):
                    act.wait_ge(y_done, at(i, 1, -1))
                act.activation(ONT[:, e, :, :], psU[:, e, 0:D].rearrange("p (k n) -> p k n", k=KD), ACT.Copy).then_inc(turned_in, 1)

            copy(0, 0)
            copy(1, 1)
            with act.Fori(1, NT // 2) as j:
                copy(j * 2, 0)
                copy(j * 2 + 1, 1)


def phase_context(nc, T):
    ident, KX, VX = T["ident"], T["KX"], T["VX"]
    with ExitStack() as ctx:
        def sb(name, shape, dt=F32):
            return ctx.enter_context(nc.sbuf_tensor(name, shape, dt))

        def sem(name):
            return ctx.enter_context(nc.semaphore(name))

        wk = sb("wkx_sb", [P, KD, XW])
        wv = sb("wvx_sb", [P, KD, XW])
        cx = sb("cx", [SC, 2, D])
        cxT = sb("cxT", [P, KD, SC])
        psT = ctx.enter_context(nc.psum_tensor("psTc", [P, KD, P], F32))
        psK = ctx.enter_context(nc.psum_tensor("psKc", [P, 2, HALF], F32))
        psV = ctx.enter_context(nc.psum_tensor("psVc", [P, 2, HALF], F32))
        w_in = sem("cx_w_in")
        cleared = sem("cx_cleared")
        c_in = [sem("cx_in_even"), sem("cx_in_odd")]
        turned = sem("cx_turned")
        turned_in = sem("cx_turned_in")
        k_done = sem("cx_k_done")
        k_in = sem("cx_k_in")
        v_done = sem("cx_v_done")
        v_in = sem("cx_v_in")
        block = ctx.enter_context(nc.Block())

        @block.sync
        def _(sp):
            sp.dma_start(wk[:, :, :], T["Wkx"].rearrange("(k p) n -> p k n", p=P)).then_inc(w_in, 16)
            sp.dma_start(wv[:, :, :], T["Wvx"].rearrange("(k p) n -> p k n", p=P)).then_inc(w_in, 16)
            for b in range(B):
                if b >= 2:
                    sp.wait_ge(turned, b - 1)
                sp.dma_start(cx[:, b % 2, :], T["ctx"][b, :, :]).then_inc(c_in[b % 2], 16)

        @block.gpsimd
        def _(pool):
            pool.memset(KX[:, :, :, :], 0.0).then_inc(cleared, 1)
            pool.wait_ge(cleared, 1)
            pool.memset(VX[:, :, :], 0.0).then_inc(cleared, 1)

        @block.tensor
        def _(pe):
            pe.wait_ge(w_in, 32)
            for b in range(B):
                pe.wait_ge(c_in[b % 2], 16 * (b // 2 + 1))
                if b:
                    pe.wait_ge(turned_in, b)
                for k in range(KD):
                    mm = pe.transpose(psT[:, k, 0:SC], cx[:, b % 2, k * P:(k + 1) * P], ident[0:SC, 0:SC])
                mm.then_inc(turned, 1)
                pe.wait_ge(turned_in, b + 1)
                for r in range(NPR):
                    if b and r % 4 == 0:
                        pe.wait_ge(k_in, 4 * (b - 1) + 2 * (r // 4) + 2)
                    for k in range(KD):
                        mm = pe.matmul(psK[:, r // 4, (r % 4) * SC:(r % 4 + 1) * SC], wk[:, k, r * P:(r + 1) * P], cxT[:, k, :],
                                       start=(k == 0), stop=(k == KD - 1))
                    if r % 4 == 3:
                        mm.then_inc(k_done, 1)
                for n in range(2):
                    if b:
                        pe.wait_ge(v_in, 2 * (b - 1) + n + 1)
                    for k in range(KD):
                        mm = pe.matmul(psV[0:SC, n, :], cxT[:, k, :], wv[:, k, n * HALF:(n + 1) * HALF],
                                       start=(k == 0), stop=(k == KD - 1))
                    mm.then_inc(v_done, 1)

        @block.vector
        def _(dve):
            dve.wait_ge(cleared, 2)
            for b in range(B):
                for n in range(2):
                    dve.wait_ge(v_done, 2 * b + n + 1)
                    dve.tensor_copy(VX[0:SC, b, n * HALF:(n + 1) * HALF], psV[0:SC, n, :]).then_inc(v_in, 1)

        @block.scalar
        def _(act):
            act.wait_ge(cleared, 2)
            for b in range(B):
                act.wait_ge(turned, b + 1)
                if b:
                    act.wait_ge(v_done, 2 * b)
                act.activation(cxT[:, :, :], psT[:, :, 0:SC], ACT.Copy).then_inc(turned_in, 1)
                for q in range(2):
                    act.wait_ge(k_done, 2 * b + q + 1)
                    for half in range(2):
                        rows = slice(half * XD, (half + 1) * XD)
                        act.activation(KX[rows, b, 4 * q:4 * q + 4, half * SC:(half + 1) * SC],
                                       psK[rows, q, 0:4 * SC].rearrange("p (r n) -> p r n", n=SC), ACT.Copy).then_inc(k_in, 1)


def phase_cross(nc, T):
    X, ident, KX, VX = T["X"], T["ident"], T["KX"], T["VX"]
    with ExitStack() as ctx:
        def sb(name, shape, dt=F32):
            return ctx.enter_context(nc.sbuf_tensor(name, shape, dt))

        def sem(name):
            return ctx.enter_context(nc.semaphore(name))

        wq = sb("wqx_sb", [P, KD, XW])
        wo = sb("wox_sb", [P, NPR, D])
        mask = sb("mask_sb", [P, 2, SC], I32)
        stats = sb("x_stats", [P, 2, 6])
        mean_var = sb("x_mean_var", [P, 2, 2])
        var_eps = sb("x_var_eps", [P, 2])
        neg_half = sb("x_neg_half", [P, 1])
        rstd = sb("x_rstd", [P, 2])
        xn = sb("x_xn", [P, 2, D])
        xnT = sb("x_xnT", [P, 2, KD, P])
        qT = sb("x_qT", [P, 2, NPR, P])
        SX = sb("x_scores", [P, 2, XH, SCP])
        row_max = sb("x_row_max", [P, XH])
        row_sum = sb("x_row_sum", [P, 2, XH])
        recip = sb("x_recip", [P, 2, XH])
        ET = sb("x_ET", [SCP, XH, P])
        ON = sb("x_ON", [P, XH, XD])
        OT = sb("x_OT", [P, NPR, P])
        ps = ctx.enter_context(nc.psum_tensor("ps_cross", [P, 8, HALF], F32))
        Q, OTU, E, SU, XT, Y, O = 0, 2, 4, 8, 12, 13, 14
        L_LN, L_XT, L_Q, L_SM, L_E, L_O = 0, 1, 2, 3, 4, 5

        w_in = sem("x_w_in")
        mask_in = [sem("x_mask_in_even"), sem("x_mask_in_odd")]
        const = sem("x_const")
        waited_pool = sem("x_waited_pool")
        waited_dve = sem("x_waited_dve")
        filled = sem("x_filled")
        stats_done = sem("x_stats_done")
        mv_done = sem("x_mv_done")
        veps_done = sem("x_veps_done")
        rstd_done = sem("x_rstd_done")
        xn_done = sem("x_xn_done")
        xt_done, xt_in = sem("x_xt_done"), sem("x_xt_in")
        q_done, q_in = sem("x_q_done"), sem("x_q_in")
        s_done, s_in = sem("x_s_done"), sem("x_s_in")
        max_done = sem("x_max_done")
        sub_done = sem("x_sub_done")
        exp_done = sem("x_exp_done")
        sum_done = sem("x_sum_done")
        recip_done = sem("x_recip_done")
        e_done, e_in = sem("x_e_done"), sem("x_e_in")
        o_done, o_in = sem("x_o_done"), sem("x_o_in")
        ot_done, ot_in = sem("x_ot_done"), sem("x_ot_in")
        y_done, y_in = sem("x_y_done"), sem("x_y_in")
        block = ctx.enter_context(nc.Block())

        @block.sync
        def _(sp):
            sp.dma_start(wq[:, :, :], T["Wqx"].rearrange("(k p) n -> p k n", p=P)).then_inc(w_in, 16)
            sp.dma_start(wo[:, :, :], T["Wox"].rearrange("(k p) n -> p k n", p=P)).then_inc(w_in, 16)
            mk = T["mask"].rearrange("b (t p) n -> (b t) p n", p=P)
            def load(i, e):
                if not peeled(i, 2):
                    sp.wait_ge(s_in, at(i, 4, -4))
                sp.dma_start(mask[:, e, :], mk[i, :, :]).then_inc(mask_in[e], 16)

            load(0, 0)
            load(1, 1)
            with sp.Fori(1, NT // 2) as j:
                load(j * 2, 0)
                load(j * 2 + 1, 1)
            for e in range(2):
                sp.wait_ge(mask_in[e], 16 * (NT // 2))

        @block.gpsimd
        def _(pool):
            pool.memset(neg_half[:, :], -0.5).then_inc(const, 1)
            pool.wait_ge(const, 1)
            pool.memset(SX[:, :, :, :], 0.0).then_inc(const, 1)
            pool.wait_ge(const, 2)

            def step(tile):
                if t := tile(L_LN):
                    i, e = t
                    pool.wait_ge(veps_done, at(i, 1, 1))
                    pool.tensor_tensor(rstd[:, e:e + 1], var_eps[:, e:e + 1], neg_half[:, :], ALU.pow).then_inc(rstd_done, 1)
                    pool.wait_ge(rstd_done, at(i, 1, 1))
                if t := tile(L_Q):
                    i, e = t
                    if not peeled(i, 2):
                        pool.wait_ge(e_done, at(i, 4, -4))
                        pool.wait_ge(sum_done, at(i, 1, -1))
                        pool.sem_inc(waited_pool, 1)
                    pool.memset(SX[:, e, :, 0:SC], NEG_RAW).then_inc(filled, 1)
                    pool.wait_ge(filled, at(i, 1, 1))

            staggered(pool, NT, range(6), step)

        @block.tensor
        def _(pe):
            pe.wait_ge(w_in, 32)

            READ = {Q: (2, L_Q, q_in), OTU: (2, L_O, ot_in), E: (4, L_E, e_in), SU: (4, L_Q, s_in),
                    XT: (1, L_XT, xt_in), Y: (1, L_O, y_in), O: (2, L_E, o_in)}

            def unit_of(u):
                base = max(b for b in READ if b <= u)
                return (base,) + READ[base]

            def bank_free(tile, u):
                base, n, lag, read = unit_of(u)
                i, _ = tile(lag)
                if not peeled(i, 1):
                    pe.wait_ge(read, at(i, n, u - base + 1 - n))
                base, n, lag, read = unit_of((u + 8) % 16)
                t = tile(lag) if u >= 8 else tile(lag + 1)
                if t:
                    pe.wait_ge(read, at(t[0], n, (u + 8) % 16 - base + 1))

            def step(tile):
                if t := tile(L_Q):
                    i, e = t
                    pe.wait_ge(xt_in, at(i, 1, 1))
                    for n in range(2):
                        bank_free(tile, Q + n)
                        for r in range(4):
                            for k in range(KD):
                                pair = 4 * n + r
                                mm = pe.matmul(ps[:, (Q + n) % 8, r * P:(r + 1) * P], wq[:, k, pair * P:(pair + 1) * P],
                                               xnT[:, e, k, :], start=(k == 0), stop=(k == KD - 1))
                        mm.then_inc(q_done, 1)
                if t := tile(L_O):
                    i, e = t
                    for n in range(2):
                        bank_free(tile, OTU + n)
                        pe.wait_ge(o_in, at(i, 2, n + 1))
                        for r in range(4):
                            pair = 4 * n + r
                            mm = pe.transpose(ps[:, (OTU + n) % 8, r * P:(r + 1) * P], ON[:, 2 * pair:2 * pair + 2, :], ident[:, :])
                        mm.then_inc(ot_done, 1)
                if t := tile(L_E):
                    i, e = t
                    pe.wait_ge(exp_done, at(i, 1, 1))
                    for n in range(4):
                        bank_free(tile, E + n)
                        for h in range(4):
                            mm = pe.transpose(ps[0:SCP, (E + n) % 8, h * P:(h + 1) * P], SX[:, e, 4 * n + h, :], ident[:, :])
                        mm.then_inc(e_done, 1)
                if t := tile(L_Q):
                    i, e = t
                    for n in range(4):
                        bank_free(tile, SU + n)
                        for r in range(2):
                            pair = 2 * n + r
                            mm = pe.matmul(ps[:, (SU + n) % 8, r * 2 * SC:(r + 1) * 2 * SC], qT[:, e, pair, :],
                                           KX[:, i // TB, pair, :], start=True, stop=True)
                        mm.then_inc(s_done, 1)
                if t := tile(L_XT):
                    i, e = t
                    bank_free(tile, XT)
                    pe.wait_ge(xn_done, at(i, 1, 1))
                    for k in range(KD):
                        mm = pe.transpose(ps[:, XT % 8, k * P:(k + 1) * P], xn[:, e, k * P:(k + 1) * P], ident[:, :])
                    mm.then_inc(xt_done, 1)
                if t := tile(L_O):
                    i, e = t
                    bank_free(tile, Y)
                    pe.wait_ge(ot_in, at(i, 2, 2))
                    for k in range(NPR):
                        mm = pe.matmul(ps[:, Y % 8, 0:D], OT[:, k, :], wo[:, k, :], start=(k == 0), stop=(k == NPR - 1))
                    mm.then_inc(y_done, 1)
                if t := tile(L_E):
                    i, e = t
                    for n in range(2):
                        bank_free(tile, O + n)
                        for h in range(8):
                            head = 8 * n + h
                            mm = pe.matmul(ps[:, (O + n) % 8, h * XD:(h + 1) * XD], ET[:, head, :],
                                           VX[:, i // TB, head * XD:(head + 1) * XD], start=True, stop=True)
                        mm.then_inc(o_done, 1)

            staggered(pe, NT, range(6), step)

        @block.vector
        def _(dve):
            dve.wait_ge(const, 2)

            def step(tile):
                if t := tile(L_O):
                    i, e = t
                    dve.wait_ge(recip_done, at(i, 1, 1))
                    for n in range(2):
                        dve.wait_ge(o_done, at(i, 2, n + 1))
                        if not peeled(i, 1):
                            dve.wait_ge(ot_done, at(i, 2, n - 1))
                        dve.tensor_tensor(ON[:, 8 * n:8 * n + 8, :], ps[:, (O + n) % 8, :].rearrange("p (h d) -> p h d", d=XD),
                                          recip[:, e, 8 * n:8 * n + 8].rearrange("p (h a) -> p h a", a=1).to_broadcast([P, 8, XD]),
                                          ALU.mult).then_inc(o_in, 1)
                if t := tile(L_E):
                    i, e = t
                    dve.wait_ge(exp_done, at(i, 1, 1))
                    dve.tensor_reduce(row_sum[:, e, :], SX[:, e, :, 0:SC], axis=AX.X, op=ALU.add).then_inc(sum_done, 1)
                    dve.wait_ge(sum_done, at(i, 1, 1))
                    dve.reciprocal(recip[:, e, :], row_sum[:, e, :]).then_inc(recip_done, 1)
                if t := tile(L_SM):
                    i, e = t
                    dve.wait_ge(s_in, at(i, 4, 4))
                    dve.tensor_reduce(row_max[:, :], SX[:, e, :, 0:SC], axis=AX.X, op=ALU.max).then_inc(max_done, 1)
                    dve.wait_ge(max_done, at(i, 1, 1))
                    dve.tensor_tensor(SX[:, e, :, 0:SC], SX[:, e, :, 0:SC],
                                      row_max[:, :].rearrange("p (h a) -> p h a", a=1).to_broadcast([P, XH, SC]),
                                      ALU.subtract).then_inc(sub_done, 1)
                if t := tile(L_LN):
                    i, e = t
                    dve.bn_stats(stats[:, e, :], X[:, i, :]).then_inc(stats_done, 1)
                    dve.wait_ge(stats_done, at(i, 1, 1))
                    dve.sem_inc(waited_dve, 1)
                    dve.bn_aggr(mean_var[:, e, :], stats[:, e, :]).then_inc(mv_done, 1)
                    dve.wait_ge(mv_done, at(i, 1, 1))
                    dve.tensor_scalar(var_eps[:, e:e + 1], mean_var[:, e, 1:2], LN_EPS, None, ALU.add).then_inc(veps_done, 1)
                if t := tile(L_Q):
                    i, e = t
                    dve.wait_ge(filled, at(i, 1, 1))
                    dve.wait_ge(mask_in[e], at(i - e, 8, 16))
                    for n in range(4):
                        dve.wait_ge(s_done, at(i, 4, n + 1))
                        dve.sem_inc(waited_dve, 1)
                        dve.copy_predicated(SX[:, e, 4 * n:4 * n + 4, 0:SC], mask[:, e, :].rearrange("p (a n) -> p a n", a=1).to_broadcast([P, 4, SC]),
                                            ps[:, (SU + n) % 8, 0:4 * SC].rearrange("p (h n) -> p h n", n=SC)).then_inc(s_in, 1)
                if t := tile(L_LN):
                    i, e = t
                    dve.wait_ge(rstd_done, at(i, 1, 1))
                    if not peeled(i, 2):
                        dve.wait_ge(xt_done, at(i, 1, -1))
                    dve.tensor_scalar(xn[:, e, :], X[:, i, :], mean_var[:, e, 0:1], rstd[:, e:e + 1],
                                      ALU.subtract, ALU.mult).then_inc(xn_done, 1)
                if t := tile(L_O):
                    i, e = t
                    dve.wait_ge(y_done, at(i, 1, 1))
                    dve.tensor_tensor(X[:, i, :], ps[:, Y % 8, 0:D], X[:, i, :], ALU.add).then_inc(y_in, 1)

            staggered(dve, NT, range(6), step)

        @block.scalar
        def _(act):
            def step(tile):
                if t := tile(L_Q):
                    i, e = t
                    for n in range(2):
                        act.wait_ge(q_done, at(i, 2, n + 1))
                        if not peeled(i, 2):
                            act.wait_ge(s_done, at(i, 4, -4))
                        act.activation(qT[:, e, 4 * n:4 * n + 4, :], ps[:, (Q + n) % 8, :].rearrange("p (r n) -> p r n", n=P),
                                       ACT.Copy).then_inc(q_in, 1)
                if t := tile(L_O):
                    i, e = t
                    for n in range(2):
                        act.wait_ge(ot_done, at(i, 2, n + 1))
                        if not peeled(i, 1):
                            act.wait_ge(y_done, at(i, 1, 0))
                        act.activation(OT[:, 4 * n:4 * n + 4, :], ps[:, (OTU + n) % 8, :].rearrange("p (r n) -> p r n", n=P),
                                       ACT.Copy).then_inc(ot_in, 1)
                if t := tile(L_E):
                    i, e = t
                    for n in range(4):
                        act.wait_ge(e_done, at(i, 4, n + 1))
                        if not peeled(i, 1):
                            act.wait_ge(o_done, at(i, 2, n // 2 - 1))
                        act.activation(ET[:, 4 * n:4 * n + 4, :], ps[0:SCP, (E + n) % 8, :].rearrange("p (h n) -> p h n", n=P),
                                       ACT.Copy).then_inc(e_in, 1)
                if t := tile(L_SM):
                    i, e = t
                    act.wait_ge(sub_done, at(i, 1, 1))
                    act.activation(SX[:, e, :, 0:SC], SX[:, e, :, 0:SC], ACT.Exp, scale=XSCALE).then_inc(exp_done, 1)
                if t := tile(L_XT):
                    i, e = t
                    act.wait_ge(xt_done, at(i, 1, 1))
                    if not peeled(i, 2):
                        act.wait_ge(q_done, at(i, 2, -2))
                    act.activation(xnT[:, e, :, :], ps[:, XT % 8, 0:D].rearrange("p (k n) -> p k n", n=P), ACT.Copy).then_inc(xt_in, 1)

            staggered(act, NT, range(6), step)


NE = 8
TOP = 2
FI = 512
KF = FI // P
TOPK_EPS = 1e-5
NTM = (TOP * B * S + NE * (P - 1)) // P
NTM += NTM % 2
NSLOT = NTM * P


QUAD = 4


def phase_norm(nc, T):
    X, XF, LG, ident = T["X"], T["XF"], T["LG"], T["ident"]
    WG, WU, WD = T["WG"], T["WU"], T["WD"]
    with ExitStack() as ctx:
        def sb(name, shape, dt=F32):
            return ctx.enter_context(nc.sbuf_tensor(name, shape, dt))

        def sem(name):
            return ctx.enter_context(nc.semaphore(name))

        gate = sb("gate_sb", [P, KD, NE])
        affine = sb("affine_sb", [P, 2, KD])
        stats = sb("n_stats", [P, 2, 2, QUAD, 6])
        mean_var = sb("n_mean_var", [P, 2, 2, QUAD, 2])
        var_eps = sb("n_var_eps", [P, 2, 2, QUAD])
        neg_half = sb("n_neg_half", [P, QUAD])
        rstd = sb("n_rstd", [P, 2, 2, QUAD])
        xr = sb("n_xr", [P, 2, QUAD, D])
        xrT = sb("n_xrT", [P, 2, KD, QUAD * P])
        psT = ctx.enter_context(nc.psum_tensor("n_psT", [P, 2, KD, QUAD * P], F32))
        psL = ctx.enter_context(nc.psum_tensor("n_psL", [P, 2, HALF], F32))
        w_in = sem("n_w_in")
        const = sem("n_const")
        waited_dve = sem("n_waited_dve")
        experts_in = sem("n_experts_in")
        stats_done = [sem("n_stats1"), sem("n_stats2")]
        mv_done = [sem("n_mv1"), sem("n_mv2")]
        veps_done = [sem("n_veps1"), sem("n_veps2")]
        rstd_done = [sem("n_rstd1"), sem("n_rstd2")]
        xf_done, xr_done = sem("n_xf_done"), sem("n_xr_done")
        t_done, xr_in = sem("n_t_done"), sem("n_xr_in")
        l_done, l_in = sem("n_l_done"), sem("n_l_in")
        block = ctx.enter_context(nc.Block())
        NQ = NT // QUAD

        @block.sync
        def _(sp):
            sp.dma_start(gate[:, :, :], T["gateT"].rearrange("(k p) n -> p k n", p=P)).then_inc(w_in, 16)
            sp.dma_start(affine[:, :, :], T["affine"]).then_inc(w_in, 16)
            for x in range(NE):
                sp.dma_start(WG[:, x, :, :], T["Wg"][x, :, :].rearrange("(k p) n -> p k n", p=P)).then_inc(experts_in, 16)
                sp.dma_start(WU[:, x, :, :], T["Wu"][x, :, :].rearrange("(k p) n -> p k n", p=P)).then_inc(experts_in, 16)
                sp.dma_start(WD[:, x, :, :], T["Wd"][x, :, :].rearrange("(k p) n -> p k n", p=P)).then_inc(experts_in, 16)
            sp.wait_ge(experts_in, 16 * 3 * NE)

        @block.gpsimd
        def _(pool):
            pool.memset(neg_half[:, :], -0.5).then_inc(const, 1)
            pool.wait_ge(const, 1)

            def step(quad):
                for which in range(2):
                    if t := quad(which):
                        i, e = t
                        pool.wait_ge(veps_done[which], at(i, 1, 1))
                        pool.tensor_tensor(rstd[:, which, e, :], var_eps[:, which, e, :], neg_half[:, :],
                                           ALU.pow).then_inc(rstd_done[which], 1)
                        pool.wait_ge(rstd_done[which], at(i, 1, 1))

            staggered(pool, NQ, range(4), step)

        @block.tensor
        def _(pe):
            pe.wait_ge(w_in, 16 * 2)

            def step(quad):
                if t := quad(3):
                    i, e = t
                    pe.wait_ge(xr_in, at(i, 1, 1))
                    if not peeled(i, 2):
                        pe.wait_ge(l_in, at(i, 1, -1))
                    for q in range(QUAD):
                        for k in range(KD):
                            mm = pe.matmul(psL[:, e, q * NE:(q + 1) * NE], xrT[:, e, k, q * P:(q + 1) * P], gate[:, k, :],
                                           start=(k == 0), stop=(k == KD - 1))
                    mm.then_inc(l_done, 1)
                if t := quad(2):
                    i, e = t
                    pe.wait_ge(xr_done, at(i, QUAD, QUAD))
                    if not peeled(i, 2):
                        pe.wait_ge(xr_in, at(i, 1, -1))
                    for q in range(QUAD):
                        for k in range(KD):
                            mm = pe.transpose(psT[:, e, k, q * P:(q + 1) * P], xr[:, e, q, k * P:(k + 1) * P], ident[:, :])
                    mm.then_inc(t_done, 1)

            staggered(pe, NQ, range(4), step)

        @block.vector
        def _(dve):
            def statistics(i, e, which, source):
                for q in range(QUAD):
                    dve.bn_stats(stats[:, which, e, q, :], source[:, i * QUAD + q, :]).then_inc(stats_done[which], 1)
                dve.wait_ge(stats_done[which], at(i, QUAD, QUAD))
                dve.sem_inc(waited_dve, 1)
                for q in range(QUAD):
                    dve.bn_aggr(mean_var[:, which, e, q, :], stats[:, which, e, q, :]).then_inc(mv_done[which], 1)
                dve.wait_ge(mv_done[which], at(i, QUAD, QUAD))
                dve.tensor_scalar(var_eps[:, which, e, :], mean_var[:, which, e, :, 1], LN_EPS, None,
                                  ALU.add).then_inc(veps_done[which], 1)

            def step(quad):
                if t := quad(1):
                    i, e = t
                    dve.wait_ge(rstd_done[0], at(i, 1, 1))
                    for q in range(QUAD):
                        dve.tensor_scalar(XF[:, i * QUAD + q, :], X[:, i * QUAD + q, :], mean_var[:, 0, e, q, 0:1],
                                          rstd[:, 0, e, q:q + 1], ALU.subtract, ALU.mult).then_inc(xf_done, 1)
                if t := quad(2):
                    i, e = t
                    dve.wait_ge(rstd_done[1], at(i, 1, 1))
                    if not peeled(i, 2):
                        dve.wait_ge(t_done, at(i, 1, -1))
                    for q in range(QUAD):
                        dve.tensor_scalar(xr[:, e, q, :], XF[:, i * QUAD + q, :], mean_var[:, 1, e, q, 0:1],
                                          rstd[:, 1, e, q:q + 1], ALU.subtract, ALU.mult).then_inc(xr_done, 1)
                if t := quad(0):
                    i, e = t
                    if not peeled(i, 2):
                        dve.wait_ge(xf_done, at(i, QUAD, -QUAD))
                        dve.sem_inc(waited_dve, 1)
                    statistics(i, e, 0, X)
                if t := quad(1):
                    i, e = t
                    dve.wait_ge(xf_done, at(i, QUAD, QUAD))
                    dve.sem_inc(waited_dve, 1)
                    if not peeled(i, 2):
                        dve.wait_ge(xr_done, at(i, QUAD, -QUAD))
                        dve.sem_inc(waited_dve, 1)
                    statistics(i, e, 1, XF)
                if t := quad(3):
                    i, e = t
                    dve.wait_ge(l_done, at(i, 1, 1))
                    dve.tensor_copy(LG[:, bass.ds(i * QUAD, QUAD), :],
                                    psL[:, e, 0:QUAD * NE].rearrange("p (q n) -> p q n", n=NE)).then_inc(l_in, 1)

            staggered(dve, NQ, range(4), step)

        @block.scalar
        def _(act):
            act.wait_ge(w_in, 16 * 2)

            def step(quad):
                if t := quad(2):
                    i, e = t
                    act.wait_ge(t_done, at(i, 1, 1))
                    if not peeled(i, 2):
                        act.wait_ge(l_done, at(i, 1, -1))
                    for k in range(KD):
                        ins = act.activation(xrT[:, e, k, :], psT[:, e, k, :], ACT.Identity,
                                             scale=affine[:, 0, k:k + 1], bias=affine[:, 1, k:k + 1])
                    ins.then_inc(xr_in, 1)

            staggered(act, NQ, range(4), step)


def tile_semaphores(stack, nc):
    def sem(name):
        return stack.enter_context(nc.semaphore(f"tile_{name}"))

    return ([sem("x_even"), sem("x_odd")],) + tuple(sem(name) for name in (
        "t_done", "t_in", "g_done", "u_done", "silu_done", "h_done", "ht_done", "ht_in", "y_done", "y_in"))


def shared_half(nc, T, first, base, pool_beside, dve_beside=None, sync_beside=None):
    X, XF, ident = T["X"], T["XF"], T["ident"]
    N = NT // 2
    tag = f"s{first}"
    with ExitStack() as ctx:
        def sb(name, shape, dt=F32):
            return ctx.enter_context(nc.sbuf_tensor(f"{tag}_{name}", shape, dt))

        def psum(name, banks):
            return ctx.enter_context(nc.psum_tensor(f"{tag}_{name}", [P, banks, HALF], F32))

        def sem(name):
            return ctx.enter_context(nc.semaphore(f"{tag}_{name}"))

        wg = sb("wg", [P, KD, FI])
        wu = sb("wu", [P, KD, FI])
        wd = sb("wd", [P, KF, D])
        xt = sb("xt", [P, 2, D])
        xfT = sb("xfT", [P, 2, KD, P])
        SG = sb("silu", [P, 2, FI])
        H = sb("h", [P, 2, FI])
        HT = sb("hT", [P, 2, KF, P])
        psG, psU, psT, psH, psY = psum("psG", 2), psum("psU", 2), psum("psT", 1), psum("psH", 1), psum("psY", 2)
        w_in = sem("w_in")
        x_in, t_done, t_in, g_done, u_done, silu_done, h_done, ht_done, ht_in, y_done, y_in = T["tile_sems"]
        block = ctx.enter_context(nc.Block())

        @block.sync
        def _(sp):
            sp.dma_start(wg[:, :, :], T["sWg"].rearrange("(k p) n -> p k n", p=P)).then_inc(w_in, 16)
            sp.dma_start(wu[:, :, :], T["sWu"].rearrange("(k p) n -> p k n", p=P)).then_inc(w_in, 16)
            sp.dma_start(wd[:, :, :], T["sWd"].rearrange("(k p) n -> p k n", p=P)).then_inc(w_in, 16)

            def load(i, e):
                if not peeled(i, 2):
                    sp.wait_ge(t_done, at(i, 1, base - 1))
                sp.dma_start(xt[:, e, :], XF[:, bass.ds(i + first, 1), :]).then_inc(x_in[e], 16)

            load(0, 0)
            load(1, 1)
            load(2, 0)
            load(3, 1)
            with sp.Fori(2, N // 2) as j:
                load(j * 2, 0)
                load(j * 2 + 1, 1)
                if sync_beside:
                    sync_beside(sp, j - 2)
            for e in range(2):
                sp.wait_ge(x_in[e], 8 * (base + N))
            if sync_beside:
                for j in range(N // 2 - 2, N // 2):
                    sync_beside(sp, j)

        @block.gpsimd
        def _(pool):
            pool_beside(pool)

        @block.tensor
        def _(pe):
            def step(tile):
                if t := tile(2):
                    i, e = t
                    pe.wait_ge(h_done, at(i, 1, base + 1))
                    if not peeled(i, 1):
                        pe.wait_ge(ht_in, at(i, 1, base))
                    for k in range(KF):
                        mm = pe.transpose(psH[:, 0, k * P:(k + 1) * P], H[:, e, k * P:(k + 1) * P], ident[:, :])
                    mm.then_inc(ht_done, 1)
                if t := tile(1):
                    i, e = t
                    if isinstance(i, int) and i == 0:
                        pe.wait_ge(w_in, 16 * 3)
                    pe.wait_ge(t_in, at(i, 1, base + 1))
                    for w, bank, done, read in ((wg, psG, g_done, silu_done), (wu, psU, u_done, h_done)):
                        if not peeled(i, 2):
                            pe.wait_ge(read, at(i, 1, base - 1))
                        for k in range(KD):
                            mm = pe.matmul(bank[:, e, :], xfT[:, e, k, :], w[:, k, :], start=(k == 0), stop=(k == KD - 1))
                        mm.then_inc(done, 1)
                if t := tile(0):
                    i, e = t
                    pe.wait_ge(x_in[e], at(i - e, 8, 8 * base + 16))
                    if not peeled(i, 1):
                        pe.wait_ge(t_in, at(i, 1, base))
                    for k in range(KD):
                        mm = pe.transpose(psT[:, 0, k * P:(k + 1) * P], xt[:, e, k * P:(k + 1) * P], ident[:, :])
                    mm.then_inc(t_done, 1)
                if t := tile(2):
                    i, e = t
                    pe.wait_ge(ht_in, at(i, 1, base + 1))
                    if not peeled(i, 2):
                        pe.wait_ge(y_in, at(i, 1, base - 1))
                    for k in range(KF):
                        mm = pe.matmul(psY[:, e, 0:D], HT[:, e, k, :], wd[:, k, :], start=(k == 0), stop=(k == KF - 1))
                    mm.then_inc(y_done, 1)

            staggered(pe, N, range(3), step)

        @block.vector
        def _(dve):
            def step(tile):
                if t := tile(1):
                    i, e = t
                    dve.wait_ge(silu_done, at(i, 1, base + 1))
                    dve.wait_ge(u_done, at(i, 1, base + 1))
                    if not peeled(i, 2):
                        dve.wait_ge(ht_done, at(i, 1, base - 1))
                    dve.tensor_tensor(H[:, e, :], psU[:, e, :], SG[:, e, :], ALU.mult).then_inc(h_done, 1)
                if t := tile(2):
                    i, e = t
                    dve.wait_ge(y_done, at(i, 1, base + 1))
                    dve.tensor_tensor(X[:, i + first, :], psY[:, e, 0:D], X[:, i + first, :], ALU.add).then_inc(y_in, 1)
                    if dve_beside:
                        dve.wait_ge(y_in, at(i, 1, base + 1))
                        dve_beside(dve, i, e)

            staggered(dve, N, range(3), step)

        @block.scalar
        def _(act):
            def step(tile):
                if t := tile(2):
                    i, e = t
                    act.wait_ge(ht_done, at(i, 1, base + 1))
                    if not peeled(i, 2):
                        act.wait_ge(y_done, at(i, 1, base - 1))
                    act.activation(HT[:, e, :, :], psH[:, 0, :].rearrange("p (k n) -> p k n", n=P), ACT.Copy).then_inc(ht_in, 1)
                if t := tile(1):
                    i, e = t
                    act.wait_ge(g_done, at(i, 1, base + 1))
                    if not peeled(i, 2):
                        act.wait_ge(h_done, at(i, 1, base - 1))
                    act.activation(SG[:, e, :], psG[:, e, :], ACT.Silu).then_inc(silu_done, 1)
                if t := tile(0):
                    i, e = t
                    act.wait_ge(t_done, at(i, 1, base + 1))
                    if not peeled(i, 2):
                        act.wait_ge(u_done, at(i, 1, base - 1))
                    act.activation(xfT[:, e, :, :], psT[:, 0, 0:D].rearrange("p (k n) -> p k n", n=P), ACT.Copy).then_inc(t_in, 1)

            staggered(act, N, range(3), step)


def phase_scatter(nc, T):
    XF, POS, xs = T["XF"], T["POS"], T["xs"]
    with nc.semaphore("scattered") as scattered:
        def scatter(pool):
            for t in range(NT):
                for c in range(TOP):
                    pool.indirect_dma_start(out=xs, out_offset=bass.IndirectOffsetOnAxis(ap=POS[:, c, t:t + 1], axis=0),
                                            in_=XF[:, t, :], in_offset=None).then_inc(scattered, 16)
            pool.wait_ge(scattered, 16 * TOP * NT)

        shared_half(nc, T, 0, 0, scatter)


def phase_route(nc, T):
    LG, W12, POS, tile_expert = T["LG"], T["W12"], T["POS"], T["tile_expert"]
    with ExitStack() as ctx:
        def sb(name, shape, dt=F32):
            return ctx.enter_context(nc.sbuf_tensor(name, shape, dt))

        def sem(name):
            return ctx.enter_context(nc.semaphore(name))

        A3 = [P, NT, NE]
        top = sb("r_top", [P, NT])
        ex = sb("r_ex", A3)
        total = sb("r_total", [P, NT])
        probs = sb("r_probs", A3)
        order = sb("r_order", [P, NE])
        value = sb("r_value", A3)
        best = sb("r_best", [P, 2, NT])
        pick = sb("r_pick", [P, NT])
        chosen = sb("r_chosen", [P, 2, NT, NE])
        both = sb("r_both", A3)
        den = sb("r_den", [P, NT])
        before = sb("r_before", [P, P])
        ones = sb("r_ones", [P, P])
        sums = sb("r_sums", [P, 2, NT, NE])
        counts = sb("r_counts", [P, NE])
        counts_i = sb("r_counts_i", [P, NE], I32)
        tiles = sb("r_tiles", [P, NE])
        ends = sb("r_ends", [P, 2, NE])
        slot = sb("r_slot", A3)
        slot_of = sb("r_slot_of", [P, 2, NT])
        tile_no = sb("r_tile_no", [P, NTM])
        expert = sb("r_expert", [P, NTM])
        ps = ctx.enter_context(nc.psum_tensor("r_ps", [P, 2, NT, NE], F32))
        const = sem("r_const")
        step_done = sem("r_step_done")
        max_off = sem("r_max_off")
        exp_done = sem("r_exp_done")
        chosen_done = sem("r_chosen_done")
        counted = sem("r_counted")
        slots_done = sem("r_slots_done")
        block = ctx.enter_context(nc.Block())

        def over_e(ap):
            return ap.rearrange("p (t a) -> p t a", a=1).to_broadcast(A3)

        def over_t(ap):
            return ap.rearrange("p (a e) -> p a e", a=1).to_broadcast(A3)

        @block.gpsimd
        def _(pool):
            pool.memset(ones[:, :], 1.0).then_inc(const, 1)
            pool.wait_ge(const, 1)
            pool.affine_select(out=before[:, :], in_=ones[:, :], compare_op=ALU.is_gt, fill=0.0,
                               base=0, pattern=[[1, P]], channel_multiplier=-1).then_inc(const, 1)
            pool.wait_ge(const, 2)
            pool.iota(order[:, :], [[-1, NE]], base=NE, channel_multiplier=0,
                      allow_small_or_imprecise_dtypes=True).then_inc(const, 1)
            pool.wait_ge(const, 3)
            pool.iota(tile_no[:, :], [[1, NTM]], base=0, channel_multiplier=0,
                      allow_small_or_imprecise_dtypes=True).then_inc(const, 1)

        @block.scalar
        def _(act):
            act.wait_ge(max_off, 1)
            act.activation(ex[:, :, :], ex[:, :, :], ACT.Exp).then_inc(exp_done, 1)

        @block.tensor
        def _(pe):
            pe.wait_ge(const, 2)
            pe.wait_ge(chosen_done, 1)
            flat = both[:, :, :].rearrange("p t e -> p (t e)")
            pe.matmul(ps[:, 0, :, :].rearrange("p t e -> p (t e)"), before[:, :], flat, start=True, stop=True)
            pe.matmul(ps[:, 1, :, :].rearrange("p t e -> p (t e)"), ones[:, :], flat, start=True, stop=True).then_inc(counted, 1)

        @block.vector
        def _(dve):
            n = [0]

            def link(ins):
                n[0] += 1
                ins.then_inc(step_done, 1)
                dve.wait_ge(step_done, n[0])

            dve.wait_ge(const, 4)
            link(dve.tensor_reduce(top[:, :], LG[:, :, :], axis=AX.X, op=ALU.max))
            dve.tensor_tensor(ex[:, :, :], LG[:, :, :], over_e(top[:, :]), ALU.subtract).then_inc(max_off, 1)
            dve.wait_ge(exp_done, 1)
            link(dve.tensor_reduce(total[:, :], ex[:, :, :], axis=AX.X, op=ALU.add))
            link(dve.reciprocal(total[:, :], total[:, :]))
            link(dve.tensor_tensor(probs[:, :, :], ex[:, :, :], over_e(total[:, :]), ALU.mult))
            for c in range(TOP):
                link(dve.tensor_reduce(best[:, c, :], probs[:, :, :], axis=AX.X, op=ALU.max))
                link(dve.tensor_tensor(value[:, :, :], probs[:, :, :], over_e(best[:, c, :]), ALU.is_equal))
                link(dve.tensor_tensor(value[:, :, :], value[:, :, :], over_t(order[:, :]), ALU.mult))
                link(dve.tensor_reduce(pick[:, :], value[:, :, :], axis=AX.X, op=ALU.max))
                link(dve.tensor_tensor(chosen[:, c, :, :], value[:, :, :], over_e(pick[:, :]), ALU.is_equal))
                if c == 0:
                    link(dve.scalar_tensor_tensor(probs[:, :, :], chosen[:, 0, :, :], -2.0, probs[:, :, :], ALU.mult, ALU.add))
            dve.tensor_tensor(both[:, :, :], chosen[:, 0, :, :], chosen[:, 1, :, :], ALU.add).then_inc(chosen_done, 1)
            link(dve.tensor_tensor(den[:, :], best[:, 0, :], best[:, 1, :], ALU.add))
            link(dve.tensor_scalar(den[:, :], den[:, :], TOPK_EPS, None, ALU.add))
            link(dve.reciprocal(den[:, :], den[:, :]))
            for c in range(TOP):
                link(dve.tensor_tensor(W12[:, c, :], best[:, c, :], den[:, :], ALU.mult))
            dve.wait_ge(counted, 1)
            link(dve.tensor_copy(sums[:, 0, :, :], ps[:, 1, :, :]))
            a, shift = 0, 1
            while shift < NT:
                link(dve.tensor_copy(sums[:, 1 - a, 0:shift, :], sums[:, a, 0:shift, :]))
                link(dve.tensor_tensor(sums[:, 1 - a, shift:NT, :], sums[:, a, shift:NT, :], sums[:, a, 0:NT - shift, :], ALU.add))
                a, shift = 1 - a, 2 * shift
            link(dve.tensor_scalar(counts[:, :], sums[:, a, NT - 1, :], float(P - 1), None, ALU.add))
            link(dve.tensor_copy(counts_i[:, :], counts[:, :]))
            link(dve.tensor_scalar(counts_i[:, :], counts_i[:, :], P.bit_length() - 1, None, ALU.logical_shift_right))
            link(dve.tensor_copy(tiles[:, :], counts_i[:, :]))
            link(dve.tensor_copy(ends[:, 0, :], tiles[:, :]))
            c, shift = 0, 1
            while shift < NE:
                link(dve.tensor_copy(ends[:, 1 - c, 0:shift], ends[:, c, 0:shift]))
                link(dve.tensor_tensor(ends[:, 1 - c, shift:NE], ends[:, c, shift:NE], ends[:, c, 0:NE - shift], ALU.add))
                c, shift = 1 - c, 2 * shift
            link(dve.tensor_tensor(tiles[:, :], ends[:, c, :], tiles[:, :], ALU.subtract))
            link(dve.tensor_scalar(tiles[:, :], tiles[:, :], float(P), None, ALU.mult))
            link(dve.tensor_tensor(slot[:, :, :], ps[:, 0, :, :], sums[:, a, :, :], ALU.add))
            link(dve.tensor_tensor(slot[:, :, :], slot[:, :, :], over_t(tiles[:, :]), ALU.add))
            link(dve.tensor_tensor(slot[:, :, :], ps[:, 1, :, :], slot[:, :, :], ALU.subtract))
            for k in range(TOP):
                link(dve.tensor_tensor(value[:, :, :], chosen[:, k, :, :], slot[:, :, :], ALU.mult))
                link(dve.tensor_reduce(slot_of[:, k, :], value[:, :, :], axis=AX.X, op=ALU.add, negate=True))
            link(dve.tensor_copy(POS[:, :, :], slot_of[:, :, :]))
            link(dve.tensor_scalar(expert[:, :], tile_no[:, :], ends[:, c, 0:1], None, ALU.is_ge))
            for x in range(1, NE - 1):
                link(dve.scalar_tensor_tensor(expert[:, :], tile_no[:, :], ends[:, c, x:x + 1], expert[:, :], ALU.is_ge, ALU.add))
            dve.tensor_copy(tile_expert[:, :], expert[:, :]).then_inc(slots_done, 1)


def phase_experts(nc, T):
    base = NT // 2
    ident, WG, WU, WD, tile_expert, xs, ys = (T[k] for k in ("ident", "WG", "WU", "WD", "tile_expert", "xs", "ys"))
    with ExitStack() as ctx:
        def sb(name, shape, dt=F32):
            return ctx.enter_context(nc.sbuf_tensor(name, shape, dt))

        def sem(name):
            return ctx.enter_context(nc.semaphore(name))

        xt = sb("m_x", [P, 2, D])
        xT = sb("m_xT", [P, 2, KD, P])
        SG = sb("m_silu", [P, 2, FI])
        H = sb("m_h", [P, 2, FI])
        HT = sb("m_hT", [P, 2, KF, P])
        yt = sb("m_y", [P, 2, D])
        psG = ctx.enter_context(nc.psum_tensor("m_psG", [P, 2, HALF], F32))
        psU = ctx.enter_context(nc.psum_tensor("m_psU", [P, 2, HALF], F32))
        psT = ctx.enter_context(nc.psum_tensor("m_psT", [P, 1, HALF], F32))
        psH = ctx.enter_context(nc.psum_tensor("m_psH", [P, 1, HALF], F32))
        psY = ctx.enter_context(nc.psum_tensor("m_psY", [P, 2, HALF], F32))
        x_in, t_done, t_in, g_done, u_done, silu_done, h_done, ht_done, ht_in, y_done, y_in = T["tile_sems"]
        y_out = [sem("m_y_out_even"), sem("m_y_out_odd")]
        block = ctx.enter_context(nc.Block())
        xs_t = xs.rearrange("(t p) d -> t p d", p=P)
        ys_t = ys.rearrange("(t p) d -> t p d", p=P)

        @block.sync
        def _(sp):
            def load(i, e):
                if not peeled(i, 2):
                    sp.wait_ge(t_done, at(i, 1, base - 1))
                sp.dma_start(xt[:, e, :], xs_t[i, :, :]).then_inc(x_in[e], 16)

            load(0, 0)
            load(1, 1)
            with sp.Fori(1, NTM // 2) as j:
                load(j * 2, 0)
                load(j * 2 + 1, 1)
            for e in range(2):
                sp.wait_ge(x_in[e], 8 * (base + NTM))

        @block.gpsimd
        def _(pool):
            def store(i, e):
                pool.wait_ge(y_in, at(i, 1, base + 1))
                pool.dma_start(ys_t[i, :, :], yt[:, e, :]).then_inc(y_out[e], 16)

            with pool.Fori(0, NTM // 2) as j:
                store(j * 2, 0)
                store(j * 2 + 1, 1)
            for e in range(2):
                pool.wait_ge(y_out[e], 16 * (NTM // 2))

        @block.tensor
        def _(pe):
            def expert_of(i):
                return pe.value_load(tile_expert[0:1, bass.ds(i, 1)], min_val=0, max_val=NE - 1)

            def step(tile):
                if t := tile(2):
                    i, e = t
                    pe.wait_ge(h_done, at(i, 1, base + 1))
                    if not peeled(i, 1):
                        pe.wait_ge(ht_in, at(i, 1, base))
                    for k in range(KF):
                        mm = pe.transpose(psH[:, 0, k * P:(k + 1) * P], H[:, e, k * P:(k + 1) * P], ident[:, :])
                    mm.then_inc(ht_done, 1)
                if t := tile(1):
                    i, e = t
                    x = expert_of(i)
                    pe.wait_ge(t_in, at(i, 1, base + 1))
                    for w, psum, done, read in ((WG, psG, g_done, silu_done), (WU, psU, u_done, h_done)):
                        if not peeled(i, 2):
                            pe.wait_ge(read, at(i, 1, base - 1))
                        for k in range(KD):
                            mm = pe.matmul(psum[:, e, :], xT[:, e, k, :], w[:, x, k, :], start=(k == 0), stop=(k == KD - 1))
                        mm.then_inc(done, 1)
                if t := tile(0):
                    i, e = t
                    pe.wait_ge(x_in[e], at(i - e, 8, 8 * base + 16))
                    if not peeled(i, 1):
                        pe.wait_ge(t_in, at(i, 1, base))
                    for k in range(KD):
                        mm = pe.transpose(psT[:, 0, k * P:(k + 1) * P], xt[:, e, k * P:(k + 1) * P], ident[:, :])
                    mm.then_inc(t_done, 1)
                if t := tile(2):
                    i, e = t
                    x = expert_of(i)
                    pe.wait_ge(ht_in, at(i, 1, base + 1))
                    if not peeled(i, 2):
                        pe.wait_ge(y_in, at(i, 1, base - 1))
                    for k in range(KF):
                        mm = pe.matmul(psY[:, e, 0:D], HT[:, e, k, :], WD[:, x, k, :], start=(k == 0), stop=(k == KF - 1))
                    mm.then_inc(y_done, 1)

            staggered(pe, NTM, range(3), step)

        @block.vector
        def _(dve):
            def step(tile):
                if t := tile(1):
                    i, e = t
                    dve.wait_ge(silu_done, at(i, 1, base + 1))
                    dve.wait_ge(u_done, at(i, 1, base + 1))
                    if not peeled(i, 2):
                        dve.wait_ge(ht_done, at(i, 1, base - 1))
                    dve.tensor_tensor(H[:, e, :], psU[:, e, :], SG[:, e, :], ALU.mult).then_inc(h_done, 1)
                if t := tile(2):
                    i, e = t
                    dve.wait_ge(y_done, at(i, 1, base + 1))
                    if not peeled(i, 2):
                        dve.wait_ge(y_out[e], at(i - e, 8, 0))
                    dve.tensor_copy(yt[:, e, :], psY[:, e, 0:D]).then_inc(y_in, 1)

            staggered(dve, NTM, range(3), step)

        @block.scalar
        def _(act):
            def step(tile):
                if t := tile(2):
                    i, e = t
                    act.wait_ge(ht_done, at(i, 1, base + 1))
                    if not peeled(i, 2):
                        act.wait_ge(y_done, at(i, 1, base - 1))
                    act.activation(HT[:, e, :, :], psH[:, 0, :].rearrange("p (k n) -> p k n", n=P), ACT.Copy).then_inc(ht_in, 1)
                if t := tile(1):
                    i, e = t
                    act.wait_ge(g_done, at(i, 1, base + 1))
                    if not peeled(i, 2):
                        act.wait_ge(h_done, at(i, 1, base - 1))
                    act.activation(SG[:, e, :], psG[:, e, :], ACT.Silu).then_inc(silu_done, 1)
                if t := tile(0):
                    i, e = t
                    act.wait_ge(t_done, at(i, 1, base + 1))
                    if not peeled(i, 2):
                        act.wait_ge(u_done, at(i, 1, base - 1))
                    act.activation(xT[:, e, :, :], psT[:, 0, 0:D].rearrange("p (k n) -> p k n", n=P), ACT.Copy).then_inc(t_in, 1)

            staggered(act, NTM, range(3), step)


def phase_combine(nc, T):
    X, W12, POS, ys, out = T["X"], T["W12"], T["POS"], T["ys"], T["out"]
    with ExitStack() as ctx:
        def sem(name):
            return ctx.enter_context(nc.semaphore(name))

        NB = 4
        rows = ctx.enter_context(nc.sbuf_tensor("c_rows", [P, TOP, NB, D], F32))
        gathered = [sem(f"c_gathered{n}") for n in range(NB)]
        first = sem("c_first")
        added = sem("c_added")
        stored = sem("c_stored")
        out_t = out.rearrange("b (t p) d -> p (b t) d", p=P)

        def gather(pool):
            for t in range(NT):
                if t >= NB:
                    pool.wait_ge(added, t - NB + 1)
                for c in range(TOP):
                    pool.indirect_dma_start(out=rows[:, c, t % NB, :], out_offset=None, in_=ys,
                                            in_offset=bass.IndirectOffsetOnAxis(ap=POS[:, c, t:t + 1], axis=0),
                                            ).then_inc(gathered[t % NB], 16)

        def add(dve, i, e):
            for d in range(2):
                t = at(i, 2, d)
                n = 2 * e + d
                dve.wait_ge(gathered[n], at(i - e, 16, 32))
                dve.scalar_tensor_tensor(X[:, t, :], rows[:, 0, n, :], W12[:, 0, bass.ds(t, 1)], X[:, t, :],
                                         ALU.mult, ALU.add).then_inc(first, 1)
                dve.wait_ge(first, at(i, 2, d + 1))
                dve.scalar_tensor_tensor(X[:, t, :], rows[:, 1, n, :], W12[:, 1, bass.ds(t, 1)], X[:, t, :],
                                         ALU.mult, ALU.add).then_inc(added, 1)

        def store(sp, j):
            sp.wait_ge(added, at(j, 4, 4))
            sp.dma_start(out_t[:, bass.ds(j * 4, 4), :], X[:, bass.ds(j * 4, 4), :]).then_inc(stored, 16)
            if isinstance(j, int) and j == NT // 4 - 1:
                sp.wait_ge(stored, 16 * (NT // 4))

        shared_half(nc, T, NT // 2, NT // 2 + NTM, gather, add, store)


def phase_scratch(nc, T):
    with ExitStack() as ctx:
        zero = ctx.enter_context(nc.sbuf_tensor("zero_row", [P, 1, D], F32))
        zeroed = ctx.enter_context(nc.semaphore("zeroed"))
        xs_cleared = ctx.enter_context(nc.semaphore("xs_cleared"))
        block = ctx.enter_context(nc.Block())

        @block.vector
        def _(dve):
            dve.memset(zero[:, :, :], 0.0).then_inc(zeroed, 1)

        @block.sync
        def _(sp):
            sp.wait_ge(zeroed, 1)
            sp.dma_start(T["xs"].rearrange("(t p) d -> p t d", p=P),
                         zero[:, :, :].to_broadcast([P, NTM, D])).then_inc(xs_cleared, 16)
            sp.wait_ge(xs_cleared, 16)


def decoder_layer(nc, T):
    with ExitStack() as ctx:
        def dram(name, shape, dt):
            return nc.dram_tensor(name, shape, dt, kind="Internal").ap()

        def sb(stack, name, shape, dt=F32):
            T[name] = stack.enter_context(nc.sbuf_tensor(name, shape, dt))

        T["q_parts"] = dram("q_parts", [NG, 3, HD, GH, S], BF16)
        T["k_parts"] = dram("k_parts", [NG, 3, HD, S], BF16)
        T["m_parts"] = dram("m_parts", [NG, 3, GH * S], BF16)
        T["xs"] = dram("xs", [NSLOT, D], F32)
        T["ys"] = dram("ys", [NSLOT, D], F32)
        sb(ctx, "X", [P, NT, D])
        sb(ctx, "ident", [P, P])
        phase_scratch(nc, T)
        with ExitStack() as attention:
            sb(attention, "VA", [P, NG, TB, VW])
            sb(attention, "OU", [P, NKV, B * S])
            phase_qkv(nc, T)
            phase_attention(nc, T)
            phase_self_out(nc, T)
        with ExitStack() as cross:
            sb(cross, "KX", [P, B, NPR, 2 * SC])
            sb(cross, "VX", [SCP, B, XW])
            phase_context(nc, T)
            phase_cross(nc, T)
        sb(ctx, "XF", [P, NT, D])
        sb(ctx, "LG", [P, NT, NE])
        sb(ctx, "W12", [P, TOP, NT])
        sb(ctx, "POS", [P, TOP, NT], U32)
        sb(ctx, "tile_expert", [P, NTM], I32)
        sb(ctx, "WG", [P, NE, KD, FI])
        sb(ctx, "WU", [P, NE, KD, FI])
        sb(ctx, "WD", [P, NE, KF, D])
        T["tile_sems"] = tile_semaphores(ctx, nc)
        phase_norm(nc, T)
        phase_route(nc, T)
        phase_scatter(nc, T)
        phase_experts(nc, T)
        phase_combine(nc, T)


def kernel(**inputs):
    import numpy as np
    import concourse.bacc as bacc
    from concourse.bass_utils import run_bass_kernel_spmd

    def rows(name):
        return np.ascontiguousarray(inputs[name])

    def per_head(name):
        w = np.asarray(inputs[name])
        return np.ascontiguousarray(w.transpose(1, 0, 2).reshape(w.shape[1], -1))

    def columns(*vectors):
        v = np.concatenate([np.asarray(x) for x in vectors])
        v = np.concatenate([v, np.zeros(-len(v) % P, v.dtype)])
        return np.ascontiguousarray(v.reshape(-1, P).T)

    wo = np.asarray(inputs["L0_attn_Wo"]).reshape(GH, NKV, HD, D).transpose(1, 0, 2, 3)
    arrays = {
        "x": rows("x"), "ctx": rows("ctx_1024"), "mask": rows("mask_BxSxS2_ik1"),
        "Wq": rows("L0_attn_Wq"), "Wk": rows("L0_attn_Wk"), "Wv": rows("L0_attn_Wv"),
        "bqk": columns(inputs["L0_attn_bq"], inputs["L0_attn_bk"]), "bv": rows("L0_attn_bv"),
        "Wo": np.ascontiguousarray(wo.reshape(D, D)), "bo": rows("L0_attn_bo"),
        "Wqx": per_head("L0_xattn_Wq"), "Wkx": per_head("L0_xattn_Wk"), "Wvx": per_head("L0_xattn_Wv"),
        "Wox": rows("L0_xattn_Wo"),
        "sWg": rows("L0_ffn_sWg"), "sWu": rows("L0_ffn_sWu"), "sWd": rows("L0_ffn_sWd"),
        "gateT": np.ascontiguousarray(np.asarray(inputs["L0_ffn_gate_w"]).T),
        "affine": np.ascontiguousarray(np.stack([columns(inputs["L0_ffn_ln_scale"]), columns(inputs["L0_ffn_ln_bias"])], 1)),
        "Wg": rows("L0_ffn_Wg"), "Wu": rows("L0_ffn_Wu"), "Wd": rows("L0_ffn_Wd"),
    }
    nc = bacc.Bacc("TRN2", target_bir_lowering=False, num_devices=1)
    T = {name: nc.dram_tensor(f"in_{name}", a.shape, mybir.dt.from_np(a.dtype), kind="ExternalInput").ap()
         for name, a in arrays.items()}
    T["out"] = nc.dram_tensor("out", (B, S, D), F32, kind="ExternalOutput").ap()
    decoder_layer(nc, T)
    r = run_bass_kernel_spmd(nc, [{f"in_{name}": a for name, a in arrays.items()}], core_ids=[0])
    return r.results[0]["out"]
```

```python
import concourse.bass as bass
from concourse import mybir
from contextlib import ExitStack

F32 = mybir.dt.float32
F32R = mybir.dt.float32r
BF16 = mybir.dt.bfloat16
I32 = mybir.dt.int32
U32 = mybir.dt.uint32
ALU = mybir.AluOpType
ACT = mybir.ActivationFunctionType
AX = mybir.AxisListType

P = 128
D = 256
KD = D // P
B = 4
S = 1024
TB = S // P
NT = B * TB
PRODUCTS = [(0, 0), (0, 1), (1, 0)]
LN_EPS = 1e-5
QUAD = 4
NH = 16
NKV = 4
GH = NH // NKV
HD = D // NH
NG = B * NKV
SCALE = HD ** -0.5
NE = 8
TOP = 2
NTM = (TOP * B * S + NE * (P - 1)) // P
NTM += NTM % 2
NSLOT = NTM * P
VW = 32
Q_PARTS = (3, 2, 1)
KQ = sum(Q_PARTS) * HD
KM = KQ + 3
HALF = 512
SLOTS = 4
TURN_AT = 4
LEAD = 10
NU = GH * TB


def at(i, per, plus):
    return i * per + plus


def peeled(i, below):
    return isinstance(i, int) and i < below


def staggered(eng, n, lags, step):
    depth = max(lags) + 1
    low = depth + 1 + (depth + 1) % 2
    for s in range(low):
        step(lambda lag, s=s: (s - lag, (s - lag) % 2) if 0 <= s - lag < n else None)
    if low < n:
        with eng.Fori(low // 2, n // 2) as j:
            for e in range(2):
                step(lambda lag, j=j, e=e: (j * 2 + (e - lag), (e - lag) % 2))
    for s in range(n, n + depth - 1):
        step(lambda lag, s=s: (s - lag, (s - lag) % 2) if 0 <= s - lag < n else None)


def load_group(eng, T, i, e):
    g, b = i // B, i % B
    row = 0
    for kp, nq in enumerate(Q_PARTS):
        eng.dma_start(T["KS"][row:row + nq * HD, i % SLOTS, :],
                      T["k_parts"][b, kp:kp + 1, g, :, :].to_broadcast([nq, HD, S])).then_inc(T["loaded"][e], 16)
        for a in range(nq):
            eng.dma_start(T["QS"][row:row + HD, i % SLOTS, :, :],
                          T["q_parts"][b, a, g, :, :, :].rearrange("h d n -> d h n")).then_inc(T["loaded"][e], 16)
            row += HD


def phase_qkv(nc, T):
    X, ident, VA, q_parts, k_parts = T["X"], T["ident"], T["VA"], T["q_parts"], T["k_parts"]
    with ExitStack() as ctx:
        def sb(name, shape, dt=F32):
            return ctx.enter_context(nc.sbuf_tensor(name, shape, dt))

        def sem(name):
            return ctx.enter_context(nc.semaphore(name))

        wq = sb("wq_sb", [P, KD, D])
        wk = sb("wk_sb", [P, KD, NKV * HD])
        wv = sb("wv_sb", [P, KD, NKV * HD])
        bqk = sb("bqk_sb", [P, 3])
        bv = sb("bv_sb", [P, NKV * HD])
        stats = sb("stats", [P, 2, QUAD, 6])
        mean_var = sb("mean_var", [P, 2, QUAD, 2])
        var_eps = sb("var_eps", [P, 2, QUAD])
        neg_half = sb("neg_half", [P, QUAD])
        rstd = sb("rstd", [P, 2, QUAD])
        xn = sb("xn", [P, 2, QUAD, D])
        xnT = sb("xnT", [P, 2, KD, HALF])
        part = sb("part", [P, 2, 3, 3, HALF], BF16)
        rest = sb("rest", [P, 2, 3, HALF])
        psT = ctx.enter_context(nc.psum_tensor("psT", [P, 2, HALF], F32))
        psQ = ctx.enter_context(nc.psum_tensor("psQ", [P, 3, HALF], F32))
        psV = ctx.enter_context(nc.psum_tensor("psV", [P, 2, HALF], F32))

        NQ = NT // QUAD
        XLOADS = 4
        x_loaded = [sem(f"x_loaded{n}") for n in range(XLOADS)]
        w_loaded = sem("w_loaded")
        consts = sem("consts")
        stats_done = sem("stats_done")
        mv_done = sem("mv_done")
        veps_done = sem("veps_done")
        rstd_done = sem("rstd_done")
        xn_done = sem("xn_done")
        tr_done = sem("tr_done")
        xnT_done = sem("xnT_done")
        proj_done = sem("proj_done")
        p1_done = sem("p1_done")
        rest_done = sem("rest_done")
        p2_done = sem("p2_done")
        p3_done = sem("p3_done")
        v_done = sem("v_done")
        va_done = sem("va_done")
        stored = [sem("stored_even"), sem("stored_odd")]
        MS = [(0, P), (1, P), (2, NKV * HD)]
        NM = len(MS)
        NSTORE = 16 * NM
        block = ctx.enter_context(nc.Block())

        @block.sync
        def _(sp):
            x = T["x"].rearrange("b (t p) d -> p (b t) d", p=P)
            for n in range(XLOADS):
                tiles = slice(n * QUAD, (n + 1) * QUAD if n < XLOADS - 1 else NT)
                sp.dma_start(X[:, tiles, :], x[:, tiles, :]).then_inc(x_loaded[n], 16)
                if n < 2:
                    sp.wait_ge(x_loaded[n], 16)

            def step(quad):
                if t := quad(2):
                    i, e = t
                    b = i // (S // HALF)
                    tokens = bass.ds(i % (S // HALF) * HALF, HALF)
                    if isinstance(i, int) and i >= NQ - 2:
                        sp.wait_ge(stored[e], NSTORE * (NQ // 2 - 2))
                        load_group(sp, T, i - (NQ - 2), e)
                    for m, rows in MS:
                        sp.wait_ge(p3_done, at(i, NM, m + 1))
                        if m < 2:
                            to = q_parts.rearrange("b j g h d n -> b j (g h d) n")[b, :, m * P:(m + 1) * P, tokens]
                        else:
                            to = k_parts.rearrange("b j g d n -> b j (g d) n")[b, :, :, tokens]
                        sp.dma_start(to.rearrange("j r n -> r j n"), part[0:rows, e, :, m, :]).then_inc(stored[e], 16)

            staggered(sp, NQ, range(3), step)
            for e in range(2):
                sp.wait_ge(stored[e], NSTORE * NQ // 2)

        @block.gpsimd
        def _(pool):
            pool.memset(neg_half[:, :], -0.5).then_inc(consts, 1)
            pool.memset(ident[:, :], 0.0).then_inc(consts, 1)
            pool.wait_ge(consts, 2)
            pool.affine_select(out=ident[:, :], in_=ident[:, :], compare_op=ALU.not_equal, fill=1.0,
                               base=0, pattern=[[-1, P]], channel_multiplier=1).then_inc(consts, 1)
            pool.memset(VA[:, :, :, :], 0.0).then_inc(consts, 1)
            pool.wait_ge(consts, 4)
            pool.memset(VA[:, :, :, HD:HD + 1], 1.0).then_inc(consts, 1)
            pool.wait_ge(consts, 5)

            def step(quad):
                if t := quad(0):
                    i, e = t
                    pool.wait_ge(veps_done, at(i, 1, 1))
                    pool.tensor_tensor(rstd[:, e, :], var_eps[:, e, :], neg_half[:, :], ALU.pow).then_inc(rstd_done, 1)
                    pool.wait_ge(rstd_done, at(i, 1, 1))
                if t := quad(2):
                    i, e = t
                    for m, rows in MS:
                        pool.wait_ge(p2_done, at(i, NM, m + 1))
                        pool.tensor_tensor(part[0:rows, e, 2, m, :], rest[0:rows, e, m, :],
                                           part[0:rows, e, 1, m, :], ALU.subtract).then_inc(p3_done, 1)
                        pool.wait_ge(p3_done, at(i, NM, m + 1))

            staggered(pool, NQ, range(3), step)

        @block.vector
        def _(dve):
            def step(quad):
                if t := quad(1):
                    i, e = t
                    dve.wait_ge(rstd_done, at(i, 1, 1))
                    if not peeled(i, 2):
                        dve.wait_ge(tr_done, at(i, QUAD, -QUAD))
                    for q in range(QUAD):
                        dve.tensor_scalar(xn[:, e, q, :], X[:, i * QUAD + q, :], mean_var[:, e, q, 0:1], rstd[:, e, q:q + 1],
                                          ALU.subtract, ALU.mult).then_inc(xn_done, 1)
                if t := quad(0):
                    i, e = t
                    if isinstance(i, int) and i < XLOADS:
                        dve.wait_ge(x_loaded[i], 16)
                    for q in range(QUAD):
                        dve.bn_stats(stats[:, e, q, :], X[:, i * QUAD + q, :]).then_inc(stats_done, 1)
                if t := quad(2):
                    i, e = t
                    if isinstance(i, int) and i == 0:
                        dve.wait_ge(w_loaded, 16 * 5)
                        dve.wait_ge(consts, 5)
                    for m, rows in MS:
                        dve.wait_ge(p1_done, at(i, NM, m + 1))
                        if not peeled(i, 2):
                            dve.wait_ge(p3_done, at(i, NM, m + 1 - 2 * NM))
                        dve.scalar_tensor_tensor(rest[0:rows, e, m, :], psQ[0:rows, m, :], bqk[0:rows, m:m + 1],
                                                 part[0:rows, e, 0, m, :], ALU.add, ALU.subtract).then_inc(rest_done, 1)
                if t := quad(0):
                    i, e = t
                    if not peeled(i, 2):
                        dve.wait_ge(xn_done, at(i, QUAD, -QUAD))
                        dve.sem_inc(T["waited_dve"], 1)
                    dve.wait_ge(stats_done, at(i, QUAD, QUAD))
                    dve.sem_inc(T["waited_dve"], 1)
                    for q in range(QUAD):
                        dve.bn_aggr(mean_var[:, e, q, :], stats[:, e, q, :]).then_inc(mv_done, 1)
                    dve.wait_ge(mv_done, at(i, QUAD, QUAD))
                    dve.tensor_scalar(var_eps[:, e, :], mean_var[:, e, :, 1], LN_EPS, None, ALU.add).then_inc(veps_done, 1)
                if t := quad(2):
                    i, e = t
                    dve.wait_ge(v_done, at(i, 1, 1))
                    for g in range(NKV):
                        dve.tensor_tensor(VA[:, i // (S // HALF) + g * B, bass.ds(i % (S // HALF) * QUAD, QUAD), 0:HD],
                                          psV[:, e, 0:QUAD * NKV * HD].rearrange("p (t g d) -> p g t d", t=QUAD, g=NKV)[:, g, :, :],
                                          bv[:, g * HD:(g + 1) * HD].rearrange("p (a d) -> p a d", a=1).to_broadcast([P, QUAD, HD]),
                                          ALU.add).then_inc(va_done, 1)

            staggered(dve, NQ, range(3), step)

        @block.scalar
        def _(act):
            act.dma_start(wq[:, :, :], T["Wq"].rearrange("(k p) n -> p k n", p=P)).then_inc(w_loaded, 16)
            act.dma_start(wk[:, :, :], T["Wk"].rearrange("(k p) n -> p k n", p=P)).then_inc(w_loaded, 16)
            act.dma_start(wv[:, :, :], T["Wv"].rearrange("(k p) n -> p k n", p=P)).then_inc(w_loaded, 16)
            act.dma_start(bqk[:, :], T["bqk"]).then_inc(w_loaded, 16)
            act.dma_start(bv[:, :], T["bv"].rearrange("(a n) -> a n", a=1).to_broadcast([P, NKV * HD])).then_inc(w_loaded, 16)
            act.wait_ge(w_loaded, 16 * 5)

            def step(quad):
                def turned(q):
                    if t := quad(1):
                        i, e = t
                        act.wait_ge(tr_done, at(i, QUAD, q + 1))
                        if q == 0 and not peeled(i, 2):
                            act.wait_ge(v_done, at(i, 1, -1))
                        act.activation(xnT[:, e, :, q * P:(q + 1) * P],
                                       psT[:, q % 2, 0:KD * P].rearrange("p (k n) -> p k n", k=KD), ACT.Copy).then_inc(xnT_done, 1)

                def part1(m, rows):
                    if t := quad(2):
                        i, e = t
                        act.wait_ge(proj_done, at(i, NM, m + 1))
                        if m == 0 and not peeled(i, 2):
                            act.wait_ge(stored[e], (i - e) // 2 * NSTORE)
                        act.activation(part[0:rows, e, 0, m, :], psQ[0:rows, m, :], ACT.Identity,
                                       bias=bqk[0:rows, m:m + 1]).then_inc(p1_done, 1)

                turned(0)
                turned(1)
                part1(*MS[0])
                turned(2)
                turned(3)
                part1(*MS[1])
                part1(*MS[2])
                if t := quad(2):
                    i, e = t
                    for m, rows in MS:
                        act.wait_ge(rest_done, at(i, NM, m + 1))
                        act.activation(part[0:rows, e, 1, m, :], rest[0:rows, e, m, :], ACT.Copy).then_inc(p2_done, 1)

            staggered(act, NQ, range(3), step)

        @block.tensor
        def _(pe):
            def step(quad):
                def turn(q):
                    if t := quad(1):
                        i, e = t
                        pe.wait_ge(xn_done, at(i, QUAD, q + 1))
                        if not peeled(i, 1) or q >= 2:
                            pe.wait_ge(xnT_done, at(i, QUAD, q - 1))
                        for k in range(KD):
                            tr = pe.transpose(psT[:, q % 2, k * P:(k + 1) * P], xn[:, e, q, k * P:(k + 1) * P], ident[:, :])
                        tr.then_inc(tr_done, 1)

                def project(m, rows):
                    if t := quad(2):
                        i, e = t
                        if m == 0:
                            pe.wait_ge(xnT_done, at(i, QUAD, QUAD))
                        if not peeled(i, 1):
                            pe.wait_ge(rest_done, at(i, NM, m + 1 - NM))
                        for k in range(KD):
                            w = wk[:, k, :] if m == 2 else wq[:, k, m * P:(m + 1) * P]
                            mm = pe.matmul(psQ[0:rows, m, :], w, xnT[:, e, k, :], start=(k == 0), stop=(k == KD - 1))
                        mm.then_inc(proj_done, 1)

                project(*MS[0])
                turn(0)
                turn(1)
                project(*MS[1])
                turn(2)
                turn(3)
                project(*MS[2])
                if t := quad(2):
                    i, e = t
                    if not peeled(i, 2):
                        pe.wait_ge(va_done, at(i, NKV, -NKV))
                    for q in range(QUAD):
                        for k in range(KD):
                            mm = pe.matmul(psV[:, e, q * NKV * HD:(q + 1) * NKV * HD], xnT[:, e, k, q * P:(q + 1) * P], wv[:, k, :],
                                           start=(k == 0), stop=(k == KD - 1))
                    mm.then_inc(v_done, 1)

            pe.wait_ge(w_loaded, 16 * 5)
            pe.wait_ge(consts, 5)
            staggered(pe, NQ, range(3), step)


def phase_attention(nc, T):
    VA, OU, QS, KS, m_parts = T["VA"], T["OU"], T["QS"], T["KS"], T["m_parts"]
    xs, loaded = T["xs"], T["loaded"]
    with ExitStack() as ctx:
        def sb(name, shape, dt=F32):
            return ctx.enter_context(nc.sbuf_tensor(name, shape, dt))

        def sem(name):
            return ctx.enter_context(nc.semaphore(name))

        VG = sb("VG", [P, 2, TB, VW])
        PT = sb("PT", [P, 2, GH, S])
        half_max = sb("half_max", [P, NU, 2])
        neg_max = sb("neg_max", [P, NU])
        max_rest = sb("max_rest", [P, NU])
        max_parts = sb("max_parts", [P, 3, NU], BF16)
        max_parts_t = sb("max_parts_t", [P, 3, NU], BF16)
        zero = sb("zero_row", [P, 1, D])
        psA = ctx.enter_context(nc.psum_tensor("psA", [P, 2, HALF], F32))
        psB = ctx.enter_context(nc.psum_tensor("psB", [P, 2, 2, HALF], F32))
        psO = ctx.enter_context(nc.psum_tensor("psO", [P, 2, HALF], F32))

        ones_set = sem("ones_set")
        xs_cleared = sem("xs_cleared")
        v_copied = sem("v_copied")
        a_done = sem("a_done")
        max_taken = sem("max_taken")
        neg_done = sem("neg_done")
        m1_done = sem("m1_done")
        mr_done = sem("mr_done")
        m2_done = sem("m2_done")
        m3_done = sem("m3_done")
        mt_done = sem("mt_done")
        m_stored = sem("m_stored")
        rows_set = [sem("rows_set_even"), sem("rows_set_odd")]
        b_done = sem("b_done")
        exp_done = sem("exp_done")
        pv_done = sem("pv_done")
        out_copied = sem("out_copied")
        NROWS = 16
        NLOAD = 16 * (len(Q_PARTS) + sum(Q_PARTS))
        block = ctx.enter_context(nc.Block())

        def count(i, per, plus):
            return i * per + plus

        @block.sync
        def _(sp):
            def load(i, e):
                if not (isinstance(i, int) and i < SLOTS):
                    sp.wait_ge(pv_done, count(i, TB, -TB * (SLOTS - 1)))
                load_group(sp, T, i, e)

            def rows(i, e):
                sp.wait_ge(mt_done, count(i, 1, 1))
                for part in range(3):
                    sp.dma_start(m_parts[i, part, :].rearrange("(u k n) -> k u n", k=4, n=32),
                                 max_parts_t[:, part, :]).then_inc(m_stored, 16)
                sp.wait_ge(m_stored, count(i, 48, 48))
                sp.dma_start(QS[KQ:KM, i % SLOTS, :, :].rearrange("a h n -> a (h n)"), m_parts[i, :, :]).then_inc(rows_set[e], 16)

            for i in range(2):
                rows(i, i)
                load(i + 2, i)
            with sp.Fori(1, NG // 2 - 1) as j:
                for e in range(2):
                    rows(j * 2 + e, e)
                    load(j * 2 + (e + 2), e)
            for i in range(NG - 2, NG):
                rows(i, i % 2)
            for e in range(2):
                sp.wait_ge(rows_set[e], NROWS * (NG // 2))

        @block.gpsimd
        def _(pool):
            pool.memset(KS[KQ:P, :, :], 1.0).then_inc(ones_set, 1)
            pool.wait_ge(ones_set, 1)
            pool.memset(zero[:, :, :], 0.0).then_inc(ones_set, 1)
            pool.wait_ge(ones_set, 2)
            pool.dma_start(xs.rearrange("(t p) d -> p t d", p=P), zero[:, :, :].to_broadcast([P, NTM, D])).then_inc(xs_cleared, 16)

            def values(i, e):
                if not (isinstance(i, int) and i < 2):
                    pool.wait_ge(pv_done, count(i, TB, -TB))
                    pool.sem_inc(T["waited_pool"], 1)
                pool.tensor_copy(VG[:, e, :, :], VA[:, i, :, :]).then_inc(v_copied, 1)

            def maxima(i):
                pool.wait_ge(v_copied, count(i, 1, 1))
                pool.wait_ge(neg_done, count(i, 1, 1))
                if not (isinstance(i, int) and i < 1):
                    pool.wait_ge(mt_done, count(i, 1, 0))
                    pool.sem_inc(T["waited_pool"], 1)
                pool.tensor_copy(max_parts[:, 0, :], neg_max[:, :]).then_inc(m1_done, 1)
                pool.wait_ge(m1_done, count(i, 1, 1))
                pool.tensor_tensor(max_rest[:, :], neg_max[:, :], max_parts[:, 0, :], ALU.subtract).then_inc(mr_done, 1)
                pool.wait_ge(mr_done, count(i, 1, 1))
                pool.sem_inc(T["waited_pool"], 1)
                pool.tensor_copy(max_parts[:, 1, :], max_rest[:, :]).then_inc(m2_done, 1)
                pool.wait_ge(m2_done, count(i, 1, 1))
                pool.tensor_tensor(max_parts[:, 2, :], max_rest[:, :], max_parts[:, 1, :], ALU.subtract).then_inc(m3_done, 1)
                pool.wait_ge(m3_done, count(i, 1, 1))

            for i in range(2):
                values(i, i)
                maxima(i)
            with pool.Fori(1, NG // 2) as j:
                for e in range(2):
                    values(j * 2 + e, e)
                    maxima(j * 2 + e)
            pool.wait_ge(xs_cleared, 16)

        @block.vector
        def _(dve):
            def turn_parts(i):
                dve.wait_ge(m3_done, count(i, 1, 1))
                if not (isinstance(i, int) and i < 1):
                    dve.wait_ge(m_stored, count(i, 48, 0))
                dve.transpose(max_parts_t[:, :, :], max_parts[:, :, :]).then_inc(mt_done, 1)

            def maxima(i):
                if not (isinstance(i, int) and i < 1):
                    dve.wait_ge(neg_done, count(i, 1, 0))
                for u in range(NU):
                    for n in range(2):
                        dve.wait_ge(a_done, count(i, 2 * NU, 2 * u + n + 1))
                        dve.tensor_reduce(half_max[:, u, n:n + 1], psA[:, n, :], axis=AX.X, op=ALU.max).then_inc(max_taken, 1)
                    if u == TURN_AT and not (isinstance(i, int) and i < 1):
                        turn_parts(count(i, 1, -1))
                dve.wait_ge(max_taken, count(i, 2 * NU, 2 * NU))
                if not (isinstance(i, int) and i < 1):
                    dve.wait_ge(m3_done, count(i, 1, 0))
                dve.tensor_reduce(neg_max[:, :], half_max[:, :, :], axis=AX.X, op=ALU.max, negate=True).then_inc(neg_done, 1)

            maxima(0)
            maxima(1)
            with dve.Fori(1, NG // 2) as j:
                for e in range(2):
                    maxima(j * 2 + e)
            turn_parts(NG - 1)

        @block.scalar
        def _(act):
            def take_out(i):
                act.wait_ge(pv_done, count(i, TB, TB))
                act.activation(OU[:, :, :].rearrange("p g (b n) -> p (g b) n", b=B)[:, i, :], psO[:, :, :].rearrange("p a n -> p (a n)"), ACT.Copy).then_inc(out_copied, 1)

            def exps(i):
                for c in range(TB):
                    for h in range(GH):
                        u = c * GH + h
                        act.wait_ge(b_done, count(i, NU, u + 1))
                        if c >= 2 or not (isinstance(i, int) and i < 1):
                            if h == 0:
                                act.wait_ge(pv_done, count(i, TB, c - 1))
                        act.activation(PT[:, c % 2, h, :], psB[:, u % 2, :, :].rearrange("p a n -> p (a n)"), ACT.Exp,
                                       scale=SCALE).then_inc(exp_done, 1)
                    if c == 0 and not (isinstance(i, int) and i < 1):
                        take_out(count(i, 1, -1))

            exps(0)
            exps(1)
            with act.Fori(1, NG // 2) as j:
                for e in range(2):
                    exps(j * 2 + e)
            take_out(NG - 1)

        @block.tensor
        def _(pe):
            def pass_a(i, u, n):
                h, t = divmod(u, TB)
                if not (isinstance(i, int) and i == 0 and u == 0):
                    pe.wait_ge(max_taken, count(i, 2 * NU, 2 * u + n - 1))
                pe.matmul(psA[:, n, :], QS[0:KQ, i % SLOTS, h, t * P:(t + 1) * P], KS[0:KQ, i % SLOTS, n * HALF:(n + 1) * HALF],
                          start=True, stop=True).then_inc(a_done, 1)

            def pass_b(i, u):
                c, h = divmod(u, GH)
                if not (isinstance(i, int) and i == 0 and u < 2):
                    pe.wait_ge(exp_done, count(i, NU, u - 1))
                for n in range(2):
                    mm = pe.matmul(psB[:, u % 2, n, :], KS[0:KM, i % SLOTS, c * P:(c + 1) * P],
                                   QS[0:KM, i % SLOTS, h, n * HALF:(n + 1) * HALF], start=True, stop=True)
                mm.then_inc(b_done, 1)

            def times_values(i, e, c, q):
                cols = slice(q % 2 * HALF // 2, (q % 2 + 1) * HALF // 2)
                if q == 0:
                    pe.wait_ge(exp_done, count(i, NU, (c + 1) * GH))
                if c == 0 and q == 0:
                    pe.wait_ge(v_copied, count(i, 1, 1))
                    if not (isinstance(i, int) and i < 1):
                        pe.wait_ge(out_copied, count(i, 1, 0))
                for h in range(GH):
                    mm = pe.matmul(psO[h * VW:(h + 1) * VW, q // 2, cols], VG[:, e, c, :], PT[:, c % 2, h, q * S // 4:(q + 1) * S // 4],
                                   start=(c == 0 and q % 2 == 0), stop=(c == TB - 1 and q % 2 == 1))
                if q == 3:
                    mm.then_inc(pv_done, 1)

            def group(i, e):
                pe.wait_ge(rows_set[e], count(i - e, NROWS // 2, NROWS))
                for u in range(NU):
                    ahead = 1 if u < NU - LEAD else 2
                    has_a = not isinstance(i, int) or i + ahead < NG
                    if u == NU - LEAD and has_a:
                        pe.wait_ge(loaded[e], count(i - e, NLOAD // 2, 2 * NLOAD))
                    if has_a:
                        pass_a(i + ahead, (u + LEAD) % NU, 0)
                    pass_b(i, u)
                    if has_a:
                        pass_a(i + ahead, (u + LEAD) % NU, 1)
                    c, q = divmod(u - GH - 1, 4)
                    if c >= 0:
                        times_values(i, e, c, q)
                    elif not (isinstance(i, int) and i < 1):
                        times_values(i - 1, 1 - e, c + TB, q)

            pe.wait_ge(loaded[0], NLOAD)
            for u in range(NU):
                for n in range(2):
                    pass_a(0, u, n)
            pe.wait_ge(loaded[1], NLOAD)
            for u in range(LEAD):
                for n in range(2):
                    pass_a(1, u, n)
            pe.wait_ge(ones_set, 1)
            group(0, 0)
            group(1, 1)
            with pe.Fori(1, NG // 2 - 1) as j:
                for e in range(2):
                    group(j * 2 + e, e)
            group(NG - 2, 0)
            group(NG - 1, 1)
            for u in range(NU, NU + GH + 1):
                times_values(NG - 1, 1, *divmod(u - GH - 1, 4))


XH = 16
XD = 64
SC = 77
XW = XH * XD
NPR = XH // 2
NPK = -(-XH * SC // P)
SBANKS = [(0, 6), (6, 6), (12, 4)]
XSCALE = XD ** -0.5
NEG = -1e10
NEG_RAW = NEG / XSCALE


def phase_self_out(nc, T):
    X, OU, ident = T["X"], T["OU"], T["ident"]
    with ExitStack() as ctx:
        def sb(name, shape, dt=F32):
            return ctx.enter_context(nc.sbuf_tensor(name, shape, dt))

        def sem(name):
            return ctx.enter_context(nc.semaphore(name))

        wo = sb("wo_sb", [P, KD, D])
        bo = sb("bo_sb", [P, D])
        OT = sb("OT", [P, 2, NKV, P])
        recip = sb("recip", [P, 2, NH])
        ON = sb("ON", [P, 2, D])
        ONT = sb("ONT", [P, 2, KD, P])
        psR = ctx.enter_context(nc.psum_tensor("psR", [P, 2, HALF], F32))
        psU = ctx.enter_context(nc.psum_tensor("psU", [P, 2, HALF], F32))
        psY = ctx.enter_context(nc.psum_tensor("psY", [P, 2, HALF], F32))
        w_in = sem("so_w_in")
        bias_added = sem("so_bias_added")
        sums_in = [sem("so_sums_in_even"), sem("so_sums_in_odd")]
        rows_done = sem("so_rows_done")
        recip_done = sem("so_recip_done")
        norm_done = sem("so_norm_done")
        turned = sem("so_turned")
        turned_in = sem("so_turned_in")
        y_done = sem("so_y_done")
        x_added = sem("so_x_added")
        block = ctx.enter_context(nc.Block())

        @block.sync
        def _(sp):
            sp.dma_start(wo[:, :, :], T["Wo"].rearrange("(k p) n -> p k n", p=P)).then_inc(w_in, 16)
            sp.dma_start(bo[:, :], T["bo"].rearrange("(a n) -> a n", a=1).to_broadcast([P, D])).then_inc(w_in, 16)

            def load(i, e):
                if not peeled(i, 2):
                    sp.wait_ge(rows_done, at(i, 1, -1))
                sp.dma_start(OT[:, e, :, :], OU[:, :, bass.ds(i * P, P)]).then_inc(sums_in[e], 16)

            load(0, 0)
            load(1, 1)
            with sp.Fori(1, NT // 2) as j:
                load(j * 2, 0)
                load(j * 2 + 1, 1)
            for e in range(2):
                sp.wait_ge(sums_in[e], 16 * (NT // 2))

        @block.gpsimd
        def _(pool):
            pool.wait_ge(w_in, 32)
            with pool.Fori(0, NT) as i:
                pool.tensor_tensor(X[:, i, :], X[:, i, :], bo[:, :], ALU.add).then_inc(bias_added, 1)
                pool.wait_ge(bias_added, at(i, 1, 1))

        @block.tensor
        def _(pe):
            pe.wait_ge(w_in, 32)

            def step(tile):
                if t := tile(2):
                    i, e = t
                    pe.wait_ge(turned_in, at(i, 1, 1))
                    if not peeled(i, 2):
                        pe.wait_ge(x_added, at(i, 1, -1))
                    for k in range(KD):
                        mm = pe.matmul(psY[:, e, 0:D], ONT[:, e, k, :], wo[:, k, :], start=(k == 0), stop=(k == KD - 1))
                    mm.then_inc(y_done, 1)
                if t := tile(1):
                    i, e = t
                    pe.wait_ge(norm_done, at(i, 1, 1))
                    if not peeled(i, 2):
                        pe.wait_ge(turned_in, at(i, 1, -1))
                    for k in range(KD):
                        mm = pe.transpose(psU[:, e, k * P:(k + 1) * P], ON[:, e, k * P:(k + 1) * P], ident[:, :])
                    mm.then_inc(turned, 1)
                if t := tile(0):
                    i, e = t
                    pe.wait_ge(sums_in[e], at(i - e, 8, 16))
                    if not peeled(i, 2):
                        pe.wait_ge(norm_done, at(i, 1, -1))
                    for g in range(NKV):
                        mm = pe.transpose(psR[:, e, g * P:(g + 1) * P], OT[:, e, g, :], ident[:, :])
                    mm.then_inc(rows_done, 1)

            staggered(pe, NT, (0, 1, 2), step)

        @block.vector
        def _(dve):
            def step(tile):
                if t := tile(0):
                    i, e = t
                    rows = psR[:, e, :].rearrange("p (h r) -> p h r", r=VW)
                    dve.wait_ge(rows_done, at(i, 1, 1))
                    if not peeled(i, 2):
                        dve.wait_ge(norm_done, at(i, 1, -1))
                        dve.wait_ge(turned, at(i, 1, -1))
                    dve.reciprocal(recip[:, e, :], rows[:, :, HD]).then_inc(recip_done, 1)
                    dve.wait_ge(recip_done, at(i, 1, 1))
                    dve.tensor_tensor(ON[:, e, :].rearrange("p (h d) -> p h d", d=HD), rows[:, :, 0:HD],
                                      recip[:, e, :].rearrange("p (h a) -> p h a", a=1).to_broadcast([P, NH, HD]),
                                      ALU.mult).then_inc(norm_done, 1)
                if t := tile(2):
                    i, e = t
                    dve.wait_ge(y_done, at(i, 1, 1))
                    dve.wait_ge(bias_added, at(i, 1, 1))
                    dve.tensor_tensor(X[:, i, :], psY[:, e, 0:D], X[:, i, :], ALU.add).then_inc(x_added, 1)

            staggered(dve, NT, (0, 1, 2), step)

        @block.scalar
        def _(act):
            def copy(i, e):
                act.wait_ge(turned, at(i, 1, 1))
                if not peeled(i, 2):
                    act.wait_ge(y_done, at(i, 1, -1))
                act.activation(ONT[:, e, :, :], psU[:, e, 0:D].rearrange("p (k n) -> p k n", k=KD), ACT.Copy).then_inc(turned_in, 1)

            copy(0, 0)
            copy(1, 1)
            with act.Fori(1, NT // 2) as j:
                copy(j * 2, 0)
                copy(j * 2 + 1, 1)


def phase_context(nc, T):
    ident, MX, VO, mx_kept, mx_in = T["ident"], T["MX"], T["VO"], T["mx_kept"], T["mx_in"]
    ORDER = [2, 3, 0, 1]
    with ExitStack() as ctx:
        def sb(name, shape, dt=F32):
            return ctx.enter_context(nc.sbuf_tensor(name, shape, dt))

        def sem(name):
            return ctx.enter_context(nc.semaphore(name))

        wk = sb("wkx_sb", [P, KD, XW])
        wv = sb("wvx_sb", [P, KD, XW])
        wqT = sb("wqxT_sb", [P, NPR, D])
        wo = sb("wox_sb", [P, NPR, D])
        cx = sb("cx", [SC, 2, D])
        cxT = sb("cxT", [P, KD, SC])
        KX = sb("cx_keys", [P, 2, NPR, 2 * SC])
        VZ = sb("cx_values", [P, NPR, P + 2 * SC + P])
        psT = ctx.enter_context(nc.psum_tensor("psTc", [P, 1, HALF], F32))
        psK = ctx.enter_context(nc.psum_tensor("psKc", [P, 2, HALF], F32))
        psV = ctx.enter_context(nc.psum_tensor("psVc", [P, 2, HALF], F32))
        psM = ctx.enter_context(nc.psum_tensor("psMc", [P, 3, HALF], F32))
        wk_in, wv_in, wq_in, wo_in = (sem(f"cx_w{n}_in") for n in "kvqo")
        cleared = sem("cx_cleared")
        c_in = [sem("cx_in_even"), sem("cx_in_odd")]
        turned = sem("cx_turned")
        turned_in = sem("cx_turned_in")
        k_done, k_in = sem("cx_k_done"), sem("cx_k_in")
        v_done, v_in = sem("cx_v_done"), sem("cx_v_in")
        prod_done = sem("cx_prod_done")
        high_in = sem("cx_high_in")
        prod_in = [sem("cx_prod_in_act"), sem("cx_prod_in_dve")]
        block = ctx.enter_context(nc.Block())
        NMX = KD * len(SBANKS)
        NPROD = NMX + NPK // 2

        def scores_unit(b, v):
            k, n = divmod(v, len(SBANKS))
            first, heads = SBANKS[n]
            cols = slice(first * SC, (first + heads) * SC)
            return MX[0][:, b % 2, k, cols], MX[1][:, b % 2, k, cols], psM[:, (NPROD * b + v) % 3, 0:heads * SC]

        def values_unit(b, v):
            c = 2 * (v - NMX)
            return VO[:, ORDER[b], c:c + 2, :], psM[:, (NPROD * b + v) % 3, :].rearrange("p (c n) -> p c n", n=D)

        def by_dve(v):
            return v < NMX or v % 2 == 1

        def read_out(u):
            engine = by_dve(u % NPROD)
            return prod_in[engine], sum(by_dve(w % NPROD) == engine for w in range(u + 1))

        @block.sync
        def _(sp):
            for b in range(B):
                if b >= 2:
                    sp.wait_ge(turned, b - 1)
                sp.dma_start(cx[:, b % 2, :], T["ctx"][ORDER[b], :, :]).then_inc(c_in[b % 2], 16)
                if b == 0:
                    sp.dma_start(wk[:, :, :], T["Wkx"].rearrange("(k p) n -> p k n", p=P)).then_inc(wk_in, 16)
                    sp.dma_start(wv[:, :, :], T["Wvx"].rearrange("(k p) n -> p k n", p=P)).then_inc(wv_in, 16)
                    sp.dma_start(wqT[:, :, :], T["WqxT"].rearrange("(k p) n -> p k n", p=P)).then_inc(wq_in, 16)
                    sp.dma_start(wo[:, :, :], T["Wox"].rearrange("(k p) n -> p k n", p=P)).then_inc(wo_in, 16)
            for b in range(2):
                semaphore, value = read_out(NPROD * b + NMX - 1)
                sp.wait_ge(semaphore, value)
                for part in range(2):
                    sp.dma_start(mx_kept[ORDER[b], part, :, :, :], MX[part][:, b, :, :].bitcast(F32)).then_inc(mx_in, 16)
                sp.wait_ge(mx_in, 32 * (b + 1))

        @block.gpsimd
        def _(pool):
            pool.memset(VZ[:, :, :], 0.0).then_inc(cleared, 1)

        @block.tensor
        def _(pe):
            def prepare(b):
                pe.wait_ge(c_in[b % 2], 16 * (b // 2 + 1))
                if b:
                    pe.wait_ge(turned_in, b)
                for k in range(KD):
                    mm = pe.transpose(psT[:, 0, k * SC:(k + 1) * SC], cx[:, b % 2, k * P:(k + 1) * P], ident[0:SC, 0:SC])
                mm.then_inc(turned, 1)
                pe.wait_ge(turned_in, b + 1)
                for w, w_in, psum, done, read in ((wk, wk_in, psK, k_done, k_in), (wv, wv_in, psV, v_done, v_in)):
                    if b == 0:
                        pe.wait_ge(w_in, 16)
                    for r in range(NPR):
                        if b and r % 4 == 0:
                            pe.wait_ge(read, 4 * (b - 1) + 2 * (r // 4) + 2)
                        for k in range(KD):
                            mm = pe.matmul(psum[:, r // 4, (r % 4) * SC:(r % 4 + 1) * SC], w[:, k, r * P:(r + 1) * P], cxT[:, k, :],
                                           start=(k == 0), stop=(k == KD - 1))
                        if r % 4 == 3:
                            mm.then_inc(done, 1)

            def products(b):
                for v in range(NPROD):
                    u = NPROD * b + v
                    if u >= 3:
                        pe.wait_ge(*read_out(u - 3))
                    if v == 0:
                        pe.wait_ge(k_in, 4 * b + 4)
                        pe.wait_ge(wq_in, 16)
                    if v == NMX:
                        pe.wait_ge(v_in, 4 * b + 4)
                        pe.wait_ge(wo_in, 16)
                    if v < NMX:
                        k, n = divmod(v, len(SBANKS))
                        first, heads = SBANKS[n]
                        for r in range(heads // 2):
                            mm = pe.matmul(psM[:, u % 3, r * 2 * SC:(r + 1) * 2 * SC], wqT[:, first // 2 + r, k * P:(k + 1) * P],
                                           KX[:, b % 2, first // 2 + r, :], start=True, stop=True)
                    else:
                        for half in range(2):
                            c = 2 * (v - NMX) + half
                            pairs = [r for r in range(NPR) if 2 * SC * r < P * (c + 1) and 2 * SC * (r + 1) > P * c]
                            for r in pairs:
                                window = P * c - 2 * SC * r + P
                                mm = pe.matmul(psM[:, u % 3, half * D:(half + 1) * D], VZ[:, r, window:window + P], wo[:, r, :],
                                               start=(r == pairs[0]), stop=(r == pairs[-1]))
                    mm.then_inc(prod_done, 1)

            prepare(0)
            for b in range(B):
                if b + 1 < B:
                    prepare(b + 1)
                products(b)

        @block.vector
        def _(dve):
            def prepare(b):
                for q in range(2):
                    dve.wait_ge(v_done, 2 * b + q + 1)
                    if b:
                        dve.wait_ge(prod_done, NPROD * b)
                    for half in range(2):
                        rows = slice(half * XD, (half + 1) * XD)
                        dve.tensor_copy(VZ[rows, 4 * q:4 * q + 4, P + half * SC:P + (half + 1) * SC],
                                        psV[rows, q, 0:4 * SC].rearrange("p (r n) -> p r n", n=SC)).then_inc(v_in, 1)

            def take_in(b):
                for v in range(NPROD):
                    if v < NMX:
                        high, low, source = scores_unit(b, v)
                        dve.wait_ge(high_in, NMX * b + v + 1)
                        dve.tensor_tensor(low, source, high, ALU.subtract).then_inc(prod_in[1], 1)
                    elif by_dve(v):
                        to, source = values_unit(b, v)
                        dve.wait_ge(prod_done, NPROD * b + v + 1)
                        dve.tensor_copy(to, source).then_inc(prod_in[1], 1)

            dve.memset(KX[:, :, :, :], 0.0).then_inc(cleared, 1)
            dve.wait_ge(cleared, 2)
            for b in range(B):
                prepare(b)
                take_in(b)

        @block.scalar
        def _(act):
            def prepare(b):
                act.wait_ge(turned, b + 1)
                if b:
                    act.wait_ge(v_done, 2 * b)
                act.activation(cxT[:, :, :], psT[:, 0, 0:KD * SC].rearrange("p (k n) -> p k n", n=SC), ACT.Copy).then_inc(turned_in, 1)
                for q in range(2):
                    act.wait_ge(k_done, 2 * b + q + 1)
                    if b >= 2:
                        act.wait_ge(prod_done, NPROD * (b - 2) + NMX)
                    for half in range(2):
                        rows = slice(half * XD, (half + 1) * XD)
                        act.activation(KX[rows, b % 2, 4 * q:4 * q + 4, half * SC:(half + 1) * SC],
                                       psK[rows, q, 0:4 * SC].rearrange("p (r n) -> p r n", n=SC), ACT.Copy).then_inc(k_in, 1)

            def take_in(b):
                for v in range(NPROD):
                    if v == 0 and b >= 2:
                        act.wait_ge(mx_in, 32 * (b - 1))
                    if v < NMX:
                        high, _, source = scores_unit(b, v)
                        act.wait_ge(prod_done, NPROD * b + v + 1)
                        act.activation(high, source, ACT.Copy).then_inc(high_in, 1)
                    elif not by_dve(v):
                        to, source = values_unit(b, v)
                        act.wait_ge(prod_done, NPROD * b + v + 1)
                        act.activation(to, source, ACT.Copy).then_inc(prod_in[0], 1)

            act.wait_ge(cleared, 2)
            prepare(0)
            for b in range(B):
                if b + 1 < B:
                    prepare(b + 1)
                take_in(b)


def phase_cross(nc, T):
    X, XF, LG, ident, MX, VO = T["X"], T["XF"], T["LG"], T["ident"], T["MX"], T["VO"]
    mx_kept, mx_in = T["mx_kept"], T["mx_in"]
    with ExitStack() as ctx:
        def sb(name, shape, dt=F32):
            return ctx.enter_context(nc.sbuf_tensor(name, shape, dt))

        def sem(name):
            return ctx.enter_context(nc.semaphore(name))

        mask = sb("mask_sb", [P, 2, SC], I32)
        stats = sb("x_stats", [P, 2, 6])
        mean_var = sb("x_mean_var", [P, 2, 2])
        var_eps = sb("x_var_eps", [P, 2])
        neg_half = sb("x_neg_half", [P, 1])
        rstd = sb("x_rstd", [P, 2])
        xn = sb("x_xn", [P, 2, D])
        xnT = [sb(f"x_xnT{part}", [P, 2, KD, P], F32R) for part in range(2)]
        SX = sb("x_scores", [P, 2, XH * SC])
        PX = sb("x_probs", [P, 2, NPK * P])
        row_max = sb("x_row_max", [P, 2, XH])
        neg_max = sb("x_neg_max", [P, 2, XH])
        row_sum = sb("x_row_sum", [P, 2, XH])
        recip = sb("x_recip", [P, XH])
        ET = sb("x_ET", [P, NPK, P])
        gate = sb("gate_sb", [P, KD, NE])
        affine = sb("affine_sb", [P, 2, KD])
        n_stats = sb("n_stats", [P, 2, 2, 6])
        n_mean_var = sb("n_mean_var", [P, 2, 2, 2])
        n_var_eps = sb("n_var_eps", [P, 2, 2])
        n_rstd = sb("n_rstd", [P, 2, 2])
        xr = sb("n_xr", [P, 2, D])
        xrT = sb("n_xrT", [P, 2, KD, P])
        psS = ctx.enter_context(nc.psum_tensor("psS", [P, 3, HALF], F32))
        psE = ctx.enter_context(nc.psum_tensor("psE", [P, 3, HALF], F32))
        psX = ctx.enter_context(nc.psum_tensor("psX", [P, 1, HALF], F32))
        psY = ctx.enter_context(nc.psum_tensor("psYx", [P, 1, HALF], F32))
        L_LN, L_XT, L_S, L_SM, L_E, L_Y, L_XF, L_XR, L_RT, L_LM, L_LG = LAGS = range(11)
        EARLY = 6
        RX, LX = slice(D, 2 * D), slice(D, D + NE)
        EBANKS = [(0, 4), (4, 4), (8, NPK - 8)]

        mask_in = [sem("x_mask_in_even"), sem("x_mask_in_odd")]
        const = sem("x_const")
        w_in = sem("n_w_in")
        n_stats_done = [sem("n_stats1"), sem("n_stats2")]
        n_mv_done = [sem("n_mv1"), sem("n_mv2")]
        n_veps_done = [sem("n_veps1"), sem("n_veps2")]
        n_rstd_done = [sem("n_rstd1"), sem("n_rstd2")]
        xf_done, xr_done = sem("n_xf_done"), sem("n_xr_done")
        rt_done, rt_in = sem("n_rt_done"), sem("n_rt_in")
        l_done, l_in = sem("n_l_done"), sem("n_l_in")
        filled = sem("x_filled")
        stats_done = sem("x_stats_done")
        mv_done = sem("x_mv_done")
        veps_done = sem("x_veps_done")
        rstd_done = sem("x_rstd_done")
        xn_done = sem("x_xn_done")
        xt_done, xt_high, xt_in = sem("x_xt_done"), sem("x_xt_high"), sem("x_xt_in")
        s_done, s_in = sem("x_s_done"), sem("x_s_in")
        max_done = sem("x_max_done")
        neg_done = sem("x_neg_done")
        exp_done = sem("x_exp_done")
        recip_done = sem("x_recip_done")
        scaled = sem("x_scaled")
        e_done, e_in = sem("x_e_done"), sem("x_e_in")
        y_done, y_in = sem("x_y_done"), sem("x_y_in")
        block = ctx.enter_context(nc.Block())

        def by_head(A, e):
            return A[:, e, 0:XH * SC].rearrange("p (h n) -> p h n", n=SC)

        def over_keys(ap):
            return ap.rearrange("p (h a) -> p h a", a=1).to_broadcast([P, XH, SC])

        @block.sync
        def _(sp):
            sp.dma_start(gate[:, :, :], T["gateT"].rearrange("(k p) n -> p k n", p=P)).then_inc(w_in, 16)
            sp.dma_start(affine[:, :, :], T["affine"]).then_inc(w_in, 16)
            mk = T["mask"].rearrange("b (t p) n -> (b t) p n", p=P)

            def load(i, e):
                if not peeled(i, 2):
                    sp.wait_ge(s_in, at(i, 3, -3))
                sp.dma_start(mask[:, e, :], mk[i, :, :]).then_inc(mask_in[e], 16)

            load(0, 0)
            load(1, 1)
            turn = 1
            for b in (2, 3):
                until = ((b - 1) * TB + 4) // 2
                with sp.Fori(turn, until) as j:
                    load(j * 2, 0)
                    load(j * 2 + 1, 1)
                turn = until
                for part in range(2):
                    sp.dma_start(MX[part][:, b % 2, :, :].bitcast(F32), mx_kept[b, part, :, :, :]).then_inc(mx_in, 16)
                sp.wait_ge(mx_in, 32 * (b + 1))
            with sp.Fori(turn, NT // 2) as j:
                load(j * 2, 0)
                load(j * 2 + 1, 1)
            for e in range(2):
                sp.wait_ge(mask_in[e], 16 * (NT // 2))

        @block.gpsimd
        def _(pool):
            pool.memset(neg_half[:, :], -0.5).then_inc(const, 1)
            pool.wait_ge(const, 1)
            pool.memset(PX[:, :, XH * SC:NPK * P], 0.0).then_inc(const, 1)
            pool.wait_ge(const, 2)

            def step(tile):
                if t := tile(L_S):
                    i, e = t
                    if not peeled(i, 2):
                        pool.wait_ge(exp_done, at(i, XH, -XH))
                        pool.sem_inc(T["waited_pool"], 1)
                    pool.memset(SX[:, e, :], NEG_RAW).then_inc(filled, 1)
                    pool.wait_ge(filled, at(i, 1, 1))
                if t := tile(L_LN):
                    i, e = t
                    pool.wait_ge(veps_done, at(i, 1, 1))
                    pool.tensor_tensor(rstd[:, e:e + 1], var_eps[:, e:e + 1], neg_half[:, :], ALU.pow).then_inc(rstd_done, 1)
                    pool.wait_ge(rstd_done, at(i, 1, 1))
                for n, lag in enumerate((L_Y, L_XF)):
                    if t := tile(lag):
                        i, e = t
                        pool.wait_ge(n_veps_done[n], at(i, 1, 1))
                        pool.tensor_tensor(n_rstd[:, n, e:e + 1], n_var_eps[:, n, e:e + 1], neg_half[:, :], ALU.pow).then_inc(n_rstd_done[n], 1)
                        pool.wait_ge(n_rstd_done[n], at(i, 1, 1))

            staggered(pool, NT, LAGS, step)

        @block.tensor
        def _(pe):
            def step(tile):
                def scores(banks):
                    if t := tile(L_S):
                        i, e = t
                        pe.wait_ge(xt_in, at(i, 1, 1))
                        pe.wait_ge(mx_in, 32 * (i // TB) + 32)
                        for n in banks:
                            first, heads = SBANKS[n]
                            if not peeled(i, 1):
                                pe.wait_ge(s_in, at(i, 3, n - 2))
                            for k in range(KD):
                                for a, b in PRODUCTS:
                                    mm = pe.matmul(psS[:, n, 0:heads * SC], xnT[a][:, e, k, :],
                                                   MX[b][:, i // TB % 2, k, first * SC:(first + heads) * SC],
                                                   start=(k == 0 and (a, b) == PRODUCTS[0]), stop=(k == KD - 1 and (a, b) == PRODUCTS[-1]))
                            mm.then_inc(s_done, 1)

                scores([0, 1])
                if t := tile(L_XT):
                    i, e = t
                    if not peeled(i, 1):
                        pe.wait_ge(xt_in, at(i, 1, 0))
                    if (t := tile(L_RT)) and not peeled(t[0], 1):
                        pe.wait_ge(rt_in, at(t[0], 1, 0))
                    pe.wait_ge(xn_done, at(i, 1, 1))
                    for k in range(KD):
                        mm = pe.transpose(psX[:, 0, k * P:(k + 1) * P], xn[:, e, k * P:(k + 1) * P], ident[:, :])
                    mm.then_inc(xt_done, 1)
                scores([2])
                if t := tile(L_E):
                    i, e = t
                    pe.wait_ge(scaled, at(i, 1, 1))
                    for n, (first, tiles) in enumerate(EBANKS):
                        if not peeled(i, 1):
                            pe.wait_ge(e_in, at(i, 3, n - 2))
                        for c in range(tiles):
                            mm = pe.transpose(psE[:, n, c * P:(c + 1) * P], PX[:, e, (first + c) * P:(first + c + 1) * P], ident[:, :])
                        mm.then_inc(e_done, 1)
                if t := tile(L_LM):
                    i, e = t
                    if isinstance(i, int) and i == 0:
                        pe.wait_ge(w_in, 32)
                    pe.wait_ge(rt_in, at(i, 1, 1))
                    if not peeled(i, 1):
                        pe.wait_ge(l_in, at(i, 1, 0))
                    if t := tile(L_Y):
                        pe.wait_ge(y_in, at(t[0], 1, 1))
                    for k in range(KD):
                        mm = pe.matmul(psY[:, 0, LX], xrT[:, e, k, :], gate[:, k, :], start=(k == 0), stop=(k == KD - 1))
                    mm.then_inc(l_done, 1)
                if t := tile(L_E):
                    i, e = t
                    if not peeled(i, 1):
                        pe.wait_ge(y_in, at(i, 1, 0))
                    for c in range(NPK):
                        if c % 4 == 0:
                            pe.wait_ge(e_in, at(i, 3, c // 4 + 1))
                        mm = pe.matmul(psY[:, 0, 0:D], ET[:, c, :], VO[:, i // TB, c, :], start=(c == 0), stop=(c == NPK - 1))
                    mm.then_inc(y_done, 1)
                if t := tile(L_RT):
                    i, e = t
                    if not peeled(i, 1):
                        pe.wait_ge(rt_in, at(i, 1, 0))
                    if t := tile(L_XT):
                        pe.wait_ge(xt_in, at(t[0], 1, 1))
                    pe.wait_ge(xr_done, at(i, 1, 1))
                    for k in range(KD):
                        mm = pe.transpose(psX[:, 0, RX][:, k * P:(k + 1) * P], xr[:, e, k * P:(k + 1) * P], ident[:, :])
                    mm.then_inc(rt_done, 1)

            staggered(pe, NT, LAGS, step)

        @block.vector
        def _(dve):
            dve.wait_ge(const, 2)

            def norm(n, e):
                if n is None:
                    return stats[:, e, :], stats_done, mean_var[:, e, :], mv_done, var_eps[:, e:e + 1], veps_done
                return (n_stats[:, n, e, :], n_stats_done[n], n_mean_var[:, n, e, :], n_mv_done[n],
                        n_var_eps[:, n, e:e + 1], n_veps_done[n])

            def take_stats(n, t, source):
                i, e = t
                out, done, *_ = norm(n, e)
                dve.bn_stats(out, source[:, i, :]).then_inc(done, 1)

            def aggregate(n, t):
                i, e = t
                source, source_done, out, done, *_ = norm(n, e)
                dve.wait_ge(source_done, at(i, 1, 1))
                dve.sem_inc(T["waited_dve"], 1)
                dve.bn_aggr(out, source).then_inc(done, 1)

            def add_eps(n, t):
                i, e = t
                _, _, source, source_done, out, done = norm(n, e)
                dve.wait_ge(source_done, at(i, 1, 1))
                dve.tensor_scalar(out, source[:, 1:2], LN_EPS, None, ALU.add).then_inc(done, 1)

            def step(tile):
                if t := tile(L_SM):
                    i, e = t
                    dve.wait_ge(s_in, at(i, 3, 3))
                    dve.tensor_reduce(row_max[:, e, :], by_head(SX, e), axis=AX.X, op=ALU.max).then_inc(max_done, 1)
                    dve.wait_ge(max_done, at(i, 1, 1))
                    if not peeled(i, 2):
                        dve.wait_ge(exp_done, at(i, XH, -XH))
                    dve.tensor_scalar(neg_max[:, e, :], row_max[:, e, :], -XSCALE, None, ALU.mult).then_inc(neg_done, 1)
                if t := tile(L_E):
                    i, e = t
                    dve.wait_ge(exp_done, at(i, XH, XH))
                    dve.reciprocal(recip[:, :], row_sum[:, e, :]).then_inc(recip_done, 1)
                    dve.wait_ge(recip_done, at(i, 1, 1))
                    dve.tensor_tensor(by_head(PX, e), by_head(PX, e), over_keys(recip[:, :]), ALU.mult).then_inc(scaled, 1)
                if t := tile(L_Y):
                    i, e = t
                    dve.wait_ge(y_done, at(i, 1, 1))
                    dve.tensor_tensor(X[:, i, :], psY[:, 0, 0:D], X[:, i, :], ALU.add).then_inc(y_in, 1)
                if t := tile(L_LG):
                    i, e = t
                    dve.wait_ge(l_done, at(i, 1, 1))
                    dve.tensor_copy(LG[:, i, :], psY[:, 0, LX]).then_inc(l_in, 1)
                ln, own = tile(L_LN), tile(L_Y)
                if ln:
                    take_stats(None, ln, X)
                if own:
                    i, e = own
                    dve.wait_ge(y_in, at(i, 1, 1))
                    if not peeled(i, 2):
                        dve.wait_ge(xf_done, at(i, 1, -1))
                    dve.sem_inc(T["waited_dve"], 1)
                    take_stats(0, own, X)
                for stage in (aggregate, add_eps):
                    if ln:
                        stage(None, ln)
                    if own:
                        stage(0, own)
                if t := tile(L_S):
                    i, e = t
                    dve.wait_ge(filled, at(i, 1, 1))
                    dve.wait_ge(mask_in[e], at(i - e, 8, 16))
                    for n, (first, heads) in enumerate(SBANKS):
                        dve.wait_ge(s_done, at(i, 3, n + 1))
                        dve.sem_inc(T["waited_dve"], 1)
                        dve.copy_predicated(by_head(SX, e)[:, first:first + heads, :],
                                            mask[:, e, :].rearrange("p (a n) -> p a n", a=1).to_broadcast([P, heads, SC]),
                                            psS[:, n, 0:heads * SC].rearrange("p (h n) -> p h n", n=SC)).then_inc(s_in, 1)
                if t := tile(L_XT):
                    i, e = t
                    dve.wait_ge(xt_high, at(i, 1, 1))
                    dve.tensor_tensor(xnT[1][:, e, :, :], psX[:, 0, 0:D].rearrange("p (k n) -> p k n", n=P), xnT[0][:, e, :, :],
                                      ALU.subtract).then_inc(xt_in, 1)
                if t := tile(L_XF):
                    i, e = t
                    dve.wait_ge(n_rstd_done[0], at(i, 1, 1))
                    dve.tensor_scalar(XF[:, i, :], X[:, i, :], n_mean_var[:, 0, e, 0:1], n_rstd[:, 0, e:e + 1],
                                      ALU.subtract, ALU.mult).then_inc(xf_done, 1)
                if t := tile(L_XR):
                    i, e = t
                    dve.wait_ge(n_rstd_done[1], at(i, 1, 1))
                    if not peeled(i, 2):
                        dve.wait_ge(rt_done, at(i, 1, -1))
                    dve.tensor_scalar(xr[:, e, :], XF[:, i, :], n_mean_var[:, 1, e, 0:1], n_rstd[:, 1, e:e + 1],
                                      ALU.subtract, ALU.mult).then_inc(xr_done, 1)
                if t := tile(L_XF):
                    i, e = t
                    dve.wait_ge(xf_done, at(i, 1, 1))
                    if not peeled(i, 2):
                        dve.wait_ge(xr_done, at(i, 1, -1))
                    dve.sem_inc(T["waited_dve"], 1)
                    take_stats(1, t, XF)
                if t := tile(L_LN):
                    i, e = t
                    dve.wait_ge(rstd_done, at(i, 1, 1))
                    if not peeled(i, 2):
                        dve.wait_ge(xt_done, at(i, 1, -1))
                    dve.tensor_scalar(xn[:, e, :], X[:, i, :], mean_var[:, e, 0:1], rstd[:, e:e + 1],
                                      ALU.subtract, ALU.mult).then_inc(xn_done, 1)
                if t := tile(L_XF):
                    aggregate(1, t)
                    add_eps(1, t)

            staggered(dve, NT, LAGS, step)

        @block.scalar
        def _(act):
            def step(tile):
                def exps(heads):
                    if t := tile(L_SM):
                        i, e = t
                        act.wait_ge(neg_done, at(i, 1, 1))
                        if heads[0] == 0 and not peeled(i, 2):
                            act.wait_ge(e_done, at(i, 3, -3))
                        for h in heads:
                            cols = slice(h * SC, (h + 1) * SC)
                            act.activation(PX[:, e, cols], SX[:, e, cols], ACT.Exp, scale=XSCALE, bias=neg_max[:, e, h:h + 1],
                                           accum_out=row_sum[:, e, h:h + 1]).then_inc(exp_done, 1)

                if t := tile(L_LM):
                    i, e = t
                    if isinstance(i, int) and i == 0:
                        act.wait_ge(w_in, 32)
                    act.wait_ge(rt_done, at(i, 1, 1))
                    if not peeled(i, 2):
                        act.wait_ge(l_done, at(i, 1, -1))
                    for k in range(KD):
                        ins = act.activation(xrT[:, e, k, :], psX[:, 0, RX][:, k * P:(k + 1) * P], ACT.Identity,
                                             scale=affine[:, 0, k:k + 1], bias=affine[:, 1, k:k + 1])
                    ins.then_inc(rt_in, 1)
                exps(range(0, EARLY))
                if t := tile(L_E):
                    i, e = t
                    for n, (first, tiles) in enumerate(EBANKS):
                        act.wait_ge(e_done, at(i, 3, n + 1))
                        if n == 0 and not peeled(i, 1):
                            act.wait_ge(y_done, at(i, 1, 0))
                        act.activation(ET[:, first:first + tiles, :], psE[:, n, 0:tiles * P].rearrange("p (c n) -> p c n", n=P),
                                       ACT.Copy).then_inc(e_in, 1)
                if t := tile(L_XT):
                    i, e = t
                    act.wait_ge(xt_done, at(i, 1, 1))
                    if not peeled(i, 2):
                        act.wait_ge(s_done, at(i, 3, -3))
                    act.activation(xnT[0][:, e, :, :], psX[:, 0, 0:D].rearrange("p (k n) -> p k n", n=P), ACT.Copy).then_inc(xt_high, 1)
                exps(range(EARLY, XH))

            staggered(act, NT, LAGS, step)


FI = 512
KF = FI // P
TOPK_EPS = 1e-5


def tile_semaphores(stack, nc):
    def sem(name):
        return stack.enter_context(nc.semaphore(f"tile_{name}"))

    return ([sem("x_even"), sem("x_odd")],) + tuple(sem(name) for name in (
        "t_done", "t_in", "g_done", "u_done", "silu_done", "h_done", "ht_done", "ht_in", "y_done", "y_in"))


def shared_half(nc, T, first, base, rows_of, pool_beside, sync_beside, dve_beside=None, sync_first=None, dve_before=None):
    X, ident = T["X"], T["ident"]
    wg, wu, wd = T["shared_split"]
    N = NT // 2
    tag = f"s{first}"
    with ExitStack() as ctx:
        def sb(name, shape, dt=F32):
            return ctx.enter_context(nc.sbuf_tensor(f"{tag}_{name}", shape, dt))

        def psum(name, banks):
            return ctx.enter_context(nc.psum_tensor(f"{tag}_{name}", [P, banks, HALF], F32))

        def sem(name):
            return ctx.enter_context(nc.semaphore(f"{tag}_{name}"))

        xt = sb("xt", [P, 2, D])
        xfT = [sb(f"xfT{part}", [P, 2, KD, P], F32R) for part in range(2)]
        SG = sb("silu", [P, 2, FI])
        HT = [sb(f"hT{part}", [P, 2, KF, P], F32R) for part in range(2)]
        psG, psU, psT, psH, psY = psum("psG", 2), psum("psU", 2), psum("psT", 1), psum("psH", 1), psum("psY", 2)
        x_in, t_done, t_in, g_done, u_done, silu_done, h_done, ht_done, ht_in, y_done, y_in = T["tile_sems"]
        t_high, ht_high = sem("t_high"), sem("ht_high")
        block = ctx.enter_context(nc.Block())

        @block.sync
        def _(sp):
            def load(i, e):
                if not peeled(i, 2):
                    sp.wait_ge(t_done, at(i, 1, base - 1))
                sp.dma_start(xt[:, e, :], rows_of(i + first)).then_inc(x_in[e], 16)

            load(0, 0)
            load(1, 1)
            if sync_first:
                sync_first(sp)
            load(2, 0)
            load(3, 1)
            with sp.Fori(2, N // 2) as j:
                load(j * 2, 0)
                load(j * 2 + 1, 1)
                sync_beside(sp, j - 2)
            for e in range(2):
                sp.wait_ge(x_in[e], 8 * (base + N))
            for j in range(N // 2 - 2, N // 2):
                sync_beside(sp, j)

        @block.gpsimd
        def _(pool):
            pool_beside(pool)

        @block.tensor
        def _(pe):
            def step(tile):
                if t := tile(2):
                    i, e = t
                    pe.wait_ge(h_done, at(i, 1, base + 1))
                    if not peeled(i, 1):
                        pe.wait_ge(ht_in, at(i, 1, base))
                    for k in range(KF):
                        mm = pe.transpose(psH[:, 0, k * P:(k + 1) * P], SG[:, e, k * P:(k + 1) * P], ident[:, :])
                    mm.then_inc(ht_done, 1)
                if t := tile(1):
                    i, e = t
                    if isinstance(i, int) and i == 0:
                        pe.wait_ge(T["shared_low"], 3)
                    pe.wait_ge(t_in, at(i, 1, base + 1))
                    for w, bank, done, read in ((wg, psG, g_done, silu_done), (wu, psU, u_done, h_done)):
                        if not peeled(i, 2):
                            pe.wait_ge(read, at(i, 1, base - 1))
                        for k in range(KD):
                            for a, b in PRODUCTS:
                                mm = pe.matmul(bank[:, e, :], xfT[a][:, e, k, :], w[b][:, k, :], start=(k == 0 and (a, b) == PRODUCTS[0]),
                                               stop=(k == KD - 1 and (a, b) == PRODUCTS[-1]))
                        mm.then_inc(done, 1)
                if t := tile(0):
                    i, e = t
                    pe.wait_ge(x_in[e], at(i - e, 8, 8 * base + 16))
                    if not peeled(i, 1):
                        pe.wait_ge(t_in, at(i, 1, base))
                    for k in range(KD):
                        mm = pe.transpose(psT[:, 0, k * P:(k + 1) * P], xt[:, e, k * P:(k + 1) * P], ident[:, :])
                    mm.then_inc(t_done, 1)
                if t := tile(2):
                    i, e = t
                    pe.wait_ge(ht_in, at(i, 1, base + 1))
                    if not peeled(i, 2):
                        pe.wait_ge(y_in, at(i, 1, base - 1))
                    for k in range(KF):
                        for a, b in PRODUCTS:
                            mm = pe.matmul(psY[:, e, 0:D], HT[a][:, e, k, :], wd[b][:, k, :], start=(k == 0 and (a, b) == PRODUCTS[0]),
                                           stop=(k == KF - 1 and (a, b) == PRODUCTS[-1]))
                    mm.then_inc(y_done, 1)

            staggered(pe, N, range(3), step)

        @block.vector
        def _(dve):
            def step(tile):
                if t := tile(2):
                    i, e = t
                    dve.wait_ge(ht_high, at(i, 1, 1))
                    dve.tensor_tensor(HT[1][:, e, :, :], psH[:, 0, :].rearrange("p (k n) -> p k n", n=P), HT[0][:, e, :, :],
                                      ALU.subtract).then_inc(ht_in, 1)
                if t := tile(0):
                    i, e = t
                    dve.wait_ge(t_high, at(i, 1, 1))
                    dve.tensor_tensor(xfT[1][:, e, :, :], psT[:, 0, 0:D].rearrange("p (k n) -> p k n", n=P), xfT[0][:, e, :, :],
                                      ALU.subtract).then_inc(t_in, 1)
                if t := tile(1):
                    i, e = t
                    dve.wait_ge(silu_done, at(i, 1, base + 1))
                    dve.wait_ge(u_done, at(i, 1, base + 1))
                    dve.tensor_tensor(SG[:, e, :], psU[:, e, :], SG[:, e, :], ALU.mult).then_inc(h_done, 1)
                if t := tile(2):
                    i, e = t
                    dve.wait_ge(y_done, at(i, 1, base + 1))
                    if dve_before:
                        dve_before(dve, i)
                    dve.tensor_tensor(X[:, i + first, :], psY[:, e, 0:D], X[:, i + first, :], ALU.add).then_inc(y_in, 1)
                    if dve_beside:
                        dve.wait_ge(y_in, at(i, 1, base + 1))
                        dve_beside(dve, i, e)

            staggered(dve, N, range(3), step)

        @block.scalar
        def _(act):
            def step(tile):
                if t := tile(2):
                    i, e = t
                    act.wait_ge(ht_done, at(i, 1, base + 1))
                    if not peeled(i, 2):
                        act.wait_ge(y_done, at(i, 1, base - 1))
                    act.activation(HT[0][:, e, :, :], psH[:, 0, :].rearrange("p (k n) -> p k n", n=P), ACT.Copy).then_inc(ht_high, 1)
                if t := tile(1):
                    i, e = t
                    act.wait_ge(g_done, at(i, 1, base + 1))
                    if not peeled(i, 2):
                        act.wait_ge(ht_done, at(i, 1, base - 1))
                    act.activation(SG[:, e, :], psG[:, e, :], ACT.Silu).then_inc(silu_done, 1)
                if t := tile(0):
                    i, e = t
                    act.wait_ge(t_done, at(i, 1, base + 1))
                    if not peeled(i, 2):
                        act.wait_ge(u_done, at(i, 1, base - 1))
                    act.activation(xfT[0][:, e, :, :], psT[:, 0, 0:D].rearrange("p (k n) -> p k n", n=P), ACT.Copy).then_inc(t_high, 1)

            staggered(act, N, range(3), step)


def phase_scatter(nc, T):
    X, XF, POS, xs, x_kept, kept = T["X"], T["XF"], T["POS"], T["xs"], T["x_kept"], T["kept"]
    added = T["tile_sems"][-1]
    with nc.semaphore("scattered") as scattered:
        def scatter(pool):
            for t in range(NT):
                for c in range(TOP):
                    pool.indirect_dma_start(out=xs, out_offset=bass.IndirectOffsetOnAxis(ap=POS[:, c, t:t + 1], axis=0),
                                            in_=XF[:, t, :], in_offset=None).then_inc(scattered, 16)
            pool.wait_ge(scattered, 16 * TOP * NT)

        def load_expert(sp, x):
            one = bass.ds(x, 1)
            for name in ("Wg", "Wu", "Wd"):
                sp.dma_start(T[name.upper()][:, one, :, :],
                             T[name][one, :, :].rearrange("a (k p) n -> p a k n", p=P)).then_inc(T["experts_in"], 16)

        def load_first(sp):
            sp.wait_ge(T["shared_low"], 3)
            load_expert(sp, 0)
            load_expert(sp, 1)

        def keep(sp, j):
            if not (isinstance(j, int) and j + 2 >= NE):
                load_expert(sp, j + 2)
            sp.wait_ge(added, at(j, 2, 2))
            sp.dma_start(x_kept[:, bass.ds(j * 2, 2), :], X[:, bass.ds(j * 2, 2), :]).then_inc(kept, 16)
            if isinstance(j, int) and j == NT // 4 - 1:
                sp.wait_ge(kept, 16 * (2 + NT // 4))

        shared_half(nc, T, 0, 0, lambda i: XF[:, bass.ds(i, 1), :], scatter, keep, sync_first=load_first)


def phase_route(nc, T):
    LG, W12, POS, tile_expert = T["LG"], T["W12"], T["POS"], T["tile_expert"]
    with ExitStack() as ctx:
        def sb(name, shape, dt=F32):
            return ctx.enter_context(nc.sbuf_tensor(name, shape, dt))

        def sem(name):
            return ctx.enter_context(nc.semaphore(name))

        A3 = [P, NT, NE]
        top = sb("r_top", [P, NT])
        ex = sb("r_ex", A3)
        total = sb("r_total", [P, NT])
        probs = sb("r_probs", A3)
        order = sb("r_order", [P, NE])
        value = sb("r_value", A3)
        best = sb("r_best", [P, 2, NT])
        pick = sb("r_pick", [P, NT])
        chosen = sb("r_chosen", [P, 2, NT, NE])
        both = sb("r_both", A3)
        den = sb("r_den", [P, NT])
        before = sb("r_before", [P, P])
        ones = sb("r_ones", [P, P])
        sums = sb("r_sums", [P, 2, NT, NE])
        counts = sb("r_counts", [P, NE])
        counts_i = sb("r_counts_i", [P, NE], I32)
        tiles = sb("r_tiles", [P, NE])
        ends = sb("r_ends", [P, 2, NE])
        slot = sb("r_slot", A3)
        slot_of = sb("r_slot_of", [P, 2, NT])
        tile_no = sb("r_tile_no", [P, NTM])
        expert = sb("r_expert", [P, NTM])
        ps = ctx.enter_context(nc.psum_tensor("r_ps", [P, 2, NT, NE], F32))
        const = sem("r_const")
        step_done = sem("r_step_done")
        shared_in = sem("r_shared_in")
        shared_high = sem("r_shared_high")
        max_off = sem("r_max_off")
        exp_done = sem("r_exp_done")
        chosen_done = sem("r_chosen_done")
        counted = sem("r_counted")
        slots_done = sem("r_slots_done")
        block = ctx.enter_context(nc.Block())

        def over_e(ap):
            return ap.rearrange("p (t a) -> p t a", a=1).to_broadcast(A3)

        def over_t(ap):
            return ap.rearrange("p (a e) -> p a e", a=1).to_broadcast(A3)

        @block.sync
        def _(sp):
            sp.dma_start(T["WG"][:, 0, :, :], T["sWg"].rearrange("(k p) n -> p k n", p=P)).then_inc(shared_in, 16)
            sp.dma_start(T["WU"][:, 0, :, :], T["sWu"].rearrange("(k p) n -> p k n", p=P)).then_inc(shared_in, 16)
            sp.dma_start(T["WD"][:, 0, :, :], T["sWd"].rearrange("(k p) n -> p k n", p=P)).then_inc(shared_in, 16)
            sp.dma_start(T["xf_kept"], T["XF"][:, NT // 2:NT, :]).then_inc(T["kept"], 16)
            sp.dma_start(T["x_kept"][:, NT // 2:NT, :], T["X"][:, NT // 2:NT, :]).then_inc(T["kept"], 16)

        @block.gpsimd
        def _(pool):
            pool.memset(ones[:, :], 1.0).then_inc(const, 1)
            pool.wait_ge(const, 1)
            pool.affine_select(out=before[:, :], in_=ones[:, :], compare_op=ALU.is_gt, fill=0.0,
                               base=0, pattern=[[1, P]], channel_multiplier=-1).then_inc(const, 1)
            pool.wait_ge(const, 2)
            pool.iota(order[:, :], [[-1, NE]], base=NE, channel_multiplier=0,
                      allow_small_or_imprecise_dtypes=True).then_inc(const, 1)
            pool.wait_ge(const, 3)
            pool.iota(tile_no[:, :], [[1, NTM]], base=0, channel_multiplier=0,
                      allow_small_or_imprecise_dtypes=True).then_inc(const, 1)
            for n, w in enumerate(("WG", "WU", "WD")):
                high, low = T["shared_split"][n]
                pool.wait_ge(shared_high, n + 1)
                pool.tensor_tensor(low[:, :, :], T[w][:, 0, :, :], high[:, :, :], ALU.subtract).then_inc(T["shared_low"], 1)

        @block.scalar
        def _(act):
            act.wait_ge(shared_in, 16 * 3)
            for n, w in enumerate(("WG", "WU", "WD")):
                act.activation(T["shared_split"][n][0][:, :, :], T[w][:, 0, :, :], ACT.Copy).then_inc(shared_high, 1)
            act.wait_ge(max_off, 1)
            act.activation(ex[:, :, :], ex[:, :, :], ACT.Exp).then_inc(exp_done, 1)

        @block.tensor
        def _(pe):
            pe.wait_ge(const, 2)
            pe.wait_ge(chosen_done, 1)
            flat = both[:, :, :].rearrange("p t e -> p (t e)")
            pe.matmul(ps[:, 0, :, :].rearrange("p t e -> p (t e)"), before[:, :], flat, start=True, stop=True)
            pe.matmul(ps[:, 1, :, :].rearrange("p t e -> p (t e)"), ones[:, :], flat, start=True, stop=True).then_inc(counted, 1)

        @block.vector
        def _(dve):
            n = [0]

            def link(ins):
                n[0] += 1
                ins.then_inc(step_done, 1)
                dve.wait_ge(step_done, n[0])

            dve.wait_ge(const, 4)
            link(dve.tensor_reduce(top[:, :], LG[:, :, :], axis=AX.X, op=ALU.max))
            dve.tensor_tensor(ex[:, :, :], LG[:, :, :], over_e(top[:, :]), ALU.subtract).then_inc(max_off, 1)
            dve.wait_ge(exp_done, 1)
            link(dve.tensor_reduce(total[:, :], ex[:, :, :], axis=AX.X, op=ALU.add))
            link(dve.reciprocal(total[:, :], total[:, :]))
            link(dve.tensor_tensor(probs[:, :, :], ex[:, :, :], over_e(total[:, :]), ALU.mult))
            for c in range(TOP):
                link(dve.tensor_reduce(best[:, c, :], probs[:, :, :], axis=AX.X, op=ALU.max))
                link(dve.tensor_tensor(value[:, :, :], probs[:, :, :], over_e(best[:, c, :]), ALU.is_equal))
                link(dve.tensor_tensor(value[:, :, :], value[:, :, :], over_t(order[:, :]), ALU.mult))
                link(dve.tensor_reduce(pick[:, :], value[:, :, :], axis=AX.X, op=ALU.max))
                link(dve.tensor_tensor(chosen[:, c, :, :], value[:, :, :], over_e(pick[:, :]), ALU.is_equal))
                if c == 0:
                    link(dve.scalar_tensor_tensor(probs[:, :, :], chosen[:, 0, :, :], -2.0, probs[:, :, :], ALU.mult, ALU.add))
            dve.tensor_tensor(both[:, :, :], chosen[:, 0, :, :], chosen[:, 1, :, :], ALU.add).then_inc(chosen_done, 1)
            link(dve.tensor_tensor(den[:, :], best[:, 0, :], best[:, 1, :], ALU.add))
            link(dve.tensor_scalar(den[:, :], den[:, :], TOPK_EPS, None, ALU.add))
            link(dve.reciprocal(den[:, :], den[:, :]))
            for c in range(TOP):
                link(dve.tensor_tensor(W12[:, c, :], best[:, c, :], den[:, :], ALU.mult))
            dve.wait_ge(counted, 1)
            link(dve.tensor_copy(sums[:, 0, :, :], ps[:, 1, :, :]))
            a, shift = 0, 1
            while shift < NT:
                link(dve.tensor_copy(sums[:, 1 - a, 0:shift, :], sums[:, a, 0:shift, :]))
                link(dve.tensor_tensor(sums[:, 1 - a, shift:NT, :], sums[:, a, shift:NT, :], sums[:, a, 0:NT - shift, :], ALU.add))
                a, shift = 1 - a, 2 * shift
            link(dve.tensor_scalar(counts[:, :], sums[:, a, NT - 1, :], float(P - 1), None, ALU.add))
            link(dve.tensor_copy(counts_i[:, :], counts[:, :]))
            link(dve.tensor_scalar(counts_i[:, :], counts_i[:, :], P.bit_length() - 1, None, ALU.logical_shift_right))
            link(dve.tensor_copy(tiles[:, :], counts_i[:, :]))
            link(dve.tensor_copy(ends[:, 0, :], tiles[:, :]))
            c, shift = 0, 1
            while shift < NE:
                link(dve.tensor_copy(ends[:, 1 - c, 0:shift], ends[:, c, 0:shift]))
                link(dve.tensor_tensor(ends[:, 1 - c, shift:NE], ends[:, c, shift:NE], ends[:, c, 0:NE - shift], ALU.add))
                c, shift = 1 - c, 2 * shift
            link(dve.tensor_tensor(tiles[:, :], ends[:, c, :], tiles[:, :], ALU.subtract))
            link(dve.tensor_scalar(tiles[:, :], tiles[:, :], float(P), None, ALU.mult))
            link(dve.tensor_tensor(slot[:, :, :], ps[:, 0, :, :], sums[:, a, :, :], ALU.add))
            link(dve.tensor_tensor(slot[:, :, :], slot[:, :, :], over_t(tiles[:, :]), ALU.add))
            link(dve.tensor_tensor(slot[:, :, :], ps[:, 1, :, :], slot[:, :, :], ALU.subtract))
            for k in range(TOP):
                link(dve.tensor_tensor(value[:, :, :], chosen[:, k, :, :], slot[:, :, :], ALU.mult))
                link(dve.tensor_reduce(slot_of[:, k, :], value[:, :, :], axis=AX.X, op=ALU.add, negate=True))
            link(dve.tensor_copy(POS[:, :, :], slot_of[:, :, :]))
            link(dve.tensor_scalar(expert[:, :], tile_no[:, :], ends[:, c, 0:1], None, ALU.is_ge))
            for x in range(1, NE - 1):
                link(dve.scalar_tensor_tensor(expert[:, :], tile_no[:, :], ends[:, c, x:x + 1], expert[:, :], ALU.is_ge, ALU.add))
            dve.tensor_copy(tile_expert[:, :], expert[:, :]).then_inc(slots_done, 1)


def phase_experts(nc, T):
    base = NT // 2
    ident, WG, WU, WD, tile_expert, xs, ys = (T[k] for k in ("ident", "WG", "WU", "WD", "tile_expert", "xs", "ys"))
    with ExitStack() as ctx:
        def sb(name, shape, dt=F32):
            return ctx.enter_context(nc.sbuf_tensor(name, shape, dt))

        def sem(name):
            return ctx.enter_context(nc.semaphore(name))

        xt = sb("m_x", [P, 2, D])
        xT = [sb(f"m_xT{part}", [P, 2, KD, P], F32R) for part in range(2)]
        SG = sb("m_silu", [P, 2, FI])
        HT = sb("m_hT", [P, 2, KF, P])
        yt = sb("m_y", [P, 2, D])
        psG = ctx.enter_context(nc.psum_tensor("m_psG", [P, 2, HALF], F32))
        psU = ctx.enter_context(nc.psum_tensor("m_psU", [P, 2, HALF], F32))
        psT = ctx.enter_context(nc.psum_tensor("m_psT", [P, 1, HALF], F32))
        psH = ctx.enter_context(nc.psum_tensor("m_psH", [P, 1, HALF], F32))
        psY = ctx.enter_context(nc.psum_tensor("m_psY", [P, 2, HALF], F32))
        x_in, t_done, t_in, g_done, u_done, silu_done, h_done, ht_done, ht_in, y_done, y_in = T["tile_sems"]
        t_high = sem("m_t_high")
        w_high, w_low, w_low_pool = sem("m_w_high"), sem("m_w_low"), sem("m_w_low_pool")
        BY_POOL = 2
        y_out = [sem("m_y_out_even"), sem("m_y_out_odd")]
        block = ctx.enter_context(nc.Block())

        def split(w, high_place, low_place):
            return [w] + [nc.alloc_sbuf_tensor_at(f"m_{place}_split", [P, NE, KD, FI], F32R, offset=T["place"][place])
                          for place in (high_place, low_place)]

        SPLIT = [split(WG, "X", "WG"), split(WU, "XF", "WU")]
        xs_t = xs.rearrange("(t p) d -> t p d", p=P)
        ys_t = ys.rearrange("(t p) d -> t p d", p=P)

        @block.sync
        def _(sp):
            def load(i, e):
                if not peeled(i, 2):
                    sp.wait_ge(t_done, at(i, 1, base - 1))
                sp.dma_start(xt[:, e, :], xs_t[i, :, :]).then_inc(x_in[e], 16)

            load(0, 0)
            load(1, 1)
            with sp.Fori(1, NTM // 2) as j:
                load(j * 2, 0)
                load(j * 2 + 1, 1)
            for e in range(2):
                sp.wait_ge(x_in[e], 8 * (base + NTM))

        @block.gpsimd
        def _(pool):
            def store(i, e):
                pool.wait_ge(y_in, at(i, 1, base + 1))
                pool.dma_start(ys_t[i, :, :], yt[:, e, :]).then_inc(y_out[e], 16)

            for m in range(2 * BY_POOL):
                w, high, low = SPLIT[m % 2]
                x = m // 2
                pool.wait_ge(w_high, m + 1)
                pool.tensor_tensor(low[:, x, :, :], w[:, x, :, :], high[:, x, :, :], ALU.subtract).then_inc(w_low_pool, 1)
                pool.wait_ge(w_low_pool, m + 1)
            with pool.Fori(0, NTM // 2) as j:
                store(j * 2, 0)
                store(j * 2 + 1, 1)
            for e in range(2):
                pool.wait_ge(y_out[e], 16 * (NTM // 2))

        @block.tensor
        def _(pe):
            def expert_of(i):
                return pe.value_load(tile_expert[0:1, bass.ds(i, 1)], min_val=0, max_val=NE - 1)

            pe.wait_ge(w_low, 2 * (NE - BY_POOL))
            pe.wait_ge(w_low_pool, 2 * BY_POOL)

            def step(tile):
                expert = {lag: expert_of(tile(lag)[0]) for lag in (1, 2) if tile(lag)}
                if t := tile(2):
                    i, e = t
                    pe.wait_ge(h_done, at(i, 1, base + 1))
                    if not peeled(i, 1):
                        pe.wait_ge(ht_in, at(i, 1, base))
                    for k in range(KF):
                        mm = pe.transpose(psH[:, 0, k * P:(k + 1) * P], SG[:, e, k * P:(k + 1) * P], ident[:, :])
                    mm.then_inc(ht_done, 1)
                if t := tile(1):
                    i, e = t
                    pe.wait_ge(t_in, at(i, 1, base + 1))
                    for (_, *w), bank, done, read in ((SPLIT[0], psG, g_done, silu_done), (SPLIT[1], psU, u_done, h_done)):
                        if not peeled(i, 2):
                            pe.wait_ge(read, at(i, 1, base - 1))
                        for k in range(KD):
                            for a, b in PRODUCTS:
                                mm = pe.matmul(bank[:, e, :], xT[a][:, e, k, :], w[b][:, expert[1], k, :], start=(k == 0 and (a, b) == PRODUCTS[0]),
                                               stop=(k == KD - 1 and (a, b) == PRODUCTS[-1]))
                        mm.then_inc(done, 1)
                if t := tile(0):
                    i, e = t
                    pe.wait_ge(x_in[e], at(i - e, 8, 8 * base + 16))
                    if not peeled(i, 1):
                        pe.wait_ge(t_in, at(i, 1, base))
                    for k in range(KD):
                        mm = pe.transpose(psT[:, 0, k * P:(k + 1) * P], xt[:, e, k * P:(k + 1) * P], ident[:, :])
                    mm.then_inc(t_done, 1)
                if t := tile(2):
                    i, e = t
                    pe.wait_ge(ht_in, at(i, 1, base + 1))
                    if not peeled(i, 2):
                        pe.wait_ge(y_in, at(i, 1, base - 1))
                    for k in range(KF):
                        mm = pe.matmul(psY[:, e, 0:D], HT[:, e, k, :], WD[:, expert[2], k, :], start=(k == 0), stop=(k == KF - 1))
                    mm.then_inc(y_done, 1)

            staggered(pe, NTM, range(3), step)

        @block.vector
        def _(dve):
            for x in range(BY_POOL, NE):
                for n, (w, high, low) in enumerate(SPLIT):
                    dve.wait_ge(w_high, 2 * x + n + 1)
                    dve.tensor_tensor(low[:, x, :, :], w[:, x, :, :], high[:, x, :, :], ALU.subtract).then_inc(w_low, 1)

            def step(tile):
                if t := tile(0):
                    i, e = t
                    dve.wait_ge(t_high, at(i, 1, 1))
                    dve.tensor_tensor(xT[1][:, e, :, :], psT[:, 0, 0:D].rearrange("p (k n) -> p k n", n=P), xT[0][:, e, :, :],
                                      ALU.subtract).then_inc(t_in, 1)
                if t := tile(1):
                    i, e = t
                    dve.wait_ge(silu_done, at(i, 1, base + 1))
                    dve.wait_ge(u_done, at(i, 1, base + 1))
                    dve.tensor_tensor(SG[:, e, :], psU[:, e, :], SG[:, e, :], ALU.mult).then_inc(h_done, 1)
                if t := tile(2):
                    i, e = t
                    dve.wait_ge(y_done, at(i, 1, base + 1))
                    if not peeled(i, 2):
                        dve.wait_ge(y_out[e], at(i - e, 8, 0))
                    dve.tensor_copy(yt[:, e, :], psY[:, e, 0:D]).then_inc(y_in, 1)

            staggered(dve, NTM, range(3), step)

        @block.scalar
        def _(act):
            act.wait_ge(T["experts_in"], 16 * 3 * NE)
            for x in range(NE):
                for w, high, low in SPLIT:
                    act.activation(high[:, x, :, :], w[:, x, :, :], ACT.Copy).then_inc(w_high, 1)

            def step(tile):
                if t := tile(2):
                    i, e = t
                    act.wait_ge(ht_done, at(i, 1, base + 1))
                    if not peeled(i, 2):
                        act.wait_ge(y_done, at(i, 1, base - 1))
                    act.activation(HT[:, e, :, :], psH[:, 0, :].rearrange("p (k n) -> p k n", n=P), ACT.Copy).then_inc(ht_in, 1)
                if t := tile(1):
                    i, e = t
                    act.wait_ge(g_done, at(i, 1, base + 1))
                    if not peeled(i, 2):
                        act.wait_ge(ht_done, at(i, 1, base - 1))
                    act.activation(SG[:, e, :], psG[:, e, :], ACT.Silu).then_inc(silu_done, 1)
                if t := tile(0):
                    i, e = t
                    act.wait_ge(t_done, at(i, 1, base + 1))
                    if not peeled(i, 2):
                        act.wait_ge(u_done, at(i, 1, base - 1))
                    act.activation(xT[0][:, e, :, :], psT[:, 0, 0:D].rearrange("p (k n) -> p k n", n=P), ACT.Copy).then_inc(t_high, 1)

            staggered(act, NTM, range(3), step)


def phase_combine(nc, T):
    X, W12, POS, ys, out = T["X"], T["W12"], T["POS"], T["ys"], T["out"]
    with ExitStack() as ctx:
        def sem(name):
            return ctx.enter_context(nc.semaphore(name))

        NB = 4
        rows = ctx.enter_context(nc.sbuf_tensor("c_rows", [P, TOP, NB, D], F32))
        gathered = [sem(f"c_gathered{n}") for n in range(NB)]
        first = sem("c_first")
        added = sem("c_added")
        stored = sem("c_stored")
        out_t = out.rearrange("b (t p) d -> p (b t) d", p=P)

        def gather(pool):
            for t in range(NT):
                if t >= NB:
                    pool.wait_ge(added, t - NB + 1)
                for c in range(TOP):
                    pool.indirect_dma_start(out=rows[:, c, t % NB, :], out_offset=None, in_=ys,
                                            in_offset=bass.IndirectOffsetOnAxis(ap=POS[:, c, t:t + 1], axis=0),
                                            ).then_inc(gathered[t % NB], 16)

        def add(dve, i, e):
            for d in range(2):
                t = at(i, 2, d)
                n = 2 * e + d
                dve.wait_ge(gathered[n], at(i - e, 16, 32))
                dve.scalar_tensor_tensor(X[:, t, :], rows[:, 0, n, :], W12[:, 0, bass.ds(t, 1)], X[:, t, :],
                                         ALU.mult, ALU.add).then_inc(first, 1)
                dve.wait_ge(first, at(i, 2, d + 1))
                dve.scalar_tensor_tensor(X[:, t, :], rows[:, 1, n, :], W12[:, 1, bass.ds(t, 1)], X[:, t, :],
                                         ALU.mult, ALU.add).then_inc(added, 1)

        first_in, rest_in = sem("c_first_in"), sem("c_rest_in")

        def load_back(sp):
            for start in (NT // 2, 0):
                sp.dma_start(X[:, start:start + NB, :], T["x_kept"][:, start:start + NB, :]).then_inc(first_in, 16)
            for start in (NT // 2, 0):
                sp.dma_start(X[:, start + NB:start + NT // 2, :], T["x_kept"][:, start + NB:start + NT // 2, :]).then_inc(rest_in, 16)

        def stream_in(dve, i):
            if isinstance(i, int) and i < 2:
                dve.wait_ge((first_in, rest_in)[i], 32)

        def store(sp, j):
            sp.wait_ge(added, at(j, 4, 4))
            sp.dma_start(out_t[:, bass.ds(j * 4, 4), :], X[:, bass.ds(j * 4, 4), :]).then_inc(stored, 16)
            if isinstance(j, int) and j == NT // 4 - 1:
                sp.wait_ge(stored, 16 * (NT // 4))

        shared_half(nc, T, NT // 2, NT // 2 + NTM, lambda i: T["xf_kept"][:, bass.ds(i - NT // 2, 1), :], gather, store, add, load_back,
                    stream_in)


def decoder_layer(nc, T):
    with ExitStack() as ctx:
        def dram(name, shape, dt):
            return nc.dram_tensor(name, shape, dt, kind="Internal").ap()

        T["place"] = {}

        def sb(stack, name, shape, dt=F32):
            T["place"][name] = -(-nc.sbuf_base // 32) * 32
            T[name] = stack.enter_context(nc.sbuf_tensor(name, shape, dt))

        T["q_parts"] = dram("q_parts", [B, 3, NKV, GH, HD, S], BF16)
        T["k_parts"] = dram("k_parts", [B, 3, NKV, HD, S], BF16)
        T["m_parts"] = dram("m_parts", [NG, 3, GH * S], BF16)
        T["xs"] = dram("xs", [NSLOT, D], F32)
        T["ys"] = dram("ys", [NSLOT, D], F32)
        T["x_kept"] = dram("x_kept", [P, NT, D], F32)
        T["xf_kept"] = dram("xf_kept", [P, NT // 2, D], F32)
        T["mx_kept"] = dram("mx_kept", [B, 2, P, KD, XH * SC], F32)
        T["mx_in"] = ctx.enter_context(nc.semaphore("mx_in"))
        T["kept"] = ctx.enter_context(nc.semaphore("kept"))
        T["waited_dve"] = ctx.enter_context(nc.semaphore("waited_dve"))
        T["waited_pool"] = ctx.enter_context(nc.semaphore("waited_pool"))
        sb(ctx, "X", [P, NT, D])
        sb(ctx, "ident", [P, P])
        with ExitStack() as attention:
            sb(attention, "VA", [P, NG, TB, VW])
            sb(attention, "OU", [P, NKV, B * S])
            with ExitStack() as stacks:
                sb(stacks, "QS", [P, SLOTS, GH, S], BF16)
                sb(stacks, "KS", [P, SLOTS, S], BF16)
                T["loaded"] = [stacks.enter_context(nc.semaphore(f"loaded_{e}")) for e in ("even", "odd")]
                phase_qkv(nc, T)
                phase_attention(nc, T)
            phase_self_out(nc, T)
        sb(ctx, "XF", [P, NT, D])
        sb(ctx, "LG", [P, NT, NE])
        with ExitStack() as cross:
            T["MX"] = [cross.enter_context(nc.sbuf_tensor(f"MX_{part}", [P, 2, KD, XH * SC], F32R)) for part in ("high", "low")]
            sb(cross, "VO", [P, B, NPK, D])
            phase_context(nc, T)
            phase_cross(nc, T)
        T["shared_split"] = [[ctx.enter_context(nc.sbuf_tensor(f"{name}_{part}", shape, F32R)) for part in ("high", "low")]
                             for name, shape in (("swg", [P, KD, FI]), ("swu", [P, KD, FI]), ("swd", [P, KF, D]))]
        T["shared_low"] = ctx.enter_context(nc.semaphore("shared_low"))
        sb(ctx, "W12", [P, TOP, NT])
        sb(ctx, "POS", [P, TOP, NT], U32)
        sb(ctx, "tile_expert", [P, NTM], I32)
        T["experts_in"] = ctx.enter_context(nc.semaphore("experts_in"))
        T["tile_sems"] = tile_semaphores(ctx, nc)
        with ExitStack() as weights:
            sb(weights, "WG", [P, NE, KD, FI])
            sb(weights, "WU", [P, NE, KD, FI])
            sb(weights, "WD", [P, NE, KF, D])
            phase_route(nc, T)
            phase_scatter(nc, T)
            phase_experts(nc, T)
        phase_combine(nc, T)


def kernel(**inputs):
    import numpy as np
    import concourse.bacc as bacc
    from concourse.bass_utils import run_bass_kernel_spmd

    def rows(name):
        return np.ascontiguousarray(inputs[name])

    def per_head(name):
        w = np.asarray(inputs[name])
        return np.ascontiguousarray(w.transpose(1, 0, 2).reshape(w.shape[1], -1))

    def columns(*vectors):
        v = np.concatenate([np.asarray(x) for x in vectors])
        v = np.concatenate([v, np.zeros(-len(v) % P, v.dtype)])
        return np.ascontiguousarray(v.reshape(-1, P).T)

    wo = np.asarray(inputs["L0_attn_Wo"]).reshape(GH, NKV, HD, D).transpose(1, 0, 2, 3)
    wqx = np.asarray(inputs["L0_xattn_Wq"])
    arrays = {
        "x": rows("x"), "ctx": rows("ctx_1024"), "mask": rows("mask_BxSxS2_ik1"),
        "Wq": rows("L0_attn_Wq"), "Wk": rows("L0_attn_Wk"), "Wv": rows("L0_attn_Wv"),
        "bqk": columns(inputs["L0_attn_bq"], inputs["L0_attn_bk"]), "bv": rows("L0_attn_bv"),
        "Wo": np.ascontiguousarray(wo.reshape(D, D)), "bo": rows("L0_attn_bo"),
        "WqxT": np.ascontiguousarray(wqx.transpose(0, 2, 1).reshape(-1, wqx.shape[1])),
        "Wkx": per_head("L0_xattn_Wk"), "Wvx": per_head("L0_xattn_Wv"),
        "Wox": rows("L0_xattn_Wo"),
        "sWg": rows("L0_ffn_sWg"), "sWu": rows("L0_ffn_sWu"), "sWd": rows("L0_ffn_sWd"),
        "gateT": np.ascontiguousarray(np.asarray(inputs["L0_ffn_gate_w"]).T),
        "affine": np.ascontiguousarray(np.stack([columns(inputs["L0_ffn_ln_scale"]), columns(inputs["L0_ffn_ln_bias"])], 1)),
        "Wg": rows("L0_ffn_Wg"), "Wu": rows("L0_ffn_Wu"), "Wd": rows("L0_ffn_Wd"),
    }
    nc = bacc.Bacc("TRN2", target_bir_lowering=False, num_devices=1)
    T = {name: nc.dram_tensor(f"in_{name}", a.shape, mybir.dt.from_np(a.dtype), kind="ExternalInput").ap()
         for name, a in arrays.items()}
    T["out"] = nc.dram_tensor("out", (B, S, D), F32, kind="ExternalOutput").ap()
    decoder_layer(nc, T)
    r = run_bass_kernel_spmd(nc, [{f"in_{name}": a for name, a in arrays.items()}], core_ids=[0])
    return r.results[0]["out"]
```
